# Optimizing a Trainium2 kernel written in Bass

```python
import numpy as np
import jax
import jax.numpy as jnp

def _softmax(x, axis=-1):
    return jax.nn.softmax(x, axis=axis)

def _gelu(x):
    return jax.nn.gelu(x, approximate=True)

def _silu(x):
    return jax.nn.silu(x)

def _sigmoid(x):
    return jax.nn.sigmoid(x)

def _layernorm(x, axis=-1, eps=1e-05):
    m = jnp.mean(x, axis=axis, keepdims=True)
    v = jnp.var(x, axis=axis, keepdims=True)
    return (x - m) / jnp.sqrt(v + eps)

def _scatter_add(tgt, idx, src, axis=0):
    return tgt.at[idx].add(src)

def _segment_sum(src, seg, n):
    return jax.ops.segment_sum(src, seg, n)
kernel_name = 'mk_gps_d1_gnn_r8_a67115'

def setup_inputs(seed: int=0):
    np.random.seed(seed)
    _w = jnp.asarray

    def _rec_inputs():
        import jax
        import jax.numpy as jnp
        _gk = jax.random.key(seed)
        x = -0.0001913 + 0.9998 * jax.random.normal(jax.random.fold_in(_gk, 1), (6250, 256), jnp.float32)
        src = jax.random.randint(jax.random.fold_in(_gk, 2), (200000,), 0, 6250, jnp.int32)
        dst = jax.random.randint(jax.random.fold_in(_gk, 3), (200000,), 0, 6250, jnp.int32)
        _o = jnp.argsort(dst, stable=True)
        src = src[_o]
        dst = dst[_o]
        return (x, src, dst)
    x, src, dst = _rec_inputs()

    def _L0_gnn_setup():
        import jax, jax.numpy as jnp
        import numpy as np
        N_NODES = 2500
        N_EDGES = 40000
        D_IN = 256
        D_OUT = 256
        key = jax.random.key(seed)
        k1, k2, k3, k4 = jax.random.split(key, 4)
        A = jax.random.randint(k1, (2, N_EDGES), 0, N_NODES, dtype=jnp.int64)
        X = jax.random.normal(k2, (N_NODES, D_IN), dtype=jnp.float32)
        W = jax.random.normal(k3, (D_IN, D_OUT), dtype=jnp.float32) / np.sqrt(D_IN)
        b = jax.random.normal(k4, (D_OUT,), dtype=jnp.float32) * 0.01
        return {'A': A, 'X': X, 'W': W, 'b': b}
    _L0_gnn_all = _L0_gnn_setup()
    _L0_gnn_in = {k: v for k, v in _L0_gnn_all.items() if k in ('W', 'b')}
    del _L0_gnn_all

    def _L0_mix_setup():
        import jax, jax.numpy as jnp
        import numpy as np
        N, F, C, H = (32, 512, 256, 8)
        D = C // H
        EPS_ATTN = 1e-06
        EPS_LN = 1e-05

        def layer_norm(x, g, b):
            mu = jnp.mean(x, axis=-1, keepdims=True)
            var = jnp.var(x, axis=-1, keepdims=True)
            return (x - mu) * jax.lax.rsqrt(var + EPS_LN) * g + b
        key = jax.random.key(seed)
        ks = jax.random.split(key, 8)
        s = 1.0 / np.sqrt(C)
        return {'x': jax.random.normal(ks[0], (N, F, C), jnp.float32), 'Wqkv': jax.random.uniform(ks[1], (3 * C, C), jnp.float32, -s, s), 'ln1_g': jnp.ones((C,), jnp.float32), 'ln1_b': jnp.zeros((C,), jnp.float32), 'W1': jax.random.uniform(ks[2], (C, C), jnp.float32, -s, s), 'b1': jax.random.uniform(ks[3], (C,), jnp.float32, -s, s), 'W2': jax.random.uniform(ks[4], (C, C), jnp.float32, -s, s), 'b2': jax.random.uniform(ks[5], (C,), jnp.float32, -s, s), 'ln2_g': jnp.ones((C,), jnp.float32), 'ln2_b': jnp.zeros((C,), jnp.float32)}
    _L0_mix_all = _L0_mix_setup()
    _L0_mix_in = {k: v for k, v in _L0_mix_all.items() if k in ('Wqkv', 'ln1_g', 'ln1_b', 'W1', 'b1', 'W2', 'b2', 'ln2_g', 'ln2_b')}
    del _L0_mix_all

    def _L0_ffn_setup():
        import math
        import jax, jax.numpy as jnp
        import numpy as np
        CAPACITY_FACTOR = 1.25
        key = jax.random.key(seed)
        ks = jax.random.split(key, 5)
        B, L, D, F, E = (8, 1024, 256, 1024, 8)
        h = jax.random.normal(ks[0], (B, L, D), dtype=jnp.float32)
        gate_w = jax.random.normal(ks[1], (D, E), dtype=jnp.float32) * 0.02
        gate_b = jnp.zeros((E,), dtype=jnp.float32)
        w1 = jax.random.normal(ks[2], (E, D, F), dtype=jnp.float32) * (1.0 / math.sqrt(D))
        b1 = jnp.zeros((E, F), dtype=jnp.float32)
        w2 = jax.random.normal(ks[3], (E, F, D), dtype=jnp.float32) * (1.0 / math.sqrt(F))
        b2 = jnp.zeros((E, D), dtype=jnp.float32)
        return {'h': h, 'gate_w': gate_w, 'gate_b': gate_b, 'w1': w1, 'b1': b1, 'w2': w2, 'b2': b2}
    _L0_ffn_all = _L0_ffn_setup()
    _L0_ffn_in = {k: v for k, v in _L0_ffn_all.items() if k in ('gate_w', 'gate_b', 'w1', 'b1', 'w2', 'b2')}
    del _L0_ffn_all
    return {'x': x, 'src': src, 'dst': dst, 'L0_gnn_W': _L0_gnn_in['W'], 'L0_gnn_b': _L0_gnn_in['b'], 'L0_mix_Wqkv': _L0_mix_in['Wqkv'], 'L0_mix_ln1_g': _L0_mix_in['ln1_g'], 'L0_mix_ln1_b': _L0_mix_in['ln1_b'], 'L0_mix_W1': _L0_mix_in['W1'], 'L0_mix_b1': _L0_mix_in['b1'], 'L0_mix_W2': _L0_mix_in['W2'], 'L0_mix_b2': _L0_mix_in['b2'], 'L0_mix_ln2_g': _L0_mix_in['ln2_g'], 'L0_mix_ln2_b': _L0_mix_in['ln2_b'], 'L0_ffn_gate_w': _L0_ffn_in['gate_w'], 'L0_ffn_gate_b': _L0_ffn_in['gate_b'], 'L0_ffn_w1': _L0_ffn_in['w1'], 'L0_ffn_b1': _L0_ffn_in['b1'], 'L0_ffn_w2': _L0_ffn_in['w2'], 'L0_ffn_b2': _L0_ffn_in['b2']}

def reference(x, src, dst, L0_gnn_W, L0_gnn_b, L0_mix_Wqkv, L0_mix_ln1_g, L0_mix_ln1_b, L0_mix_W1, L0_mix_b1, L0_mix_W2, L0_mix_b2, L0_mix_ln2_g, L0_mix_ln2_b, L0_ffn_gate_w, L0_ffn_gate_b, L0_ffn_w1, L0_ffn_b1, L0_ffn_w2, L0_ffn_b2):
    import jax
    import jax.numpy as jnp

    def _L0_gnn_ref(A, X, W, b):
        import jax, jax.numpy as jnp
        import numpy as np
        N_NODES = 2500
        N_EDGES = 40000
        D_IN = 256
        D_OUT = 256
        'GCNConv (PyG semantics: self-loops + symmetric norm) followed by ReLU.'
        N = X.shape[0]
        loop = jnp.arange(N, dtype=A.dtype)
        src = jnp.concatenate([A[0], loop])
        dst = jnp.concatenate([A[1], loop])
        deg = jax.ops.segment_sum(jnp.ones_like(dst, dtype=X.dtype), dst, num_segments=N)
        dinv = jnp.where(deg > 0, jax.lax.rsqrt(deg), 0.0)
        norm = dinv[src] * dinv[dst]
        h = X @ W
        msgs = h[src] * norm[:, None]
        out = jax.ops.segment_sum(msgs, dst, num_segments=N) + b
        return jax.nn.relu(out)

    def _L0_mix_ref(x, Wqkv, ln1_g, ln1_b, W1, b1, W2, b2, ln2_g, ln2_b):
        import jax, jax.numpy as jnp
        import numpy as np
        N, F, C, H = (32, 512, 256, 8)
        D = C // H
        EPS_ATTN = 1e-06
        EPS_LN = 1e-05

        def layer_norm(x, g, b):
            mu = jnp.mean(x, axis=-1, keepdims=True)
            var = jnp.var(x, axis=-1, keepdims=True)
            return (x - mu) * jax.lax.rsqrt(var + EPS_LN) * g + b
        n, f, c = x.shape
        qkv = jnp.einsum('nfc,oc->nfo', x, Wqkv)
        q, k, v = jnp.split(qkv, 3, axis=-1)
        q = q.reshape(n, f, H, D)
        k = k.reshape(n, f, H, D)
        v = v.reshape(n, f, H, D)
        q = jax.nn.elu(q) + 1.0
        k = jax.nn.elu(k) + 1.0
        kv = jnp.einsum('nshd,nshm->nhmd', k, v)
        ksum = jnp.sum(k, axis=1)
        z = 1.0 / (jnp.einsum('nlhd,nhd->nlh', q, ksum) + EPS_ATTN)
        t = jnp.einsum('nlhd,nhmd,nlh->nlhm', q, kv, z)
        t = t.reshape(n, f, c)
        x1 = layer_norm(t + x, ln1_g, ln1_b)
        h = jax.nn.gelu(jnp.einsum('nfc,oc->nfo', x1, W1) + b1, approximate=False)
        y = jnp.einsum('nfc,oc->nfo', h, W2) + b2
        return layer_norm(y + x1, ln2_g, ln2_b)

    def _L0_ffn_ref(h, gate_w, gate_b, w1, b1, w2, b2):
        import math
        import jax, jax.numpy as jnp
        import numpy as np
        CAPACITY_FACTOR = 1.25
        B, L, D = h.shape
        E = gate_w.shape[1]
        T = B * L
        C = max(1, math.ceil(CAPACITY_FACTOR * T / E))
        x = h.reshape(T, D)
        logits = x @ gate_w + gate_b
        probs = jax.nn.softmax(logits, axis=-1)
        idx = jnp.argmax(probs, axis=-1)
        prb = jnp.take_along_axis(probs, idx[:, None], axis=1)[:, 0]
        one_hot = jax.nn.one_hot(idx, E, dtype=jnp.float32)
        pos = (jnp.cumsum(one_hot, axis=0) * one_hot).sum(-1).astype(jnp.int32) - 1
        kept = pos < C
        pos_safe = jnp.where(kept, pos, C)
        buf = jnp.zeros((E, C, D), dtype=h.dtype).at[idx, pos_safe].set(x, mode='drop')
        hmid = jax.nn.relu(jnp.einsum('ecd,edf->ecf', buf, w1) + b1[:, None, :])
        ybuf = jnp.einsum('ecf,efd->ecd', hmid, w2) + b2[:, None, :]
        pos_g = jnp.minimum(pos, C - 1)
        y_tok = ybuf[idx, pos_g] * (prb * kept)[:, None]
        y = y_tok.reshape(B, L, D)
        y = jnp.nan_to_num(y, nan=0.0, posinf=10000.0, neginf=-10000.0)
        return y
    edge_index = jnp.stack([src, dst])
    xn = _layernorm(x, axis=-1)
    x = x + _L0_gnn_ref(edge_index, xn, L0_gnn_W, L0_gnn_b) + _L0_mix_ref(xn[None], L0_mix_Wqkv, L0_mix_ln1_g, L0_mix_ln1_b, L0_mix_W1, L0_mix_b1, L0_mix_W2, L0_mix_b2, L0_mix_ln2_g, L0_mix_ln2_b)[0]
    x = x + _L0_ffn_ref(_layernorm(x, axis=-1)[None], L0_ffn_gate_w, L0_ffn_gate_b, L0_ffn_w1, L0_ffn_b1, L0_ffn_w2, L0_ffn_b2)[0]
    return x

_drawn_inputs = setup_inputs


def setup_inputs(seed=0):
    import zlib

    import numpy as np

    out = dict(_drawn_inputs(seed))
    spreads = {'L0_mix_ln1_g': (1.0, 0.2),
     'L0_mix_ln1_b': (0.0, 0.1),
     'L0_mix_ln2_g': (1.0, 0.2),
     'L0_mix_ln2_b': (0.0, 0.1),
     'L0_ffn_gate_b': (0.0, 0.1),
     'L0_ffn_b1': (0.0, 0.8),
     'L0_ffn_b2': (0.0, 0.8)}
    factors = {'L0_gnn_b': 8.0, 'L0_mix_Wqkv': 8.0, 'L0_mix_b1': 8.0, 'L0_mix_b2': 2.89}
    for name, (base, spread) in spreads.items():
        noise = np.random.default_rng([zlib.crc32(name.encode()), seed]).standard_normal(out[name].shape)
        drawn = base * np.exp(spread * noise) if base else spread * noise
        out[name] = jnp.asarray(drawn.astype(out[name].dtype))
    for name, factor in factors.items():
        out[name] = (out[name] * factor).astype(out[name].dtype)
    return out
```

```python
from contextlib import ExitStack

import numpy as np

import concourse.bass as bass
from concourse import mybir

ALU = mybir.AluOpType
ACT = mybir.ActivationFunctionType
F32 = mybir.dt.float32
BF16 = mybir.dt.bfloat16
I32 = mybir.dt.int32
I16 = mybir.dt.int16
AX = mybir.AxisListType

P = 128
N = 6250
C = 256
CH = C // P
E = 200000
NBLK = -(-N // P)
NPAD = NBLK * P
NCHUNK = -(-E // P)
NT = -(-NCHUNK // P)
EPAD = NT * P * P
PAD_DST = 1 << 20
PER = 33
NITEM = NBLK * PER
assert NITEM >= NCHUNK + NBLK - 1 and NITEM <= NT * P
HB = 16
NHB = NT * P // HB
RING = 11
LAG = 4
PSLOT = 3
H, DH = 8, C // 8
EXP = 8
F = 1024
CAP = -(-5 * N // (4 * EXP))
SLOTS = EXP * CAP
SLOTS9 = (EXP + 1) * CAP
ROW = C + 4
NOWHERE = 1 << 17
EPS = 1e-5
EPS_ATTN = 1e-6
FT = F // P
RT = -(-CAP // P)
FLT_MAX = 3.4028234e38
LAST = N - (NBLK - 1) * P


def wait(eng, sem, value):
    if isinstance(value, int) and value <= 0:
        return
    eng.wait_ge(sem, value)


def wait_apart(eng, sem, value, long_sem, long_value):
    if isinstance(value, int):
        if value > 0:
            eng.wait_ge(sem, value)
        return
    value = eng.to_reg(value)
    eng.wait_ge(long_sem, long_value)
    eng.wait_ge(sem, value)


def build(nc, x, srcR, dstR, gW, gb, WqkvT, ln1g, ln1b, W1T, b1, W2T, b2, ln2g, ln2b, gateW, gateb,
          w1, fb1, w2, fb2, out):
    table = nc.dram_tensor("node_rows", (NPAD, C), F32, kind="Internal").ap()
    slots = nc.dram_tensor("expert_rows", (SLOTS9, ROW), F32, kind="Internal").ap()

    with ExitStack() as top:
        names = {}

        def sb(name, shape, dt=F32, st=top):
            return st.enter_context(nc.sbuf_tensor(name, shape, dt))

        def ps(name, shape, st):
            return st.enter_context(nc.psum_tensor(name, shape, F32))

        def sem(name, st=top):
            return st.enter_context(nc.semaphore(name))

        ident = sb("ident", [P, P])
        col = sb("col", [P, P])
        eps_ln = sb("eps_ln", [P, 1])
        fb1_sb = sb("fb1_sb", [P, EXP, FT])
        dma_fb = sem("dma_fb")
        dma_empty = sem("dma_empty")
        dma_out = sem("dma_out")
        consts = sem("consts")

        with ExitStack() as mid:
            acc = sb("acc", [P, NBLK, ROW], st=mid)
            res = sb("res", [P, NBLK, C], st=mid)
            src_item = sb("src_item", [P, NT * P], I32, st=mid)
            dst_item = sb("dst_item", [P, NT * P], st=mid)
            blk_item = sb("blk_item", [1, LAG + NT * P], I16, st=mid)
            rstd = sb("rstd", [P, NBLK], st=mid)
            nmr = sb("nmr", [P, NBLK], st=mid)
            dinv = sb("dinv", [P, NBLK], st=mid)
            kvz = sb("kvz", [P, CH, 2 * P], st=mid)
            headmask = sb("headmask", [P, P], st=mid)
            w1t_sb = sb("w1t_sb", [P, CH, C], st=mid)
            w2t_sb = sb("w2t_sb", [P, CH, C], st=mid)
            wq_sb = sb("wq_sb", [P, CH, 3 * C], st=mid)
            bias_b = {k: sb("bc_" + k, [P, C], st=mid) for k in ("gb", "ln2g", "ln2b")}
            b2row = sb("b2row", [1, C], st=mid)
            ones_row = sb("ones_row", [1, P], st=mid)
            cols = {k: sb("col_" + k, [P, CH], st=mid) for k in ("b1", "ln1g", "ln1b")}
            gate_sb = sb("gate_sb", [P, CH, EXP], st=mid)
            gateb_b = sb("gateb_b", [P, EXP], st=mid)
            dma_w = sem("dma_w", mid)

            prepare(nc, mid, sb, ps, sem, locals())
            aggregate_and_mix(nc, sb, ps, sem, locals())
            route(nc, sb, ps, sem, locals())
        experts(nc, sb, ps, sem, locals())


def rsqrt_steps(nc, link, out, var, tmp, eps):
    link(nc.vector.scalar_tensor_tensor(tmp, var, eps, out, ALU.add, ALU.mult))
    link(nc.vector.tensor_tensor(tmp, tmp, out, ALU.mult))
    link(nc.vector.tensor_scalar(tmp, tmp, -0.5, 1.5, ALU.mult, ALU.add))
    link(nc.vector.tensor_tensor(out, out, tmp, ALU.mult))


def prepare(nc, mid, sb, ps, sem, g):
    (x, srcR, dstR, table, acc, res, src_item, dst_item, blk_item, rstd, nmr, dinv, kvz, headmask, ident,
     col, eps_ln, wq_sb, w1t_sb, w2t_sb, dma_w, consts) = (g[k] for k in (
        "x", "srcR", "dstR", "table", "acc", "res", "src_item", "dst_item", "blk_item", "rstd", "nmr",
        "dinv", "kvz", "headmask", "ident", "col", "eps_ln", "wq_sb", "w1t_sb", "w2t_sb", "dma_w", "consts"))
    XL = 8
    NXL = -(-NBLK // XL)
    with ExitStack() as st:
        src_rows = sb("src_rows", [P, NT, P], I32, st)
        dst_rows = sb("dst_rows", [P, NT, P], I32, st)
        next_first = sb("next_first", [P, NT, 1], I32, st)
        gw_sb = sb("gw_sb", [P, CH, C], st=st)
        blk_i = sb("blk_i", [P, 2, NT], I32, st)
        key = sb("key", [P, 2, NT], st=st)
        col256 = sb("col256", [P, 2 * P], st=st)
        col128x = sb("col128x", [P, P], st=st)
        part = sb("part", [P, 1], st=st)
        chunk0 = sb("chunk0", [P, NT], st=st)
        chunkn = sb("chunkn", [P, NT], st=st)
        band_m = sb("band_m", [P, 2 * P], BF16, st)
        bandf = sb("bandf", [P, 2, 2 * P], st=st)
        rowf = sb("rowf", [P, 2, 2, P], st=st)
        brow = sb("brow", [1, P], st=st)
        code_i = sb("code_i", [P, NT * P], I32, st)
        code_hi = sb("code_hi", [P, NT * P], BF16, st)
        code_lo = sb("code_lo", [P, NT * P], BF16, st)
        iota_h = sb("iota_h", [P, P, HB], BF16, st)
        one_lo = sb("one_lo", [P, 2, P, HB], BF16, st)
        one_hi = sb("one_hi", [P, 2, NBLK, HB], BF16, st)
        stats = sb("stats", [P, 2, 6], st=st)
        mv = sb("mv", [P, NBLK, 2], st=st)
        tmp = sb("tmp", [P, NBLK], st=st)
        xn = sb("xn", [P, 2, C], st=st)
        xnT = sb("xnT", [P, 2, CH, P], st=st)
        kr = sb("kr", [P, C], st=st)
        ke = sb("ke", [P, 2, C], st=st)
        kf = sb("kf", [P, 2, C], st=st)
        v1 = sb("v1", [P, 2, CH, P + 2], st=st)

        p_it = ps("p_it", [P, 4, P], st)
        p_row = ps("p_row", [P, 512], st)
        p_deg = ps("p_deg", [P, 512], st)
        p_tr = ps("p_tr", [P, 4, P], st)
        p_h = ps("p_h", [P, 512], st)
        p_kv = ps("p_kv", [P, 512], st)
        p_k0 = ps("p_k0", [P, 512], st)
        p_k1 = ps("p_k1", [P, 512], st)
        p_kk = [p_k0, p_k1]

        dma_rows, dma_gw = sem("dma_rows", st), sem("dma_gw", st)
        dma_x = [sem(f"dma_x{i}", st) for i in range(NXL)]
        dma_tab = sem("dma_tab", st)
        bands = sem("bands", st)
        item_ps = sem("item_ps", st)
        items = sem("items", st)
        stat = sem("stat", st)
        dve = sem("dve1", st)
        var_ok, std_ok, rstd_ok = sem("var_ok", st), sem("std_ok", st), sem("rstd_ok", st)
        xn_ok, tr_ok, xnT_ok = sem("xn_ok", st), sem("tr_ok", st), sem("xnT_ok", st)
        h_ok, h_out = sem("h_ok", st), sem("h_out", st)
        kv_ok, kr_ok, kv_act, k_ok, kv_acc = (sem(n, st) for n in ("kv_ok", "kr_ok", "kv_act", "k_ok", "kv_acc"))
        onehots, hist = sem("onehots", st), sem("hist", st)
        deg_var, deg_std, dinv_ok, scaled = (sem(n, st) for n in ("deg_var", "deg_std", "dinv_ok", "scaled"))
        scaled_a = sem("scaled_a", st)
        kvz_ok = sem("kvz_ok", st)
        block = st.enter_context(nc.Block())

        HALF = 25

        @block.sync
        def _(sp):
            sp.dma_start(dst_rows[:], dstR[0:NT * P, :].rearrange("(t p) e -> p t e", p=P)).then_inc(dma_rows, 16)
            with nc.allow_non_contiguous_dma("first destination of every chunk"):
                sp.dma_start(next_first[:], dstR[1:NT * P + 1, 0:1].rearrange("(t p) e -> p t e", p=P)
                             ).then_inc(dma_rows, 16)
            sp.dma_start(src_rows[:], srcR[0:NT * P, :].rearrange("(t p) e -> p t e", p=P)).then_inc(dma_rows, 16)
            for i in range(NXL):
                n = min(XL, NBLK - i * XL)
                sp.dma_start(res[:, i * XL:i * XL + n, :],
                             x[i * XL * P:(i * XL + n) * P, :].rearrange("(b p) c -> p b c", p=P)
                             ).then_inc(dma_x[i], 16)
            sp.dma_start(gw_sb[:], g["gW"].rearrange("(k p) c -> p k c", p=P)).then_inc(dma_gw, 16)
            sp.dma_start(wq_sb[:], g["WqkvT"].rearrange("(k p) c -> p k c", p=P)).then_inc(dma_gw, 16)
            sp.dma_start(w1t_sb[:], g["W1T"].rearrange("(k p) c -> p k c", p=P)).then_inc(dma_w, 16)
            sp.dma_start(w2t_sb[:], g["W2T"].rearrange("(k p) c -> p k c", p=P)).then_inc(dma_w, 16)
            sp.dma_start(g["gate_sb"][:], g["gateW"].rearrange("(k p) c -> p k c", p=P)).then_inc(dma_w, 16)
            for k, v in (("gb", g["gb"]), ("ln2g", g["ln2g"]), ("ln2b", g["ln2b"])):
                sp.dma_start(g["bias_b"][k][:], v.rearrange("(a c) -> a c", a=1).broadcast_to([P, C])
                             ).then_inc(dma_w, 16)
            sp.dma_start(g["gateb_b"][:], g["gateb"].rearrange("(a c) -> a c", a=1).broadcast_to([P, EXP])
                         ).then_inc(dma_w, 16)
            sp.dma_start(g["b2row"][:], g["b2"].rearrange("(a c) -> a c", a=1)).then_inc(dma_w, 16)
            with nc.allow_non_contiguous_dma("small per-feature columns"):
                for k in ("b1", "ln1g", "ln1b"):
                    sp.dma_start(g["cols"][k][:], g[k].rearrange("(k p) -> p k", p=P)).then_inc(dma_w, 16)
            sp.wait_ge(scaled, HALF)
            sp.dma_start(table[0:HALF * P, :].rearrange("(b p) c -> p b c", p=P), acc[:, 0:HALF, 0:C]
                         ).then_inc(dma_tab, 16)
            sp.wait_ge(scaled_a, NBLK - HALF)
            sp.dma_start(table[HALF * P:NPAD, :].rearrange("(b p) c -> p b c", p=P), acc[:, HALF:NBLK, 0:C]
                         ).then_inc(dma_tab, 16)
            sp.wait_ge(dma_tab, 32)

        @block.gpsimd
        def _(pool):
            nc.gpsimd.iota(col[:], [[1, P]], 0, 0, allow_small_or_imprecise_dtypes=True).then_inc(consts, 1)
            nc.gpsimd.iota(col256[:], [[1, 2 * P]], 0, 0, allow_small_or_imprecise_dtypes=True).then_inc(consts, 1)
            nc.gpsimd.iota(col128x[:], [[P, P]], 0, 0, allow_small_or_imprecise_dtypes=True).then_inc(consts, 1)
            nc.gpsimd.iota(part[:], [[0, 1]], 0, 1, allow_small_or_imprecise_dtypes=True).then_inc(consts, 1)
            nc.gpsimd.iota(chunk0[:], [[P * P, NT]], 0, P, allow_small_or_imprecise_dtypes=True).then_inc(consts, 1)
            nc.gpsimd.iota(chunkn[:], [[P, NT]], 0, 1, allow_small_or_imprecise_dtypes=True).then_inc(consts, 1)
            nc.gpsimd.iota(iota_h[:], [[1, P], [0, HB]], 0, 0, allow_small_or_imprecise_dtypes=True
                           ).then_inc(consts, 1)
            nc.gpsimd.memset(ident[:], 0.0).then_inc(consts, 1)
            nc.gpsimd.memset(headmask[:], 1.0).then_inc(consts, 1)
            nc.gpsimd.memset(v1[:], 1.0).then_inc(consts, 1)
            nc.gpsimd.memset(eps_ln[:], EPS).then_inc(consts, 1)
            nc.gpsimd.memset(g["ones_row"][:], 1.0).then_inc(consts, 1)
            nc.gpsimd.memset(blk_item[:], 0).then_inc(consts, 1)
            pool.wait_ge(consts, 13)
            nc.gpsimd.affine_select(ident[:], ident[:], [[-1, P]], ALU.not_equal, 1.0, 0, 1).then_inc(consts, 1)
            hm = headmask[:].rearrange("p (h d) -> p h d", d=DH)
            nc.gpsimd.affine_select(hm, hm, [[-DH, P // DH], [0, DH]], ALU.is_ge, 0.0, 0, 1).then_inc(consts, 1)
            pool.wait_ge(consts, 15)
            nc.gpsimd.affine_select(hm, hm, [[DH, P // DH], [0, DH]], ALU.is_ge, 0.0, DH - 1, -1
                                    ).then_inc(consts, 1)

        @block.vector
        def _(v):
            n = [0]

            def link(ins):
                n[0] += 1
                ins.then_inc(dve, 1)
                v.wait_ge(dve, n[0])

            v.wait_ge(consts, 16)
            v.wait_ge(dma_rows, 48)
            nc.vector.tensor_scalar(blk_i[:, 0, :], dst_rows[:, :, 0], 7, None, ALU.arith_shift_right).then_inc(dve, 1)
            n[0] += 1
            link(nc.vector.tensor_scalar(blk_i[:, 1, :], next_first[:, :, 0], 7, None, ALU.arith_shift_right))
            link(nc.vector.memset(blk_i[0:1, 0, 0:1], 0))
            nc.vector.tensor_scalar(key[:, 0, :], blk_i[:, 0, :], part[:, 0:1], None, ALU.add).then_inc(dve, 1)
            n[0] += 1
            link(nc.vector.tensor_scalar(key[:, 1, :], blk_i[:, 1, :], part[:, 0:1], 1.0, ALU.add, ALU.add))
            for t in range(NT):
                link(nc.vector.tensor_scalar(band_m[:], col256[:], key[:, 1, t:t + 1], None, ALU.is_lt))
                nc.vector.scalar_tensor_tensor(bandf[:, t % 2, :], col256[:], key[:, 0, t:t + 1], band_m[:],
                                               ALU.is_ge, ALU.mult).then_inc(bands, 1)
                nc.vector.tensor_copy(rowf[:, t % 2, 0, :], src_rows[:, t, :]).then_inc(bands, 1)
                nc.vector.tensor_scalar(rowf[:, t % 2, 1, :], dst_rows[:, t, :], chunk0[:, t:t + 1], None,
                                        ALU.add).then_inc(bands, 1)
                v.wait_ge(bands, 3 * t + 3)
                v.wait_ge(item_ps, t + 1)
                w = slice(t * P, (t + 1) * P)
                nc.vector.tensor_copy(src_item[:, w], p_it[:, 0, :]).then_inc(items, 1)
                nc.vector.scalar_tensor_tensor(dst_item[:, w], p_it[:, 1, :], float(t * P * P), col128x[:],
                                               ALU.subtract, ALU.subtract).then_inc(items, 1)
                nc.vector.scalar_tensor_tensor(brow[:], p_row[0:1, 0:P], -1.0, col[0:1, :],
                                               ALU.mult, ALU.add).then_inc(items, 1)
                v.wait_ge(items, 3 * t + 3)
                link(nc.vector.tensor_scalar(blk_item[0:1, LAG + t * P:LAG + (t + 1) * P], brow[:], float(t * P),
                                             float(NBLK - 1), ALU.add, ALU.min))
            for b in range(NBLK):
                if b % XL == 0:
                    v.wait_ge(dma_x[b // XL], 16)
                link(nc.vector.bn_stats(stats[:, b % 2, :], res[:, b, :]))
                nc.vector.bn_aggr(mv[:, b, :], stats[:, b % 2, :]).then_inc(stat, 1)
            v.wait_ge(stat, NBLK)
            nc.vector.tensor_copy(tmp[:], mv[:, :, 1]).then_inc(var_ok, 1)
            v.wait_ge(std_ok, 1)
            link(nc.vector.reciprocal(rstd[:], rstd[:]))
            rsqrt_steps(nc, link, rstd[:], mv[:, :, 1], tmp[:], EPS)
            nc.vector.scalar_tensor_tensor(nmr[:], mv[:, :, 0], -1.0, rstd[:], ALU.mult, ALU.mult
                                           ).then_inc(rstd_ok, 1)
            flat = dst_rows[:].rearrange("p t e -> p (t e)")
            link(nc.vector.tensor_scalar(code_i[:], flat, 7, None, ALU.arith_shift_right))
            link(nc.vector.tensor_copy(code_hi[:], code_i[:]))
            link(nc.vector.tensor_scalar(code_i[:], flat, P - 1, None, ALU.bitwise_and))
            link(nc.vector.tensor_copy(code_lo[:], code_i[:]))

            def onehot(j, u):
                c_lo = code_lo[:, bass.ds(j * HB, HB)].rearrange("p (a c) -> p a c", a=1)
                c_hi = code_hi[:, bass.ds(j * HB, HB)].rearrange("p (a c) -> p a c", a=1)
                wait(v, hist, j - 1)
                nc.vector.tensor_tensor(one_lo[:, u], iota_h[:], c_lo.broadcast_to([P, P, HB]), ALU.is_equal
                                        ).then_inc(onehots, 1)
                nc.vector.tensor_tensor(one_hi[:, u], iota_h[:, 0:NBLK, :], c_hi.broadcast_to([P, NBLK, HB]),
                                        ALU.is_equal).then_inc(onehots, 1)

            def keys_of(b, u):
                v.wait_ge(kv_act, b + 1)
                wait(v, kv_acc, b - 1)
                nc.vector.scalar_tensor_tensor(kf[:, u, :], p_kv[:, 0:C], 0.0, ke[:, u, :], ALU.max, ALU.add
                                               ).then_inc(k_ok, 1)

            for u in range(2):
                onehot(2 * u, 0)
                onehot(2 * u + 1, 1)
                keys_of(u, u)
            with v.Fori(1, NBLK // 2) as it:
                for u in range(2):
                    onehot(it * 4 + 2 * u, 0)
                    onehot(it * 4 + 2 * u + 1, 1)
                    keys_of(it * 2 + u, u)
            for j in range(4 * (NBLK // 2), NHB):
                onehot(j, j % 2)
            keys_of(NBLK - 1, 0)
            v.wait_ge(kv_acc, NBLK)
            for a in range(CH):
                link(nc.vector.tensor_tensor(kvz[:, a, 0:P], p_kk[a][:, 0:P], headmask[:], ALU.mult))
                link(nc.vector.tensor_scalar(kvz[:, a, P:2 * P], headmask[:], p_kk[a][:, P:P + 1], None, ALU.mult))
            v.wait_ge(hist, NHB)
            nc.vector.tensor_scalar(tmp[:], p_deg[:, 0:NBLK], 1.0, None, ALU.add).then_inc(deg_var, 1)
            v.wait_ge(deg_std, 1)
            v.wait_ge(deg_var, 1)
            link(nc.vector.reciprocal(dinv[:], dinv[:]))
            link(nc.vector.tensor_tensor(mv[:, :, 0], dinv[:], dinv[:], ALU.mult))
            link(nc.vector.tensor_tensor(mv[:, :, 0], mv[:, :, 0], tmp[:], ALU.mult))
            link(nc.vector.tensor_scalar(mv[:, :, 0], mv[:, :, 0], -0.5, 1.5, ALU.mult, ALU.add))
            nc.vector.tensor_tensor(dinv[:], dinv[:], mv[:, :, 0], ALU.mult).then_inc(dinv_ok, 1)
            v.wait_ge(dinv_ok, 1)
            v.wait_ge(h_out, NBLK)
            for b in range(HALF):
                nc.vector.tensor_scalar(acc[:, b, 0:C], acc[:, b, 0:C], dinv[:, b:b + 1], None, ALU.mult
                                        ).then_inc(scaled, 1)

        @block.scalar
        def _(s):
            s.wait_ge(consts, 16)
            s.wait_ge(var_ok, 1)
            nc.scalar.activation(rstd[:], tmp[:], ACT.Sqrt, bias=eps_ln[:]).then_inc(std_ok, 1)
            s.wait_ge(rstd_ok, 1)

            def node_block(b, u):
                wait(s, tr_ok, b - 1)
                nc.scalar.activation(xn[:, u, :], res[:, bass.ds(b, 1), :].rearrange("p a c -> p (a c)"),
                                     ACT.Identity, scale=rstd[:, bass.ds(b, 1)], bias=nmr[:, bass.ds(b, 1)]
                                     ).then_inc(xn_ok, 1)
                s.wait_ge(tr_ok, b + 1)
                wait(s, kv_ok, b - 1)
                nc.scalar.copy(xnT[:, u], p_tr[:, 0:CH, :]).then_inc(xnT_ok, 1)
                s.wait_ge(h_ok, b + 1)
                nc.scalar.copy(acc[:, bass.ds(b, 1), 0:C].rearrange("p a c -> p (a c)"), p_h[:, 0:C]
                               ).then_inc(h_out, 1)
                s.wait_ge(kv_ok, b + 1)
                wait(s, kv_act, b)
                nc.scalar.activation(kr[:], p_kv[:, 0:C], ACT.Relu, scale=-1.0).then_inc(kr_ok, 1)
                s.wait_ge(kr_ok, b + 1)
                wait(s, k_ok, b - 1)
                wait(s, kv_acc, b - 1)
                nc.scalar.copy(v1[:, u, :, 0:P], p_kv[:, C:2 * C].rearrange("p (a c) -> p a c", a=CH)
                               )
                nc.scalar.activation(ke[:, u, :], kr[:], ACT.Exp, scale=-1.0).then_inc(kv_act, 1)

            for u in range(2):
                node_block(u, u)
            with s.Fori(1, NBLK // 2) as it:
                for u in range(2):
                    node_block(it * 2 + u, u)
            node_block(NBLK - 1, 0)
            s.wait_ge(deg_var, 1)
            nc.scalar.activation(dinv[:], tmp[:], ACT.Sqrt).then_inc(deg_std, 1)
            s.wait_ge(dinv_ok, 1)
            for b in range(HALF, NBLK):
                nc.scalar.mul(acc[:, b, 0:C], acc[:, b, 0:C], dinv[:, b:b + 1]).then_inc(scaled_a, 1)

        @block.tensor
        def _(t_):
            pe = nc.tensor
            t_.wait_ge(consts, 16)
            for t in range(NT):
                t_.wait_ge(bands, 3 * t + 3)
                wait(t_, items, 3 * t)
                for k, wt in enumerate([t - 1, t] if t else [t]):
                    f = slice(P, 2 * P) if wt < t else slice(0, P)
                    lastk = wt == t
                    for q in range(2):
                        pe.matmul(p_it[:, q, :], rowf[:, wt % 2, q, :], bandf[:, wt % 2, f],
                                  start=(k == 0 and q == 0), stop=lastk, skip_group_check=True)
                    mm = pe.matmul(p_row[0:1, 0:P], chunkn[:, wt:wt + 1], bandf[:, wt % 2, f],
                                   start=(k == 0), stop=lastk)
                mm.then_inc(item_ps, 1)
            t_.wait_ge(dma_gw, 32)

            def transposes(b, u):
                t_.wait_ge(xn_ok, b + 1)
                wait(t_, xnT_ok, b)
                for a in range(CH):
                    mm = pe.transpose(p_tr[:, a, :], xn[:, u, a * P:(a + 1) * P], ident[:])
                mm.then_inc(tr_ok, 1)

            def products(b, u):
                t_.wait_ge(xnT_ok, b + 1)
                wait(t_, h_out, b)
                for a in range(CH):
                    mm = pe.matmul(p_h[:, 0:C], xnT[:, u, a, :], gw_sb[:, a, :], start=(a == 0), stop=(a == CH - 1))
                mm.then_inc(h_ok, 1)
                wait(t_, k_ok, b)
                for a in range(CH):
                    mm = pe.matmul(p_kv[:], xnT[:, u, a, :], wq_sb[:, a, C:3 * C], start=(a == 0),
                                   stop=(a == CH - 1))
                mm.then_inc(kv_ok, 1)

            def kv_sums(b, u, rows, first, last):
                t_.wait_ge(k_ok, b + 1)
                for a in range(CH):
                    mm = pe.matmul(p_kk[a][:, 0:P + 2], kf[0:rows, u, a * P:(a + 1) * P], v1[0:rows, u, a, :],
                                   start=first, stop=last)
                mm.then_inc(kv_acc, 1)

            def hist_step(j, u, first=False, last=False):
                t_.wait_ge(onehots, j * 2 + 2)
                for c in range(HB):
                    mm = pe.matmul(p_deg[:, 0:NBLK], one_lo[:, u, :, c], one_hi[:, u, :, c],
                                   start=(first and c == 0), stop=(last and c == HB - 1))
                mm.then_inc(hist, 1)

            for u in range(2):
                transposes(u, u)
                hist_step(2 * u, 0, first=(u == 0))
                products(u, u)
                hist_step(2 * u + 1, 1)
                kv_sums(u, u, P, u == 0, False)
            with t_.Fori(1, NBLK // 2) as it:
                for u in range(2):
                    transposes(it * 2 + u, u)
                    hist_step(it * 4 + 2 * u, 0)
                    products(it * 2 + u, u)
                    hist_step(it * 4 + 2 * u + 1, 1)
                    kv_sums(it * 2 + u, u, P, False, False)
            for j in range(4 * (NBLK // 2), NHB):
                hist_step(j, j % 2, last=(j == NHB - 1))
            transposes(NBLK - 1, 0)
            products(NBLK - 1, 0)
            kv_sums(NBLK - 1, 0, LAST, False, True)


def aggregate_and_mix(nc, sb, ps, sem, g):
    (table, acc, res, src_item, dst_item, blk_item, rstd, nmr, kvz, ident, col, wq_sb, w1t_sb, w2t_sb,
     dma_w) = (g[k] for k in ("table", "acc", "res", "src_item", "dst_item", "blk_item", "rstd", "nmr", "kvz",
                              "ident", "col", "wq_sb", "w1t_sb", "w2t_sb", "dma_w"))
    slots, dma_empty = g["slots"], g["dma_empty"]
    NDMA_W = 11
    THIRD = PER // 3
    with ExitStack() as st:
        ring = sb("ring", [P, RING, C], st=st)
        sel = sb("sel", [P, RING, P], st=st)
        idx = sb("idx", [P, PER], I32, st)
        empty = sb("empty", [P, ROW], st=st)
        eps_at = sb("eps_at", [P, 1], st=st)
        xn = sb("xn_m", [P, C], st=st)
        xnT = sb("xnT_m", [P, CH, P], st=st)
        qr = sb("qr", [P, CH, P], st=st)
        qe = sb("qe", [P, CH, P], st=st)
        qT = sb("qT", [P, CH, P], st=st)
        den = sb("den", [P, CH, P], st=st)
        t = sb("t_m", [P, CH, P], st=st)
        st1, st2 = sb("st1", [P, 6], st=st), sb("st2", [P, 6], st=st)
        mv1, mv2 = sb("mv1", [P, 2], st=st), sb("mv2", [P, 2], st=st)
        sd1, sd2 = sb("sd1", [P, 1], st=st), sb("sd2", [P, 1], st=st)
        r1, r2 = sb("r1", [P, 1], st=st), sb("r2", [P, 1], st=st)
        nm1, nm2 = sb("nm1", [P, 1], st=st), sb("nm2", [P, 1], st=st)
        tmp1, tmp2 = sb("tmp1", [P, 1], st=st), sb("tmp2", [P, 1], st=st)
        x1n = sb("x1n", [P, C], st=st)
        x1T = sb("x1T", [P, CH, P], st=st)
        gT = sb("gT", [P, CH, P], st=st)
        yn = sb("yn", [P, C], st=st)
        p_item = [ps(f"p_item{i}", [P, 512], st) for i in range(PSLOT)]
        p_t = ps("p_t", [P, 4, P], st)
        p_q = ps("p_q", [P, 4, P], st)
        p_nd = ps("p_nd", [P, CH, 2 * P], st)
        p_g = ps("p_g", [P, 4, P], st)
        p_y = ps("p_y", [P, 512], st)

        gathered = [sem(f"gathered{i}", st) for i in range(RING)]
        multiplied = sem("multiplied", st)
        selected = sem("selected", st)
        added = sem("added", st)
        idx_ok = sem("idx_ok", st)
        const2 = sem("const2", st)
        xn_ok, tr1_ok, xnT_ok, q_ps, q_rel, q_exp, qT_ok, nd_ps, den_ok = (sem("m_" + n, st) for n in (
            "xn", "tr1", "xnT", "qps", "qrel", "qexp", "qT", "ndps", "den"))
        t_rec, t_mul, t_add, s_st1, var1, std1, n1 = (sem("m_" + n, st) for n in (
            "trec", "tmul", "tadd", "st1", "var1", "std1", "n1"))
        x1n_ok, tr2_ok, x1T_ok, g_ps, gelu_ok, y_ps = (sem("m_" + n, st) for n in (
            "x1n", "tr2", "x1T", "gps", "gelu", "yps"))
        s_st2, var2, std2, n2, yn_ok, fin = (sem("m_" + n, st) for n in ("st2", "var2", "std2", "n2", "yn", "fin"))
        block = st.enter_context(nc.Block())

        def dyn(tile, b):
            return tile[:, bass.ds(b, 1), :].rearrange("p a c -> p (a c)")

        @block.sync
        def _(sp):
            sp.dma_start(g["fb1_sb"][:], g["fb1"]).then_inc(g["dma_fb"], 16)
            sp.wait_ge(const2, 3)
            full = SLOTS9 // P
            sp.dma_start(slots[0:full * P, :].rearrange("(a p) c -> p a c", p=P),
                         empty[:].rearrange("p (a c) -> p a c", a=1).broadcast_to([P, full, ROW])
                         ).then_inc(dma_empty, 16)
            sp.dma_start(slots[full * P:SLOTS9, :], empty[0:SLOTS9 - full * P, :]).then_inc(dma_empty, 16)
            sp.wait_ge(dma_empty, 32)

        @block.gpsimd
        def _(pool):
            nc.gpsimd.memset(empty[:], 0.0).then_inc(const2, 1)
            nc.gpsimd.memset(eps_at[:], EPS_ATTN).then_inc(const2, 1)
            pool.wait_ge(const2, 2)
            nc.gpsimd.memset(empty[:, C + 3:C + 4].bitcast(I32), NOWHERE).then_inc(const2, 1)

            def gathers(it):
                for k in range(PER):
                    if k % THIRD == 0:
                        pool.wait_ge(idx_ok, it * 3 + k // THIRD + 1)
                    wait_apart(pool, multiplied, it * PER + k - RING + 1, const2, 3)
                    nc.gpsimd.indirect_dma_start(ring[:, k % RING, :], None, table,
                                                 bass.IndirectOffsetOnAxis(idx[:, k:k + 1], 0)
                                                 ).then_inc(gathered[k % RING], 16)

            gathers(0)
            with pool.Fori(1, NBLK) as it:
                gathers(it)

        @block.tensor
        def _(t_):
            pe = nc.tensor
            t_.wait_ge(dma_w, 16 * NDMA_W)

            def item(it, k):
                i = it * PER + k
                t_.wait_ge(gathered[k % RING], (it * (PER // RING) + k // RING + 1) * 16)
                t_.wait_ge(selected, i + 1)
                wait(t_, added, i - PSLOT + 1)
                pe.matmul(p_item[k % PSLOT][:, 0:C], sel[:, k % RING, :], ring[:, k % RING, :],
                          start=True, stop=True).then_inc(multiplied, 1)

            def transposes_x(b):
                t_.wait_ge(xn_ok, b + 1)
                wait(t_, x1T_ok, b * 2)
                for a in range(CH):
                    mm = pe.transpose(p_t[:, a, :], xn[:, a * P:(a + 1) * P], ident[:])
                mm.then_inc(tr1_ok, 1)

            def queries(b):
                t_.wait_ge(xnT_ok, b + 1)
                wait(t_, qT_ok, b)
                for m in range(CH):
                    for a in range(CH):
                        mm = pe.matmul(p_q[:, m, :], wq_sb[:, a, m * P:(m + 1) * P], xnT[:, a, :],
                                       start=(a == 0), stop=(a == CH - 1))
                mm.then_inc(q_ps, 1)

            def attention(b):
                t_.wait_ge(qT_ok, b + 1)
                wait(t_, t_mul, b)
                for a in range(CH):
                    mm = pe.matmul(p_nd[:, a, :], qT[:, a, :], kvz[:, a, :], start=True, stop=True)
                mm.then_inc(nd_ps, 1)

            def transposes_x1(b):
                t_.wait_ge(x1n_ok, b + 1)
                t_.wait_ge(xnT_ok, b + 1)
                for a in range(CH):
                    mm = pe.transpose(p_t[:, a, :], x1n[:, a * P:(a + 1) * P], ident[:])
                mm.then_inc(tr2_ok, 1)

            def hidden(b):
                t_.wait_ge(x1T_ok, b * 2 + 2)
                wait(t_, gelu_ok, b * 2)
                for m in range(CH):
                    for a in range(CH):
                        mm = pe.matmul(p_g[:, m, :], w1t_sb[:, a, m * P:(m + 1) * P], x1T[:, a, :],
                                       start=(a == 0), stop=(a == CH - 1))
                mm.then_inc(g_ps, 1)

            def output(b):
                t_.wait_ge(gelu_ok, b * 2 + 2)
                wait(t_, yn_ok, b)
                for a in range(CH):
                    pe.matmul(p_y[:, 0:C], gT[:, a, :], w2t_sb[:, a, :], start=(a == 0), stop=False,
                              skip_group_check=True)
                for a in range(CH):
                    pe.matmul(p_y[:, a * P:(a + 1) * P], x1T[:, a, :], ident[:], start=False, stop=False,
                              skip_group_check=True)
                pe.matmul(p_y[:, 0:C], g["ones_row"][:], g["b2row"][:], start=False, stop=True,
                          skip_group_check=True).then_inc(y_ps, 1)

            def one_pass(it):
                for k in range(PER):
                    item(it, k)
                    if k == 2:
                        transposes_x(it)
                    if k == 5:
                        queries(it)
                    if k == 9:
                        attention(it)
                    if k == 21:
                        transposes_x1(it)
                    if k == 24:
                        hidden(it)
                    if k == 27:
                        output(it)

            one_pass(0)
            with t_.Fori(1, NBLK) as it:
                one_pass(it)

        @block.scalar
        def _(s):
            s.wait_ge(const2, 2)
            s.wait_ge(dma_w, 16 * NDMA_W)

            def one_pass(b):
                wait(s, tr1_ok, b)
                wait(s, t_add, b)
                nc.scalar.activation(xn[:], dyn(res, b), ACT.Identity, scale=rstd[:, bass.ds(b, 1)],
                                     bias=nmr[:, bass.ds(b, 1)]).then_inc(xn_ok, 1)
                s.wait_ge(tr1_ok, b + 1)
                wait(s, q_ps, b)
                nc.scalar.copy(xnT[:], p_t[:, 0:CH, :]).then_inc(xnT_ok, 1)
                s.wait_ge(q_ps, b + 1)
                wait(s, q_exp, b)
                nc.scalar.activation(qr[:], p_q[:, 0:CH, :], ACT.Relu, scale=-1.0).then_inc(q_rel, 1)
                s.wait_ge(q_rel, b + 1)
                wait(s, qT_ok, b)
                nc.scalar.activation(qe[:], qr[:], ACT.Exp, scale=-1.0).then_inc(q_exp, 1)
                s.wait_ge(nd_ps, b + 1)
                wait(s, t_mul, b)
                nc.scalar.activation(den[:], p_nd[:, :, P:2 * P], ACT.Identity, bias=eps_at[:]).then_inc(den_ok, 1)
                s.wait_ge(var1, b + 1)
                nc.scalar.activation(sd1[:], mv1[:, 1:2], ACT.Sqrt, bias=g["eps_ln"][:]).then_inc(std1, 1)
                s.wait_ge(n1, b * 6 + 6)
                wait(s, tr2_ok, b)
                nc.scalar.activation(x1n[:], t[:].rearrange("p a c -> p (a c)"), ACT.Identity, scale=r1[:],
                                     bias=nm1[:]).then_inc(x1n_ok, 1)
                s.wait_ge(tr2_ok, b + 1)
                wait(s, y_ps, b)
                for a in range(CH):
                    nc.scalar.activation(x1T[:, a, :], p_t[:, a, :], ACT.Identity,
                                         scale=g["cols"]["ln1g"][:, a:a + 1], bias=g["cols"]["ln1b"][:, a:a + 1]
                                         ).then_inc(x1T_ok, 1)
                s.wait_ge(g_ps, b + 1)
                for a in range(CH):
                    nc.scalar.activation(gT[:, a, :], p_g[:, a, :], ACT.Gelu, bias=g["cols"]["b1"][:, a:a + 1]
                                         ).then_inc(gelu_ok, 1)
                s.wait_ge(var2, b + 1)
                nc.scalar.activation(sd2[:], mv2[:, 1:2], ACT.Sqrt, bias=g["eps_ln"][:]).then_inc(std2, 1)
                s.wait_ge(n2, b * 6 + 6)
                wait(s, fin, b * 3)
                nc.scalar.activation(yn[:], p_y[:, 0:C], ACT.Identity, scale=r2[:], bias=nm2[:]).then_inc(yn_ok, 1)

            one_pass(0)
            with s.Fori(1, NBLK) as it:
                one_pass(it)

        @block.vector
        def _(v):
            v.wait_ge(dma_w, 16 * NDMA_W)
            regs = [v.alloc_register(f"item_block{i}") for i in range(THIRD)]

            def sources(it, q):
                nc.vector.tensor_copy(idx[:, q * THIRD:(q + 1) * THIRD],
                                      src_item[:, bass.ds(it * PER + q * THIRD, THIRD)]).then_inc(idx_ok, 1)

            def select(it, k):
                nc.vector.tensor_scalar(sel[:, k % RING, :], col[:], dst_item[:, bass.ds(it * PER + k, 1)], None,
                                        ALU.is_equal).then_inc(selected, 1)

            def add(j, slot, blk):
                v.wait_ge(multiplied, j + 1)
                wait(v, added, j)
                a = acc[:, bass.ds(blk, 1), 0:C].rearrange("p a c -> p (a c)")
                nc.vector.tensor_tensor(a, a, p_item[slot][:, 0:C], ALU.add).then_inc(added, 1)

            def queries(b):
                v.wait_ge(q_exp, b + 1)
                wait(v, nd_ps, b)
                nc.vector.scalar_tensor_tensor(qT[:], p_q[:, 0:CH, :], 0.0, qe[:], ALU.max, ALU.add
                                               ).then_inc(qT_ok, 1)

            def attention(b, n):
                if n == 0:
                    v.wait_ge(den_ok, b + 1)
                    nc.vector.reciprocal(den[:], den[:]).then_inc(t_rec, 1)
                if n == 1:
                    v.wait_ge(t_rec, b + 1)
                    wait(v, x1n_ok, b)
                    nc.vector.tensor_tensor(t[:], p_nd[:, :, 0:P], den[:], ALU.mult).then_inc(t_mul, 1)
                if n == 2:
                    v.wait_ge(t_mul, b + 1)
                    t2 = t[:].rearrange("p a c -> p (a c)")
                    nc.vector.tensor_tensor(t2, t2, xn[:], ALU.add).then_inc(t_add, 1)

            def norm(b, n, src, ready, stt, st_sem, mv, var, sd, std, r, nm, tmp, s_n):
                V = nc.vector
                if n == 0:
                    wait_apart(v, ready, b + 1, g["consts"], 16)
                    V.bn_stats(stt[:], src).then_inc(st_sem, 1)
                if n == 1:
                    wait_apart(v, st_sem, b + 1, g["consts"], 16)
                    V.bn_aggr(mv[:], stt[:]).then_inc(var, 1)
                if n == 2:
                    v.wait_ge(std, b + 1)
                    V.reciprocal(r[:], sd[:]).then_inc(s_n, 1)
                if n > 2:
                    v.wait_ge(s_n, b * 6 + n - 2)
                if n == 3:
                    V.scalar_tensor_tensor(tmp[:], mv[:, 1:2], EPS, r[:], ALU.add, ALU.mult).then_inc(s_n, 1)
                if n == 4:
                    V.tensor_tensor(tmp[:], tmp[:], r[:], ALU.mult).then_inc(s_n, 1)
                if n == 5:
                    V.tensor_scalar(tmp[:], tmp[:], -0.5, 1.5, ALU.mult, ALU.add).then_inc(s_n, 1)
                if n == 6:
                    V.tensor_tensor(r[:], r[:], tmp[:], ALU.mult).then_inc(s_n, 1)
                if n == 7:
                    V.scalar_tensor_tensor(nm[:], mv[:, 0:1], -1.0, r[:], ALU.mult, ALU.mult).then_inc(s_n, 1)

            def norm1(b, n):
                norm(b, n, t[:].rearrange("p a c -> p (a c)"), t_add, st1, s_st1, mv1, var1, sd1, std1, r1, nm1,
                     tmp1, n1)

            def norm2(b, n):
                norm(b, n, p_y[:, 0:C], y_ps, st2, s_st2, mv2, var2, sd2, std2, r2, nm2, tmp2, n2)

            def finish(b, n):
                if n == 0:
                    v.wait_ge(yn_ok, b + 1)
                    nc.vector.tensor_tensor(yn[:], yn[:], g["bias_b"]["ln2g"][:], ALU.mult).then_inc(fin, 1)
                if n == 1:
                    v.wait_ge(fin, b * 3 + 1)
                    nc.vector.tensor_tensor(yn[:], yn[:], g["bias_b"]["ln2b"][:], ALU.add).then_inc(fin, 1)
                if n == 2:
                    v.wait_ge(fin, b * 3 + 2)
                    nc.vector.tensor_tensor(dyn(res, b), dyn(res, b), yn[:], ALU.add).then_inc(fin, 1)

            def one_pass(it):
                first = isinstance(it, int) and it == 0
                for k in range(PER):
                    if k % THIRD == 0:
                        v.load(regs, blk_item[0:1, bass.ds(it * PER + k, THIRD)])
                        blk = [v.snap(r, min_val=0, max_val=NBLK - 1) for r in regs]
                    select(it, k)
                    if not (first and k < LAG):
                        add(it * PER + k - LAG, (k - LAG) % PSLOT, blk[k % THIRD])
                    if k in (0, 1, 2) and not first:
                        finish(it - 1, k)
                    if k == 4:
                        sources(it, 2)
                    if k == 7:
                        queries(it)
                    if k in (11, 12, 13):
                        attention(it, k - 11)
                    if k in (14, 15):
                        norm1(it, k - 14)
                    if k == 16:
                        sources(it + 1, 0)
                    if k in (17, 18, 19):
                        norm1(it, 2 * (k - 17) + 2)
                        norm1(it, 2 * (k - 17) + 3)
                    if k == 27:
                        sources(it + 1, 1)
                    if k in (28, 29):
                        norm2(it, k - 28)
                    if k in (30, 31, 32):
                        norm2(it, 2 * (k - 30) + 2)
                        norm2(it, 2 * (k - 30) + 3)

            sources(0, 0)
            sources(0, 1)
            one_pass(0)
            with v.Fori(1, NBLK) as it:
                one_pass(it)
            v.load(regs[0:LAG], blk_item[0:1, NITEM:NITEM + LAG])
            for q in range(LAG):
                j = NITEM - LAG + q
                add(j, (PER - LAG + q) % PSLOT, v.snap(regs[q], min_val=0, max_val=NBLK - 1))
            for n in range(3):
                finish(NBLK - 1, n)


def route(nc, sb, ps, sem, g):
    (acc, res, rstd, nmr, dinv, ident, gate_sb, gateb_b, slots, dma_empty, dma_out, out) = (g[k] for k in (
        "acc", "res", "rstd", "nmr", "dinv", "ident", "gate_sb", "gateb_b", "slots", "dma_empty", "dma_out", "out"))
    GR = 7
    NG = NBLK // GR
    assert NG * GR == NBLK
    with ExitStack() as st:
        stt = sb("stt", [P, GR, 6], st=st)
        mvg = sb("mvg", [P, GR, 2], st=st)
        sdg = sb("sdg", [P, GR], st=st)
        tmp = sb("tmp_r", [P, GR], st=st)
        xr = sb("xr", [P, GR, C], st=st)
        xrT = sb("xrT", [P, GR, CH, P], st=st)
        triu = sb("triu", [P, P], st=st)
        ones = sb("ones", [P, P], st=st)
        e8 = sb("e8", [P, EXP], st=st)
        base = sb("base", [P, EXP], st=st)
        node_i = sb("node_i", [P, NBLK], I32, st)
        node_f = sb("node_f", [P, NBLK], st=st)
        B8 = [P, NBLK, EXP]
        lg, ex, oh, cand = sb("lg", B8, st=st), sb("ex", B8, st=st), sb("oh", B8, st=st), sb("cand", B8, st=st)
        sa, sc = sb("sa", B8, st=st), sb("sc", B8, st=st)
        tot = sb("tot", B8, st=st)
        m1 = sb("m1", [P, NBLK], st=st)
        prob = sb("prob", [P, NBLK], st=st)
        rowno = sb("rowno", [P, NBLK], st=st)
        kept = sb("kept", [P, NBLK], st=st)
        dest = sb("dest", [P, NBLK], I32, st)
        p_t = [ps(f"r_t{i}", [P, 4, P], st) for i in range(2)]
        p_l = ps("r_l", [P, 512], st)
        p_in = ps("r_in", [P, 512], st)
        p_to = ps("r_to", [P, 512], st)
        const3, s1, s2, s3, s4, g5, std, xr_ok, tr_ok, xT_ok, l_ps, dv, e_ok, e_act, oh_ok, cum, dest_ok, x2_ok, sent = (
            sem("r_" + n, st) for n in ("const3", "s1", "s2", "s3", "s4", "g5", "std", "xr", "tr", "xT", "lps",
                                        "dv", "e", "eact", "oh", "cum", "dest", "x2", "sent"))
        block = st.enter_context(nc.Block())

        def row(tile, b):
            return tile[:, bass.ds(b, 1), 0:C].rearrange("p a c -> p (a c)")

        @block.gpsimd
        def _(pool):
            nc.gpsimd.memset(ones[:], 1.0).then_inc(const3, 1)
            nc.gpsimd.memset(triu[:], 1.0).then_inc(const3, 1)
            nc.gpsimd.iota(e8[:], [[1, EXP]], 0, 0, allow_small_or_imprecise_dtypes=True).then_inc(const3, 1)
            nc.gpsimd.iota(base[:], [[CAP, EXP]], -1, 0, allow_small_or_imprecise_dtypes=True).then_inc(const3, 1)
            nc.gpsimd.iota(node_i[:], [[P, NBLK]], 0, 1).then_inc(const3, 1)
            nc.gpsimd.iota(node_f[:], [[P, NBLK]], 0, 1, allow_small_or_imprecise_dtypes=True).then_inc(const3, 1)
            pool.wait_ge(const3, 6)
            nc.gpsimd.affine_select(triu[:], triu[:], [[1, P]], ALU.is_ge, 0.0, 0, -1).then_inc(const3, 1)
            pool.wait_ge(dma_empty, 32)
            pool.wait_ge(dest_ok, 1)
            for b in range(NBLK):
                nc.gpsimd.indirect_dma_start(slots, bass.IndirectOffsetOnAxis(dest[:, b:b + 1], 0), acc[:, b, :],
                                             None, bounds_check=SLOTS - 1, oob_is_err=False).then_inc(sent, 16)
            pool.wait_ge(sent, 16 * NBLK)

        @block.sync
        def _(sp):
            sp.wait_ge(x2_ok, 1)
            sp.dma_start(out.rearrange("(b p) c -> p b c", p=P), acc[:, :, 0:C]).then_inc(dma_out, 16)
            sp.wait_ge(dma_out, 16)

        @block.vector
        def _(v):
            V = nc.vector

            def group(gi):
                for u in range(GR):
                    b = gi * GR + u
                    V.scalar_tensor_tensor(row(acc, b), row(acc, b), dinv[:, bass.ds(b, 1)], g["bias_b"]["gb"][:],
                                           ALU.mult, ALU.add).then_inc(s1, 1)
                for u in range(GR):
                    b = gi * GR + u
                    v.wait_ge(s1, b + 1)
                    V.scalar_tensor_tensor(row(acc, b), row(acc, b), 0.0, row(res, b), ALU.max, ALU.add
                                           ).then_inc(s2, 1)
                for u in range(GR):
                    b = gi * GR + u
                    wait_apart(v, s2, b + 1, const3, 7)
                    V.bn_stats(stt[:, u, :], row(acc, b)).then_inc(s3, 1)
                for u in range(GR):
                    b = gi * GR + u
                    wait_apart(v, s3, b + 1, const3, 7)
                    V.bn_aggr(mvg[:, u, :], stt[:, u, :]).then_inc(s4, 1)
                gs = slice(0, GR)
                r = rstd[:, bass.ds(gi * GR, GR)]
                nm = nmr[:, bass.ds(gi * GR, GR)]
                v.wait_ge(std, gi + 1)

                def step(n, ins):
                    ins.then_inc(g5, 1)
                    v.wait_ge(g5, gi * 6 + n)

                step(1, V.reciprocal(r, sdg[:]))
                step(2, V.scalar_tensor_tensor(tmp[:], mvg[:, :, 1], EPS, r, ALU.add, ALU.mult))
                step(3, V.tensor_tensor(tmp[:], tmp[:], r, ALU.mult))
                step(4, V.tensor_scalar(tmp[:], tmp[:], -0.5, 1.5, ALU.mult, ALU.add))
                step(5, V.tensor_tensor(r, r, tmp[:], ALU.mult))
                step(6, V.scalar_tensor_tensor(nm, mvg[:, :, 0], -1.0, r, ALU.mult, ALU.mult))

            v.wait_ge(const3, 7)
            group(0)
            with v.Fori(1, NG) as gi:
                group(gi)
            V.memset(m1[:], 0.0).then_inc(x2_ok, 1)

            n = [0]

            def link(ins):
                n[0] += 1
                ins.then_inc(dv, 1)
                v.wait_ge(dv, n[0])

            def over_e(a):
                return a[:].rearrange("p (b e) -> p b e", e=1).broadcast_to(B8)

            def over_b(a):
                return a[:].rearrange("p (b e) -> p b e", b=1).broadcast_to(B8)

            v.wait_ge(x2_ok, 1)
            v.wait_ge(l_ps, NBLK)
            link(V.tensor_tensor(lg[:], p_l[:, 0:NBLK * EXP].rearrange("p (b e) -> p b e", e=EXP),
                                 over_b(gateb_b), ALU.add))
            link(V.tensor_reduce(m1[:], lg[:], AX.X, ALU.max))
            V.tensor_tensor(ex[:], lg[:], over_e(m1), ALU.subtract).then_inc(e_ok, 1)
            link(V.tensor_tensor(cand[:], lg[:], over_e(m1), ALU.is_equal))
            link(V.tensor_scalar(cand[:], cand[:], -float(EXP), None, ALU.mult))
            link(V.tensor_tensor(cand[:], cand[:], over_b(e8), ALU.add))
            link(V.tensor_reduce(m1[:], cand[:], AX.X, ALU.min))
            V.tensor_tensor(oh[:], cand[:], over_e(m1), ALU.is_equal).then_inc(oh_ok, 1)
            v.wait_ge(oh_ok, 1)
            v.wait_ge(e_act, 1)
            link(V.tensor_reduce(prob[:], ex[:], AX.X, ALU.add))
            link(V.reciprocal(prob[:], prob[:]))
            v.wait_ge(cum, 2)
            link(V.tensor_copy(tot[:], p_to[:, 0:NBLK * EXP].rearrange("p (b e) -> p b e", e=EXP)))
            cur, nxt = tot, sa
            sh = 1
            while sh < NBLK:
                link(V.tensor_tensor(nxt[:, sh:, :], cur[:, sh:, :], cur[:, 0:NBLK - sh, :], ALU.add))
                link(V.tensor_copy(nxt[:, 0:sh, :], cur[:, 0:sh, :]))
                cur, nxt = nxt, (sc if nxt is sa else sa)
                sh *= 2
            link(V.tensor_tensor(nxt[:], cur[:], tot[:], ALU.subtract))
            link(V.tensor_tensor(nxt[:], nxt[:], p_in[:, 0:NBLK * EXP].rearrange("p (b e) -> p b e", e=EXP),
                                 ALU.add))
            link(V.tensor_tensor(cur[:], nxt[:], oh[:], ALU.mult))
            link(V.tensor_reduce(m1[:], cur[:], AX.X, ALU.add))
            link(V.tensor_tensor(nxt[:], nxt[:], over_b(base), ALU.add))
            link(V.tensor_tensor(nxt[:], nxt[:], oh[:], ALU.mult))
            link(V.tensor_reduce(rowno[:], nxt[:], AX.X, ALU.add))
            link(V.tensor_scalar(kept[:], node_f[:], float(N), None, ALU.is_lt))
            link(V.scalar_tensor_tensor(kept[:], m1[:], float(CAP), kept[:], ALU.is_le, ALU.mult))
            link(V.scalar_tensor_tensor(rowno[:], rowno[:], -float(NOWHERE), kept[:], ALU.add, ALU.mult))
            link(V.tensor_scalar(dest[:], rowno[:], float(NOWHERE), None, ALU.add))
            link(V.tensor_copy(acc[:, :, C], nmr[:]))
            link(V.tensor_copy(acc[:, :, C + 1], rstd[:]))
            link(V.tensor_copy(acc[:, :, C + 2], prob[:]))
            V.tensor_copy(acc[:, :, C + 3:C + 4].bitcast(I32).rearrange("p b a -> p (b a)"), node_i[:]
                          ).then_inc(dest_ok, 1)

        @block.scalar
        def _(s):
            def group(gi):
                s.wait_ge(s4, gi * GR + GR)
                wait(s, g5, gi * 6)
                nc.scalar.activation(sdg[:], mvg[:, :, 1], ACT.Sqrt, bias=g["eps_ln"][:]).then_inc(std, 1)
                s.wait_ge(g5, gi * 6 + 6)
                for u in range(GR):
                    b = gi * GR + u
                    wait(s, tr_ok, b - GR + 1)
                    nc.scalar.activation(xr[:, u, :], row(acc, b), ACT.Identity, scale=rstd[:, bass.ds(b, 1)],
                                         bias=nmr[:, bass.ds(b, 1)]).then_inc(xr_ok, 1)
                    if u > 0:
                        copy(b - 1, u - 1)
                copy(gi * GR + GR - 1, GR - 1)

            def copy(b, u):
                s.wait_ge(tr_ok, b + 1)
                wait(s, l_ps, b - GR + 1)
                nc.scalar.copy(xrT[:, u], p_t[u % 2][:, 0:CH, :]).then_inc(xT_ok, 1)

            group(0)
            with s.Fori(1, NG) as gi:
                group(gi)
            s.wait_ge(e_ok, 1)
            nc.scalar.activation(ex[:], ex[:], ACT.Exp).then_inc(e_act, 1)

        @block.tensor
        def _(t_):
            pe = nc.tensor
            t_.wait_ge(const3, 7)

            def group(gi):
                for u in range(GR):
                    b = gi * GR + u
                    t_.wait_ge(xr_ok, b + 1)
                    wait(t_, xT_ok, b if u == 0 else b - 1)
                    for a in range(CH):
                        mm = pe.transpose(p_t[u % 2][:, a, :], xr[:, u, a * P:(a + 1) * P], ident[:])
                    mm.then_inc(tr_ok, 1)
                    if u > 0:
                        logits(b - 1, u - 1)
                logits(gi * GR + GR - 1, GR - 1)

            def logits(b, u):
                t_.wait_ge(xT_ok, b + 1)
                o = p_l[:, bass.ds(b * EXP, EXP)]
                for a in range(CH):
                    mm = pe.matmul(o, xrT[:, u, a, :], gate_sb[:, a, :], start=(a == 0), stop=(a == CH - 1))
                mm.then_inc(l_ps, 1)

            group(0)
            with t_.Fori(1, NG) as gi:
                group(gi)
            t_.wait_ge(oh_ok, 1)
            ohf = oh[:].rearrange("p b e -> p (b e)")
            pe.matmul(p_in[:, 0:NBLK * EXP], triu[:], ohf, start=True, stop=True).then_inc(cum, 1)
            pe.matmul(p_to[:, 0:NBLK * EXP], ones[:], ohf, start=True, stop=True).then_inc(cum, 1)


def experts(nc, sb, ps, sem, g):
    slots, ident, out, fb1_sb = g["slots"], g["ident"], g["out"], g["fb1_sb"]
    w1, w2, fb2, dma_fb, dma_out = g["w1"], g["w2"], g["fb2"], g["dma_fb"], g["dma_out"]
    LASTR = CAP - (RT - 1) * P
    NH = (-(-CAP // 2), CAP // 2)
    with ExitStack() as st:
        w1s = sb("w1s", [P, 2, CH, F], st=st)
        w2s = sb("w2s", [P, 2, FT, C], st=st)
        rows = sb("rows", [P, 2, RT, ROW], st=st)
        fb2_b = sb("fb2_b", [P, EXP, C], st=st)
        xe = sb("xe", [P, 2, C], st=st)
        bT = sb("bT", [P, 2, CH, CAP], st=st)
        hT = sb("hT", [P, FT, CAP], st=st)
        yv = sb("yv", [P, 2, C], st=st)
        fin_m = sb("fin_m", [P, C], I32, st)
        big, low = sb("big", [P, C], st=st), sb("low", [P, C], st=st)
        oo = sb("oo", [P, 2, C], st=st)
        p_f = [ps(f"e_f{i}", [P, 512], st) for i in range(4)]
        p_y = [ps(f"e_y{i}", [P, 512], st) for i in range(2)]
        p_t = [ps(f"e_t{i}", [P, 4, P], st) for i in range(2)]
        d_w = [sem(f"d_w{i}", st) for i in range(2)]
        d_r = [sem(f"d_r{i}", st) for i in range(2)]
        d_b, sent = sem("d_b", st), [sem(f"e_sent{i}", st) for i in range(2)]
        xe_ok, tr_ok, bT_ok, f1_ps, h0_ok, h1_ok, f2_ps, y_dv, o_ok = (
            sem("e_" + n, st) for n in ("xe", "tr", "bT", "f1", "h0", "h1", "f2", "ydv", "o"))
        block = st.enter_context(nc.Block())
        NY = 8

        def nrows(t):
            return P if t < RT - 1 else LASTR

        def wait_rows(eng, e, u):
            if isinstance(e, int):
                eng.wait_ge(d_r[u], (e // 2 + 1) * 32)
            else:
                eng.wait_ge(d_r[u], (e - u) * 16 + 32)

        def load_rows(sp, e, u):
            sp.dma_start(rows[:, u, 0:RT - 1, :],
                         slots[bass.ds(e * CAP, (RT - 1) * P), :].rearrange("(t p) c -> p t c", p=P)
                         ).then_inc(d_r[u], 16)
            sp.dma_start(rows[0:LASTR, u, RT - 1, :], slots[bass.ds(e * CAP + (RT - 1) * P, LASTR), :]
                         ).then_inc(d_r[u], 16)

        def load_weights(sp, e, u):
            sp.dma_start(w1s[:, u], w1[bass.ds(e, 1)].rearrange("e (k p) f -> p (e k) f", p=P)).then_inc(d_w[u], 16)
            sp.dma_start(w2s[:, u], w2[bass.ds(e, 1)].rearrange("e (j p) c -> p (e j) c", p=P)).then_inc(d_w[u], 16)

        @block.sync
        def _(sp):
            load_rows(sp, 0, 0)
            load_weights(sp, 0, 0)
            load_rows(sp, 1, 1)
            load_weights(sp, 1, 1)
            sp.dma_start(fb2_b[:].rearrange("p e c -> p (e c)"),
                         fb2.rearrange("(a e) c -> a (e c)", a=1).broadcast_to([P, EXP * C])).then_inc(d_b, 16)

            def expert(e, u):
                sp.wait_ge(f2_ps, e * RT + RT)
                sp.wait_ge(o_ok, e * RT + RT)
                for q in range(2):
                    sp.wait_ge(sent[q], (e * (RT // 2) + RT // 2) * 16)
                load_rows(sp, e + 2, u)
                load_weights(sp, e + 2, u)

            for e in range(2):
                expert(e, e)
            with sp.Fori(1, EXP // 2 - 1) as it:
                for u in range(2):
                    expert(it * 2 + u, u)
            sp.wait_ge(f2_ps, (EXP - 2) * RT + RT)
            sp.wait_ge(o_ok, (EXP - 2) * RT + RT)
            for q in range(2):
                sp.wait_ge(sent[q], ((EXP - 2) * (RT // 2) + RT // 2) * 16)
            load_rows(sp, EXP, 0)
            sp.wait_ge(d_r[0], 32 * (EXP // 2 + 1))

        @block.gpsimd
        def _(pool):
            pool.wait_ge(dma_out, 16)

            def expert(e, u):
                for t in range(RT):
                    r = nrows(t)
                    wait_apart(pool, o_ok, e * RT + t + 1, dma_out, 16)
                    nc.gpsimd.indirect_dma_start(
                        out, bass.IndirectOffsetOnAxis(rows[0:r, u, t, C + 3:C + 4].bitcast(I32), 0),
                        oo[0:r, t % 2, :], None, bounds_check=N - 1, oob_is_err=False).then_inc(sent[t % 2], 16)

            for e in range(2):
                expert(e, e)
            with pool.Fori(1, EXP // 2) as it:
                for u in range(2):
                    expert(it * 2 + u, u)
            for q in range(2):
                pool.wait_ge(sent[q], 16 * EXP * RT // 2)

        @block.scalar
        def _(s):
            s.wait_ge(dma_fb, 16)

            def normalise(e, u):
                wait_rows(s, e, u)
                for t in range(RT):
                    r = nrows(t)
                    wait(s, tr_ok, e * RT + t - 1)
                    nc.scalar.activation(xe[0:r, t % 2, :], rows[0:r, u, t, 0:C], ACT.Identity,
                                         scale=rows[0:r, u, t, C + 1:C + 2], bias=rows[0:r, u, t, C:C + 1]
                                         ).then_inc(xe_ok, 1)
                    s.wait_ge(tr_ok, e * RT + t + 1)
                    nc.scalar.copy(bT[:, u, :, t * P:t * P + r], p_t[t % 2][:, 0:CH, 0:r]).then_inc(bT_ok, 1)

            def expert(e, u):
                for j in range(FT):
                    s.wait_ge(f1_ps, e * 2 * FT + 2 * j + 1)
                    wait(s, f2_ps, e * RT)
                    nc.scalar.activation(hT[:, j, 0:NH[0]], p_f[(2 * j) % 4][:, 0:NH[0]], ACT.Relu,
                                         bias=fb1_sb[:, bass.ds(e, 1), j]).then_inc(h0_ok, 1)
                normalise(e + 1, 1 - u)

            normalise(0, 0)
            for e in range(2):
                expert(e, e)
            with s.Fori(1, EXP // 2) as it:
                for u in range(2):
                    expert(it * 2 + u, u)

        @block.tensor
        def _(t_):
            pe = nc.tensor

            def transposes(e, u):
                for t in range(RT):
                    r = nrows(t)
                    t_.wait_ge(xe_ok, e * RT + t + 1)
                    wait(t_, bT_ok, e * RT + t - 1)
                    for a in range(CH):
                        mm = pe.transpose(p_t[t % 2][:, a, 0:r], xe[0:r, t % 2, a * P:(a + 1) * P],
                                          ident[0:r, 0:r])
                    mm.then_inc(tr_ok, 1)

            def expert(e, u):
                if isinstance(e, int):
                    t_.wait_ge(d_w[u], (e // 2 + 1) * 32)
                else:
                    t_.wait_ge(d_w[u], (e - u) * 16 + 32)
                t_.wait_ge(bT_ok, e * RT + RT)
                for j in range(FT):
                    for h in range(2):
                        c = 2 * j + h
                        wait(t_, (h0_ok, h1_ok)[h], e * FT + j - 1)
                        for a in range(CH):
                            mm = pe.matmul(p_f[c % 4][:, 0:NH[h]], w1s[:, u, a, j * P:(j + 1) * P],
                                           bT[:, u, a, h * NH[0]:h * NH[0] + NH[h]], start=(a == 0),
                                           stop=(a == CH - 1))
                        mm.then_inc(f1_ps, 1)
                transposes(e + 1, 1 - u)
                t_.wait_ge(h0_ok, e * FT + FT)
                t_.wait_ge(h1_ok, e * FT + FT)
                for t in range(RT):
                    r = nrows(t)
                    wait(t_, y_dv, (e * RT + t - 2) * NY + 1)
                    for j in range(FT):
                        mm = pe.matmul(p_y[t % 2][0:r, 0:C], hT[:, j, t * P:t * P + r], w2s[:, u, j, :],
                                       start=(j == 0), stop=(j == FT - 1))
                    mm.then_inc(f2_ps, 1)

            transposes(0, 0)
            for e in range(2):
                expert(e, e)
            with t_.Fori(1, EXP // 2) as it:
                for u in range(2):
                    expert(it * 2 + u, u)

        @block.vector
        def _(v):
            V = nc.vector
            v.wait_ge(dma_fb, 16)
            v.wait_ge(d_b, 16)

            def expert(e, u):
                for j in range(FT):
                    v.wait_ge(f1_ps, e * 2 * FT + 2 * j + 2)
                    wait(v, f2_ps, e * RT)
                    V.tensor_scalar(hT[:, j, NH[0]:CAP], p_f[(2 * j + 1) % 4][:, 0:NH[1]],
                                    fb1_sb[:, bass.ds(e, 1), j], 0.0, ALU.add, ALU.max).then_inc(h1_ok, 1)
                for t in range(RT):
                    r = nrows(t)
                    k = [0]

                    def link(ins):
                        k[0] += 1
                        ins.then_inc(y_dv, 1)
                        wait_apart(v, y_dv, (e * RT + t) * NY + k[0], dma_fb, 16)

                    v.wait_ge(f2_ps, e * RT + t + 1)
                    y = yv[0:r, 0, :]
                    link(V.tensor_tensor(y, p_y[t % 2][0:r, 0:C],
                                         fb2_b[0:r, bass.ds(e, 1), :].rearrange("p a c -> p (a c)"), ALU.add))
                    link(V.tensor_scalar(y, y, rows[0:r, u, t, C + 2:C + 3], None, ALU.mult))
                    link(V.tensor_scalar(low[0:r, :], y, -FLT_MAX, None, ALU.is_ge))
                    link(V.scalar_tensor_tensor(fin_m[0:r, :], y, FLT_MAX, low[0:r, :], ALU.is_le, ALU.mult))
                    link(V.tensor_scalar(big[0:r, :], y, FLT_MAX, 1e4, ALU.is_gt, ALU.mult))
                    link(V.tensor_scalar(low[0:r, :], y, -FLT_MAX, -1e4, ALU.is_lt, ALU.mult))
                    link(V.tensor_tensor(big[0:r, :], big[0:r, :], low[0:r, :], ALU.add))
                    link(V.copy_predicated(big[0:r, :], fin_m[0:r, :], y))
                    if isinstance(e, int):
                        wait(v, sent[t % 2], (e * (RT // 2) + t // 2) * 16)
                    else:
                        v.wait_ge(sent[t % 2], (e * (RT // 2) + t // 2) * 16)
                    V.tensor_tensor(oo[0:r, t % 2, :], big[0:r, :], rows[0:r, u, t, 0:C], ALU.add).then_inc(o_ok, 1)

            for e in range(2):
                expert(e, e)
            with v.Fori(1, EXP // 2) as it:
                for u in range(2):
                    expert(it * 2 + u, u)


_OUT = "out_dram"


def kernel(**inputs):
    import concourse.bacc as bacc
    from concourse.bass_utils import run_bass_kernel_spmd as run

    nc = bacc.Bacc("TRN2", target_bir_lowering=False, num_devices=1)
    a = {k: np.asarray(v) for k, v in inputs.items()}

    def padded(v, n, fill):
        w = np.full((n,) + v.shape[1:], fill, v.dtype)
        w[:v.shape[0]] = v
        return w

    given = {
        "x": padded(a["x"], NPAD, 0),
        "srcR": padded(a["src"], EPAD + P, 0).reshape(-1, P),
        "dstR": padded(a["dst"], EPAD + P, PAD_DST).reshape(-1, P),
        "gW": a["L0_gnn_W"], "gb": a["L0_gnn_b"],
        "WqkvT": a["L0_mix_Wqkv"].T, "ln1g": a["L0_mix_ln1_g"], "ln1b": a["L0_mix_ln1_b"],
        "W1T": a["L0_mix_W1"].T, "b1": a["L0_mix_b1"], "W2T": a["L0_mix_W2"].T, "b2": a["L0_mix_b2"],
        "ln2g": a["L0_mix_ln2_g"], "ln2b": a["L0_mix_ln2_b"],
        "gateW": a["L0_ffn_gate_w"], "gateb": a["L0_ffn_gate_b"],
        "w1": a["L0_ffn_w1"], "fb1": a["L0_ffn_b1"].reshape(EXP, FT, P).transpose(2, 0, 1), "w2": a["L0_ffn_w2"], "fb2": a["L0_ffn_b2"],
    }
    arrays, args = {}, []
    for k, v in given.items():
        arrays["in_" + k] = np.ascontiguousarray(v)
        args.append(nc.dram_tensor("in_" + k, v.shape, mybir.dt.from_np(v.dtype), kind="ExternalInput").ap())
    out = nc.dram_tensor(_OUT, (NPAD, C), F32, kind="ExternalOutput").ap()
    build(nc, *args, out)
    r = run(nc, [arrays], core_ids=[0])
    return r.results[0][_OUT][:N]
```

```python
from contextlib import ExitStack

import numpy as np

import concourse.bass as bass
from concourse import mybir

ALU = mybir.AluOpType
ACT = mybir.ActivationFunctionType
F32 = mybir.dt.float32
F32R = mybir.dt.float32r
BF16 = mybir.dt.bfloat16
I32 = mybir.dt.int32
I16 = mybir.dt.int16
AX = mybir.AxisListType

P = 128
N = 6250
C = 256
CH = C // P
E = 200000
NBLK = -(-N // P)
NPAD = NBLK * P
NCHUNK = -(-E // P)
NT = -(-NCHUNK // P)
EPAD = NT * P * P
PAD_DST = 1 << 20
PER = 21
NPASS = -(-(NCHUNK + NBLK - 1) // PER)
NITEM = NPASS * PER
KVB = 4
NKV = -(-NBLK // KVB)
assert NKV + NBLK < NPASS
assert NITEM >= NCHUNK + NBLK - 1 and NITEM <= NT * P
RING = PER
GRP = 7
TRI = 3
LAG = 4
PSLOT = 3
H, DH = 8, C // 8
EXP = 8
F = 1024
CAP = -(-5 * N // (4 * EXP))
SLOTS = EXP * CAP
ROW = C + 4
NOWHERE = 1 << 17
EPS = 1e-5
EPS_ATTN = 1e-6
FT = F // P
RT = -(-CAP // P)
FLT_MAX = 3.4028234e38
LAST = N - (NBLK - 1) * P


def wait(eng, sem, value):
    if isinstance(value, int) and value <= 0:
        return
    eng.wait_ge(sem, value)


def wait_apart(eng, sem, value, long_sem, long_value):
    if isinstance(value, int):
        if value > 0:
            eng.wait_ge(sem, value)
        return
    value = eng.to_reg(value)
    eng.wait_ge(long_sem, long_value)
    eng.wait_ge(sem, value)


def build(nc, x, srcR, dstR, dstF, gW, gb, WqkvT, ln1g, ln1b, W1T, b1, W2T, b2, ln2g, ln2b, gateW, gateb,
          w1, fb1, w2, fb2, out):
    table = nc.dram_tensor("node_rows", (NPAD, C), F32, kind="Internal").ap()
    slots = nc.dram_tensor("expert_rows", (SLOTS, ROW), F32, kind="Internal").ap()

    with ExitStack() as top:
        names = {}

        def sb(name, shape, dt=F32, st=top):
            return st.enter_context(nc.sbuf_tensor(name, shape, dt))

        def ps(name, shape, st):
            return st.enter_context(nc.psum_tensor(name, shape, F32))

        def sem(name, st=top):
            return st.enter_context(nc.semaphore(name))

        ident = sb("ident", [P, P])
        col = sb("col", [P, P])
        eps_ln = sb("eps_ln", [P, 1])
        fb1_sb = sb("fb1_sb", [P, EXP, FT])
        dma_fb = sem("dma_fb")
        dma_empty = sem("dma_empty")
        dma_out = sem("dma_out")
        pads = sem("pads")
        consts = sem("consts")

        with ExitStack() as mid:
            acc = sb("acc", [P, NBLK, ROW], st=mid)
            res = sb("res", [P, NBLK, C], st=mid)
            src_item = sb("src_item", [P, NT * P], I32, st=mid)
            dst_item = sb("dst_item", [P, NT * P], st=mid)
            blk_item = sb("blk_item", [1, LAG + NT * P], I16, st=mid)
            rstd = sb("rstd", [P, NBLK], st=mid)
            nmr = sb("nmr", [P, NBLK], st=mid)
            dinv = sb("dinv", [P, NBLK], st=mid)
            kvz = sb("kvz", [P, CH, P + P // DH], st=mid)
            headmask = sb("headmask", [P, P], st=mid)
            w1t_sb = sb("w1t_sb", [P, CH, C], st=mid)
            w2t_sb = sb("w2t_sb", [P, CH, C], st=mid)
            wq_sb = sb("wq_sb", [P, CH, 3 * C], st=mid)
            bias_b = {k: sb("bc_" + k, [P, C], st=mid) for k in ("gb", "ln2g", "ln2b")}
            b2row = sb("b2row", [1, C], st=mid)
            ones_row = sb("ones_row", [1, P], st=mid)
            cols = {k: sb("col_" + k, [P, CH], st=mid) for k in ("b1", "ln1g", "ln1b")}
            gate_sb = sb("gate_sb", [P, CH, EXP], st=mid)
            gateb_b = sb("gateb_b", [P, EXP], st=mid)
            v1 = sb("v1", [P, 2, CH, P + 2], st=mid)
            dma_w = sem("dma_w", mid)

            prepare(nc, mid, sb, ps, sem, locals())
            aggregate_and_mix(nc, sb, ps, sem, locals())
            route(nc, sb, ps, sem, locals())
        experts(nc, sb, ps, sem, locals())


def rsqrt_steps(nc, link, out, var, tmp, eps):
    link(nc.vector.scalar_tensor_tensor(tmp, var, eps, out, ALU.add, ALU.mult))
    link(nc.vector.tensor_tensor(tmp, tmp, out, ALU.mult))
    link(nc.vector.tensor_scalar(tmp, tmp, -0.5, 1.5, ALU.mult, ALU.add))
    link(nc.vector.tensor_tensor(out, out, tmp, ALU.mult))


def prepare(nc, mid, sb, ps, sem, g):
    (x, srcR, dstR, dstF, table, acc, res, src_item, dst_item, blk_item, rstd, nmr, dinv, headmask, ident,
     col, eps_ln, wq_sb, w1t_sb, w2t_sb, dma_w, consts, v1) = (g[k] for k in (
        "x", "srcR", "dstR", "dstF", "table", "acc", "res", "src_item", "dst_item", "blk_item", "rstd", "nmr",
        "dinv", "headmask", "ident", "col", "eps_ln", "wq_sb", "w1t_sb", "w2t_sb", "dma_w", "consts", "v1"))
    GR = 7
    NG = NBLK // GR
    SG = 6
    NRAW = SG * GR - 2
    CG = 4
    assert NG * GR == NBLK
    with ExitStack() as st:
        src_rows = sb("src_rows", [P, NT, P], I32, st)
        dst_rows = sb("dst_rows", [P, NT, P], I32, st)
        first = sb("first", [P, NT], I32, st)
        next_first = sb("next_first", [P, NT], I32, st)
        gw_sb = sb("gw_sb", [P, CH, C], st=st)
        blk_i = sb("blk_i", [P, 3, NT], I32, st)
        code_f = sb("code_f", [P, 2, NT], st=st)
        key = sb("key", [P, 2, NT], st=st)
        col256 = sb("col256", [P, 2 * P], st=st)
        col128x = sb("col128x", [P, P], st=st)
        part = sb("part", [P, 1], st=st)
        chunk0 = sb("chunk0", [P, NT], st=st)
        chunkn = sb("chunkn", [P, NT], st=st)
        node_n = sb("node_n", [P, NBLK], st=st)
        band_m = sb("band_m", [P, 2, 2 * P], BF16, st)
        bandf = sb("bandf", [P, 3, 2 * P], st=st)
        rowf = sb("rowf", [P, 3, 2, P], st=st)
        brow = sb("brow", [1, 2, P], st=st)
        one_lo = sb("one_lo", [P, NT, P], BF16, st)
        one_hi = sb("one_hi", [P, NT, NBLK], BF16, st)
        below = sb("below", [P, P], st=st)
        ones = sb("ones_p", [P, P], st=st)
        next_p = sb("next_p", [P, P], st=st)
        wrap_p = sb("wrap_p", [P, P], st=st)
        firsts = sb("firsts", [P, NBLK], st=st)
        block_n = sb("block_n", [NBLK, P], st=st)
        chunk_f = sb("chunk_f", [P, NBLK], st=st)
        chunk_i = sb("chunk_i", [P, NBLK], I32, st)
        crow = sb("crow", [P, CG * GR, P], I32, st)
        less = sb("less", [P, GR, P], BF16, st)
        place = sb("place", [P, NBLK + 1], st=st)
        stats = sb("stats", [P, 2, 6], st=st)
        mv = sb("mv", [P, NBLK, 2], st=st)
        tmp = sb("tmp", [P, NBLK], st=st)
        deg = sb("deg", [P, NBLK], st=st)
        xn = sb("xn", [P, GR, C], st=st)
        xnT = sb("xnT", [P, GR, CH, P], st=st)

        p_it = ps("p_it", [P, 4, P], st)
        p_row = ps("p_row", [P, 512], st)
        p_deg = ps("p_deg", [P, 512], st)
        p_blk = ps("p_blk", [P, 512], st)
        p_tr = [ps(f"p_tr{i}", [P, 4, P], st) for i in range(2)]
        p_h = [ps(f"p_h{i}", [P, 512], st) for i in range(2)]

        dma_first, dma_rows, dma_gw = sem("dma_first", st), sem("dma_rows", st), sem("dma_gw", st)
        dma_x = [sem(f"dma_x{i}", st) for i in range(NG)]
        dma_crow = [sem(f"dma_crow{i}", st) for i in range(NG)]
        dma_tab = sem("dma_tab", st)
        onehots, hist, hist_sb, blk_ps, blk_sb, less_ps, chunk_ok, place_ok, shifted = (
            sem(n, st) for n in ("onehots", "hist", "hist_sb", "blk_ps", "blk_sb", "less_ps", "chunk_ok",
                                 "place_ok", "shifted"))
        bands, rows_ok = sem("bands", st), sem("rows_ok", st)
        item_ps = sem("item_ps", st)
        items = sem("items", st)
        stat = sem("stat", st)
        dve = sem("dve1", st)
        std_ok, rstd_ok = sem("std_ok", st), sem("rstd_ok", st)
        xn_ok, tr_ok, xnT_ok = sem("xn_ok", st), sem("tr_ok", st), sem("xnT_ok", st)
        h_ok, h_out = sem("h_ok", st), sem("h_out", st)
        deg_ok, deg_std, dinv_ok, scaled = (sem(n, st) for n in ("deg_ok", "deg_std", "dinv_ok", "scaled"))
        compared = sem("compared", st)
        block = st.enter_context(nc.Block())
        cuts = [0, 2 * GR, 4 * GR, NRAW]

        @block.sync
        def _(sp):
            with nc.allow_non_contiguous_dma("first destination of every chunk"):
                sp.dma_start(first[:], dstF[0:NT * P].rearrange("(t p) -> p t", p=P)).then_inc(dma_first, 16)
                sp.dma_start(next_first[:], dstF[1:NT * P + 1].rearrange("(t p) -> p t", p=P)
                             ).then_inc(dma_first, 16)
            for i in range(NG):
                sp.dma_start(res[:, i * GR:(i + 1) * GR, :],
                             x[i * GR * P:(i + 1) * GR * P, :].rearrange("(b p) c -> p b c", p=P)
                             ).then_inc(dma_x[i], 16)
                if i == 0:
                    sp.dma_start(gw_sb[:], g["gW"].rearrange("(k p) c -> p k c", p=P)).then_inc(dma_gw, 16)
            sp.dma_start(dst_rows[:], dstR[0:NT * P, :].rearrange("(t p) e -> p t e", p=P)).then_inc(dma_rows, 16)
            sp.dma_start(src_rows[:], srcR[0:NT * P, :].rearrange("(t p) e -> p t e", p=P)).then_inc(dma_rows, 16)
            sp.dma_start(wq_sb[:], g["WqkvT"].rearrange("(k p) c -> p k c", p=P)).then_inc(dma_w, 16)
            sp.dma_start(w1t_sb[:], g["W1T"].rearrange("(k p) c -> p k c", p=P)).then_inc(dma_w, 16)
            sp.dma_start(w2t_sb[:], g["W2T"].rearrange("(k p) c -> p k c", p=P)).then_inc(dma_w, 16)
            sp.dma_start(g["gate_sb"][:], g["gateW"].rearrange("(k p) c -> p k c", p=P)).then_inc(dma_w, 16)
            for k, v in (("gb", g["gb"]), ("ln2g", g["ln2g"]), ("ln2b", g["ln2b"])):
                sp.dma_start(g["bias_b"][k][:], v.rearrange("(a c) -> a c", a=1).broadcast_to([P, C])
                             ).then_inc(dma_w, 16)
            sp.dma_start(g["gateb_b"][:], g["gateb"].rearrange("(a c) -> a c", a=1).broadcast_to([P, EXP])
                         ).then_inc(dma_w, 16)
            sp.dma_start(g["b2row"][:], g["b2"].rearrange("(a c) -> a c", a=1)).then_inc(dma_w, 16)
            with nc.allow_non_contiguous_dma("small per-feature columns"):
                for k in ("b1", "ln1g", "ln1b"):
                    sp.dma_start(g["cols"][k][:], g[k].rearrange("(k p) -> p k", p=P)).then_inc(dma_w, 16)

            def to_table(lo, hi):
                sp.dma_start(table[lo * P:hi * P, :].rearrange("(b p) c -> p b c", p=P), acc[:, lo:hi, 0:C]
                             ).then_inc(dma_tab, 16)

            for lo, hi in zip(cuts, cuts[1:]):
                sp.wait_ge(scaled, hi)
                to_table(lo, hi)
            sp.wait_ge(h_out, NBLK)
            to_table(NRAW, NBLK)
            sp.wait_ge(dma_tab, 16 * len(cuts))

        @block.gpsimd
        def _(pool):
            nc.gpsimd.iota(col[:], [[1, P]], 0, 0, allow_small_or_imprecise_dtypes=True).then_inc(consts, 1)
            nc.gpsimd.memset(below[:], 1.0).then_inc(consts, 1)
            nc.gpsimd.memset(ones[:], 1.0).then_inc(consts, 1)
            nc.gpsimd.memset(eps_ln[:], EPS).then_inc(consts, 1)
            nc.gpsimd.memset(ident[:], 0.0).then_inc(consts, 1)
            pool.wait_ge(consts, 5)
            nc.gpsimd.affine_select(below[:], below[:], [[1, P]], ALU.is_gt, 0.0, 0, -1).then_inc(consts, 1)
            nc.gpsimd.affine_select(ident[:], ident[:], [[-1, P]], ALU.not_equal, 1.0, 0, 1).then_inc(consts, 1)
            nc.gpsimd.iota(node_n[:], [[P, NBLK]], 0, 1, allow_small_or_imprecise_dtypes=True).then_inc(consts, 1)
            nc.gpsimd.iota(col256[:], [[1, 2 * P]], 0, 0, allow_small_or_imprecise_dtypes=True).then_inc(consts, 1)
            nc.gpsimd.iota(col128x[:], [[P, P]], 0, 0, allow_small_or_imprecise_dtypes=True).then_inc(consts, 1)
            nc.gpsimd.iota(part[:], [[0, 1]], 0, 1, allow_small_or_imprecise_dtypes=True).then_inc(consts, 1)
            nc.gpsimd.iota(chunk0[:], [[P * P, NT]], 0, P, allow_small_or_imprecise_dtypes=True).then_inc(consts, 1)
            nc.gpsimd.iota(chunkn[:], [[P, NT]], 0, 1, allow_small_or_imprecise_dtypes=True).then_inc(consts, 1)
            nc.gpsimd.memset(next_p[:], 0.0).then_inc(consts, 1)
            nc.gpsimd.memset(wrap_p[:], 0.0).then_inc(consts, 1)
            nc.gpsimd.memset(place[:], float(E)).then_inc(consts, 1)
            pool.wait_ge(chunk_ok, 1)
            for b in range(NBLK):
                if b % GR == 0 and b >= CG * GR:
                    pool.wait_ge(compared, b // GR - CG + 1)
                nc.gpsimd.indirect_dma_start(crow[:, b % (CG * GR), :], None, dstR,
                                             bass.IndirectOffsetOnAxis(chunk_i[:, b:b + 1], 0)
                                             ).then_inc(dma_crow[b // GR], 16)
                if b == GR:
                    pool.wait_ge(consts, 16)
                    nc.gpsimd.affine_select(next_p[:], next_p[:], [[-1, P]], ALU.not_equal, 1.0, -1, 1
                                            ).then_inc(consts, 1)
                    nc.gpsimd.affine_select(wrap_p[:], wrap_p[:], [[1, P]], ALU.not_equal, 1.0, 1 - P, -1
                                            ).then_inc(consts, 1)
                    nc.gpsimd.memset(headmask[:], 1.0).then_inc(consts, 1)
                    nc.gpsimd.memset(v1[:], 1.0).then_inc(consts, 1)
                    nc.gpsimd.memset(g["ones_row"][:], 1.0).then_inc(consts, 1)
                    nc.gpsimd.memset(blk_item[:], 0).then_inc(consts, 1)
                    pool.wait_ge(consts, 22)
                    hm = headmask[:].rearrange("p (h d) -> p h d", d=DH)
                    nc.gpsimd.affine_select(hm, hm, [[-DH, P // DH], [0, DH]], ALU.is_ge, 0.0, 0, 1
                                            ).then_inc(consts, 1)
                    pool.wait_ge(consts, 23)
                    nc.gpsimd.affine_select(hm, hm, [[DH, P // DH], [0, DH]], ALU.is_ge, 0.0, DH - 1, -1
                                            ).then_inc(consts, 1)

        @block.vector
        def _(v):
            n = [0]
            V = nc.vector

            def link(ins):
                n[0] += 1
                ins.then_inc(dve, 1)
                v.wait_ge(dve, n[0])

            def over_p(a, k):
                return a.rearrange("p (t e) -> p t e", e=1).broadcast_to([P, NT, k])

            v.wait_ge(consts, 9)
            v.wait_ge(dma_first, 32)
            link(V.tensor_scalar(blk_i[:, 0, :], first[:], 7, None, ALU.arith_shift_right))
            link(V.tensor_scalar(blk_i[:, 2, :], first[:], P - 1, None, ALU.bitwise_and))
            link(V.tensor_copy(code_f[:, 0, :], blk_i[:, 0, :]))
            link(V.tensor_copy(code_f[:, 1, :], blk_i[:, 2, :]))
            colb = col[:].rearrange("p (t e) -> p t e", t=1)
            V.tensor_tensor(one_lo[:], colb.broadcast_to([P, NT, P]), over_p(code_f[:, 1, :], P), ALU.is_equal
                            ).then_inc(onehots, 1)
            V.tensor_tensor(one_hi[:], colb[:, :, 0:NBLK].broadcast_to([P, NT, NBLK]),
                            over_p(code_f[:, 0, :], NBLK), ALU.is_equal).then_inc(onehots, 1)
            v.wait_ge(hist, 1)
            V.tensor_copy(firsts[:], p_deg[:, 0:NBLK]).then_inc(hist_sb, 1)
            v.wait_ge(blk_ps, 1)
            V.tensor_copy(block_n[:], p_blk[0:NBLK, 0:P]).then_inc(blk_sb, 1)
            v.wait_ge(less_ps, 1)
            link(V.tensor_scalar(chunk_f[:], p_deg[:, 0:NBLK], -1.0, 0.0, ALU.add, ALU.max))
            V.tensor_copy(chunk_i[:], chunk_f[:]).then_inc(chunk_ok, 1)

            def means(gi):
                v.wait_ge(dma_x[gi], 16)
                for b in range(gi * GR, gi * GR + GR):
                    link(V.bn_stats(stats[:, b % 2, :], res[:, b, :]))
                    V.bn_aggr(mv[:, b, :], stats[:, b % 2, :]).then_inc(stat, 1)

            def inverse_std(gi):
                w = slice(gi * GR, gi * GR + GR)
                v.wait_ge(stat, gi * GR + GR)
                v.wait_ge(std_ok, gi + 1)
                link(V.reciprocal(rstd[:, w], rstd[:, w]))
                rsqrt_steps(nc, link, rstd[:, w], mv[:, w, 1], tmp[:, w], EPS)
                V.scalar_tensor_tensor(nmr[:, w], mv[:, w, 0], -1.0, rstd[:, w], ALU.mult, ALU.mult
                                       ).then_inc(rstd_ok, 1)

            for gi in range(NG + 1):
                if gi < NG:
                    means(gi)
                if gi > 0:
                    inverse_std(gi - 1)

            for gi in range(NG):
                w = slice(gi * GR, gi * GR + GR)
                v.wait_ge(dma_crow[gi], 16 * GR)
                c0 = gi % CG * GR
                link(V.tensor_tensor(less[:], crow[:, c0:c0 + GR, :],
                                     node_n[:, w].rearrange("p (b e) -> p b e", e=1).broadcast_to([P, GR, P]),
                                     ALU.is_lt))
                V.tensor_reduce(tmp[:, w], less[:], AX.X, ALU.add).then_inc(compared, 1)
                v.wait_ge(compared, gi + 1)
            v.wait_ge(consts, 24)
            V.scalar_tensor_tensor(place[:, 0:NBLK], chunk_f[:], float(P), tmp[:], ALU.mult, ALU.add
                                   ).then_inc(place_ok, 1)
            v.wait_ge(place_ok, 1)
            v.wait_ge(shifted, 1)
            V.scalar_tensor_tensor(deg[:], p_deg[:, 0:NBLK], 1.0, place[:, 0:NBLK], ALU.add, ALU.subtract
                                   ).then_inc(deg_ok, 1)
            v.wait_ge(deg_ok, 1)
            v.wait_ge(deg_std, 1)
            link(V.reciprocal(dinv[:], dinv[:]))
            link(V.tensor_tensor(tmp[:], dinv[:], dinv[:], ALU.mult))
            link(V.tensor_tensor(tmp[:], tmp[:], deg[:], ALU.mult))
            link(V.tensor_scalar(tmp[:], tmp[:], -0.5, 1.5, ALU.mult, ALU.add))
            V.tensor_tensor(dinv[:], dinv[:], tmp[:], ALU.mult).then_inc(dinv_ok, 1)
            v.wait_ge(dinv_ok, 1)
            for b in range(NRAW):
                v.wait_ge(h_out, b + 1)
                V.tensor_scalar(acc[:, b, 0:C], acc[:, b, 0:C], dinv[:, b:b + 1], None, ALU.mult
                                ).then_inc(scaled, 1)

            link(V.tensor_scalar(blk_i[:, 1, :], next_first[:], 7, None, ALU.arith_shift_right))
            link(V.memset(blk_i[0:1, 0, 0:1], 0))
            link(V.tensor_scalar(key[:, 0, :], blk_i[:, 0, :], part[:, 0:1], None, ALU.add))
            link(V.tensor_scalar(key[:, 1, :], blk_i[:, 1, :], part[:, 0:1], 1.0, ALU.add, ALU.add))

            def band(t):
                link(V.tensor_scalar(band_m[:, t % 2, :], col256[:], key[:, 1, t:t + 1], None, ALU.is_lt))
                V.scalar_tensor_tensor(bandf[:, t % 3, :], col256[:], key[:, 0, t:t + 1], band_m[:, t % 2, :],
                                       ALU.is_ge, ALU.mult).then_inc(bands, 1)

            band(0)
            for t in range(NT):
                if t + 1 < NT:
                    band(t + 1)
                v.wait_ge(item_ps, t + 1)
                w = slice(t * P, (t + 1) * P)
                V.tensor_copy(src_item[:, w], p_it[:, 0, :]).then_inc(items, 1)
                V.scalar_tensor_tensor(dst_item[:, w], p_it[:, 1, :], float(t * P * P), col128x[:],
                                       ALU.subtract, ALU.subtract).then_inc(items, 1)
                V.scalar_tensor_tensor(brow[:, t % 2, :], p_row[0:1, 0:P], -1.0, col[0:1, :],
                                       ALU.mult, ALU.add).then_inc(items, 1)
                v.wait_ge(items, 3 * t + 3)
                link(V.tensor_scalar(blk_item[0:1, LAG + t * P:LAG + (t + 1) * P], brow[:, t % 2, :],
                                     float(t * P), float(NBLK - 1), ALU.add, ALU.min))

        @block.scalar
        def _(s):
            s.wait_ge(consts, 7)

            def root(gi):
                s.wait_ge(stat, gi * GR + GR)
                w = bass.ds(gi * GR, GR)
                nc.scalar.activation(rstd[:, w], mv[:, w, 1], ACT.Sqrt, bias=eps_ln[:]).then_inc(std_ok, 1)

            def normalise(b, u):
                wait(s, tr_ok, b - GR + 1)
                nc.scalar.activation(xn[:, u, :], res[:, bass.ds(b, 1), :].rearrange("p a c -> p (a c)"),
                                     ACT.Identity, scale=rstd[:, bass.ds(b, 1)], bias=nmr[:, bass.ds(b, 1)]
                                     ).then_inc(xn_ok, 1)

            def copy(b, u):
                s.wait_ge(tr_ok, b + 1)
                wait(s, h_ok, b - GR + 1)
                nc.scalar.copy(xnT[:, u], p_tr[u % 2][:, 0:CH, :]).then_inc(xnT_ok, 1)

            def store(b, u, scale):
                s.wait_ge(h_ok, b + 1)
                o = acc[:, bass.ds(b, 1), 0:C].rearrange("p a c -> p (a c)")
                if scale:
                    nc.scalar.activation(o, p_h[u % 2][:, 0:C], ACT.Copy, scale=dinv[:, bass.ds(b, 1)]
                                         ).then_inc(h_out, 1)
                else:
                    nc.scalar.copy(o, p_h[u % 2][:, 0:C]).then_inc(h_out, 1)

            def group(gi, scale):
                s.wait_ge(rstd_ok, gi + 1)
                for u in range(GR):
                    b = gi * GR + u
                    normalise(b, u)
                    if not (isinstance(b, int) and b < 1):
                        copy(b - 1, (u - 1) % GR)
                    if not (isinstance(b, int) and b < 2):
                        store(b - 2, (u - 2) % GR, scale)

            root(0)
            root(1)
            group(0, False)
            with s.Fori(1, SG) as gi:
                root(gi + 1)
                group(gi, False)
            s.wait_ge(deg_ok, 1)
            nc.scalar.activation(dinv[:], deg[:], ACT.Sqrt).then_inc(deg_std, 1)
            s.wait_ge(dinv_ok, 1)
            for gi in range(SG, NG):
                group(gi, True)
            copy(NBLK - 1, GR - 1)
            store(NBLK - 2, GR - 2, True)
            store(NBLK - 1, GR - 1, True)
            s.wait_ge(dma_rows, 32)
            for t in range(NT):
                wait(s, item_ps, t - 1)
                nc.scalar.copy(rowf[:, t % 3, 0, :], src_rows[:, t, :]).then_inc(rows_ok, 1)
                nc.scalar.activation(rowf[:, t % 3, 1, :], dst_rows[:, t, :], ACT.Identity,
                                     bias=chunk0[:, t:t + 1]).then_inc(rows_ok, 1)

        @block.tensor
        def _(t_):
            pe = nc.tensor
            t_.wait_ge(onehots, 2)
            for t in range(NT):
                mm = pe.matmul(p_deg[:, 0:NBLK], one_lo[:, t, :], one_hi[:, t, :], start=(t == 0),
                               stop=(t == NT - 1))
            mm.then_inc(hist, 1)
            t_.wait_ge(consts, 7)
            t_.wait_ge(hist_sb, 1)
            pe.matmul(p_blk[0:NBLK, 0:P], firsts[:], ones[:], start=True, stop=True).then_inc(blk_ps, 1)
            t_.wait_ge(blk_sb, 1)
            pe.matmul(p_deg[:, 0:NBLK], below[:], firsts[:], start=True, stop=False)
            pe.matmul(p_deg[:, 0:NBLK], block_n[:], below[0:NBLK, 0:NBLK], start=False, stop=True
                      ).then_inc(less_ps, 1)
            t_.wait_ge(dma_gw, 16)

            def transposes(b, u):
                t_.wait_ge(xn_ok, b + 1)
                wait(t_, xnT_ok, b if u == 0 else b - 1)
                for a in range(CH):
                    mm = pe.transpose(p_tr[u % 2][:, a, :], xn[:, u, a * P:(a + 1) * P], ident[:])
                mm.then_inc(tr_ok, 1)

            def products(b, u):
                t_.wait_ge(xnT_ok, b + 1)
                wait(t_, h_out, b if u == 0 else b - 1)
                for a in range(CH):
                    mm = pe.matmul(p_h[u % 2][:, 0:C], xnT[:, u, a, :], gw_sb[:, a, :], start=(a == 0),
                                   stop=(a == CH - 1))
                mm.then_inc(h_ok, 1)

            def group(gi):
                for u in range(GR):
                    b = gi * GR + u
                    transposes(b, u)
                    if not (isinstance(b, int) and b < 1):
                        products(b - 1, (u - 1) % GR)

            group(0)
            with t_.Fori(1, SG) as gi:
                group(gi)
            t_.wait_ge(consts, 24)
            t_.wait_ge(place_ok, 1)
            pe.matmul(p_deg[:, 0:NBLK], next_p[:], place[:, 0:NBLK], start=True, stop=False)
            pe.matmul(p_deg[:, 0:NBLK], wrap_p[:], place[:, 1:NBLK + 1], start=False, stop=True
                      ).then_inc(shifted, 1)
            with t_.Fori(SG, NG) as gi:
                group(gi)
            products(NBLK - 1, GR - 1)

            for t in range(NT):
                t_.wait_ge(bands, t + 1)
                t_.wait_ge(rows_ok, 2 * t + 2)
                wait(t_, items, 3 * t)
                for k, wt in enumerate([t - 1, t] if t else [t]):
                    f = slice(P, 2 * P) if wt < t else slice(0, P)
                    lastk = wt == t
                    for q in range(2):
                        pe.matmul(p_it[:, q, :], rowf[:, wt % 3, q, :], bandf[:, wt % 3, f],
                                  start=(k == 0 and q == 0), stop=lastk, skip_group_check=True)
                    mm = pe.matmul(p_row[0:1, 0:P], chunkn[:, wt:wt + 1], bandf[:, wt % 3, f],
                                   start=(k == 0), stop=lastk)
                mm.then_inc(item_ps, 1)


def aggregate_and_mix(nc, sb, ps, sem, g):
    (table, acc, res, src_item, dst_item, blk_item, rstd, nmr, kvz, ident, col, wq_sb, w1t_sb, w2t_sb,
     dma_w, v1, headmask) = (g[k] for k in ("table", "acc", "res", "src_item", "dst_item", "blk_item", "rstd", "nmr", "kvz",
                              "ident", "col", "wq_sb", "w1t_sb", "w2t_sb", "dma_w", "v1", "headmask"))
    slots, dma_empty = g["slots"], g["dma_empty"]
    NDMA_W = 12
    first_mix = NKV
    with ExitStack() as st:
        ring = sb("ring", [P, RING, C], st=st)
        sel = sb("sel", [P, RING, P], st=st)
        idx = sb("idx", [P, PER], I32, st)
        empty = sb("empty", [P, ROW], st=st)
        xn = sb("xn_m", [P, C], st=st)
        xnT = sb("xnT_m", [P, CH, P], st=st)
        qr = sb("qr", [P, CH, P], st=st)
        qe = sb("qe", [P, CH, P], st=st)
        qT = sb("qT", [P, CH, P], st=st)
        den = sb("den", [P, CH, P // DH], st=st)
        t = sb("t_m", [P, CH, P], st=st)
        st1, st2 = sb("st1", [P, 6], st=st), sb("st2", [P, 6], st=st)
        mv1, mv2 = sb("mv1", [P, 2], st=st), sb("mv2", [P, 2], st=st)
        sd1, sd2 = sb("sd1", [P, 1], st=st), sb("sd2", [P, 1], st=st)
        r1, r2 = sb("r1", [P, 1], st=st), sb("r2", [P, 1], st=st)
        nm1, nm2 = sb("nm1", [P, 1], st=st), sb("nm2", [P, 1], st=st)
        tmp1, tmp2 = sb("tmp1", [P, 1], st=st), sb("tmp2", [P, 1], st=st)
        x1n = sb("x1n", [P, C], st=st)
        x1T = sb("x1T", [P, CH, P], st=st)
        gT = sb("gT", [P, CH, P], st=st)
        yn = sb("yn", [P, C], st=st)
        kr = sb("kr", [P, C], st=st)
        ke = sb("ke", [P, 2, C], st=st)
        kf = sb("kf", [P, 2, C], st=st)
        p_item = [ps(f"p_item{i}", [P, 512], st) for i in range(PSLOT)]
        p_t = ps("p_t", [P, 4, P], st)
        p_q = ps("p_q", [P, 4, P], st)
        p_nd = ps("p_nd", [P, CH, 2 * P], st)
        p_g = ps("p_g", [P, 4, P], st)
        p_y = ps("p_y", [P, 512], st)
        p_kv = p_q[:].rearrange("p a c -> p (a c)")
        p_kk = [p_g[:].rearrange("p a c -> p (a c)"), p_y[:]]
        KSTEP = PER // KVB

        gathered = [sem(f"gathered{i}", st) for i in range(RING // TRI)]
        multiplied = sem("multiplied", st)
        selected = sem("selected", st)
        added = sem("added", st)
        idx_ok = sem("idx_ok", st)
        kx_ok, ktr, kxT_ok, kv_ok, kr_ok, kv_act, k_ok, kv_acc, kvz_st = (sem("k_" + n, st) for n in (
            "xn", "tr", "xnT", "kv", "kr", "act", "k", "acc", "z"))
        const2 = sem("const2", st)
        xn_ok, tr1_ok, xnT_ok, q_ps, q_rel, q_exp, qT_ok, nd_ps, den_ok = (sem("m_" + n, st) for n in (
            "xn", "tr1", "xnT", "qps", "qrel", "qexp", "qT", "ndps", "den"))
        t_rec, t_mul, t_add, s_st1, var1, std1, n1 = (sem("m_" + n, st) for n in (
            "trec", "tmul", "tadd", "st1", "var1", "std1", "n1"))
        x1n_ok, tr2_ok, x1T_ok, g_ps, gelu_ok, y_ps = (sem("m_" + n, st) for n in (
            "x1n", "tr2", "x1T", "gps", "gelu", "yps"))
        s_st2, var2, std2, n2, yn_ok, fin = (sem("m_" + n, st) for n in ("st2", "var2", "std2", "n2", "yn", "fin"))
        block = st.enter_context(nc.Block())

        def dyn(tile, b):
            return tile[:, bass.ds(b, 1), :].rearrange("p a c -> p (a c)")

        @block.sync
        def _(sp):
            sp.dma_start(g["fb1_sb"][:], g["fb1"]).then_inc(g["dma_fb"], 16)
            sp.wait_ge(const2, 2)
            full = SLOTS // P
            sp.dma_start(slots[0:full * P, :].rearrange("(a p) c -> p a c", p=P),
                         empty[:].rearrange("p (a c) -> p a c", a=1).broadcast_to([P, full, ROW])
                         ).then_inc(dma_empty, 16)
            sp.dma_start(slots[full * P:SLOTS, :], empty[0:SLOTS - full * P, :]).then_inc(dma_empty, 16)
            sp.wait_ge(dma_empty, 32)

        @block.gpsimd
        def _(pool):
            nc.gpsimd.memset(empty[:], 0.0).then_inc(const2, 1)
            pool.wait_ge(const2, 1)
            nc.gpsimd.memset(empty[:, C + 3:C + 4].bitcast(I32), NOWHERE).then_inc(const2, 1)

            def gathers(it):
                for k in range(PER):
                    if k % GRP == 0:
                        pool.wait_ge(idx_ok, it * (PER // GRP) + k // GRP + 1)
                    wait_apart(pool, multiplied, it * PER + k - RING + 1, const2, 2)
                    nc.gpsimd.indirect_dma_start(ring[:, k % RING, :], None, table,
                                                 bass.IndirectOffsetOnAxis(idx[:, k:k + 1], 0)
                                                 ).then_inc(gathered[k // TRI], 16)

            gathers(0)
            with pool.Fori(1, NPASS) as it:
                gathers(it)

        @block.tensor
        def _(t_):
            pe = nc.tensor
            t_.wait_ge(dma_w, 16 * NDMA_W)

            def item(it, k):
                i = it * PER + k
                if k % TRI == 0:
                    t_.wait_ge(gathered[k // TRI], (it + 1) * 16 * TRI)
                t_.wait_ge(selected, i + 1)
                wait(t_, added, i - PSLOT + 1)
                pe.matmul(p_item[k % PSLOT][:, 0:C], sel[:, k % RING, :], ring[:, k % RING, :],
                          start=True, stop=True).then_inc(multiplied, 1)

            def transposes_x(b):
                t_.wait_ge(xn_ok, b + 1)
                wait(t_, x1T_ok, b * 2)
                for a in range(CH):
                    mm = pe.transpose(p_t[:, a, :], xn[:, a * P:(a + 1) * P], ident[:])
                mm.then_inc(tr1_ok, 1)

            def queries(b):
                t_.wait_ge(xnT_ok, b + 1)
                wait(t_, qT_ok, b)
                for m in range(CH):
                    for a in range(CH):
                        mm = pe.matmul(p_q[:, m, :], wq_sb[:, a, m * P:(m + 1) * P], xnT[:, a, :],
                                       start=(a == 0), stop=(a == CH - 1))
                mm.then_inc(q_ps, 1)

            def attention(b):
                t_.wait_ge(qT_ok, b + 1)
                wait(t_, t_mul, b * CH)
                for a in range(CH):
                    mm = pe.matmul(p_nd[:, a, 0:P + P // DH], qT[:, a, :], kvz[:, a, :], start=True, stop=True)
                mm.then_inc(nd_ps, 1)

            def transposes_x1(b):
                t_.wait_ge(x1n_ok, b + 1)
                t_.wait_ge(xnT_ok, b + 1)
                for a in range(CH):
                    mm = pe.transpose(p_t[:, a, :], x1n[:, a * P:(a + 1) * P], ident[:])
                mm.then_inc(tr2_ok, 1)

            def hidden(b):
                t_.wait_ge(x1T_ok, b * 2 + 2)
                wait(t_, gelu_ok, b * 2)
                for m in range(CH):
                    for a in range(CH):
                        mm = pe.matmul(p_g[:, m, :], w1t_sb[:, a, m * P:(m + 1) * P], x1T[:, a, :],
                                       start=(a == 0), stop=(a == CH - 1))
                mm.then_inc(g_ps, 1)

            def output(b):
                t_.wait_ge(gelu_ok, b * 2 + 2)
                wait(t_, yn_ok, b)
                for a in range(CH):
                    pe.matmul(p_y[:, 0:C], gT[:, a, :], w2t_sb[:, a, :], start=(a == 0), stop=False,
                              skip_group_check=True)
                for a in range(CH):
                    pe.matmul(p_y[:, a * P:(a + 1) * P], x1T[:, a, :], ident[:], start=False, stop=False,
                              skip_group_check=True)
                pe.matmul(p_y[:, 0:C], g["ones_row"][:], g["b2row"][:], start=False, stop=True,
                          skip_group_check=True).then_inc(y_ps, 1)

            def kv_transposes(b):
                t_.wait_ge(kx_ok, b + 1)
                wait(t_, kxT_ok, b)
                for a in range(CH):
                    mm = pe.transpose(p_t[:, a, :], xn[:, a * P:(a + 1) * P], ident[:])
                mm.then_inc(ktr, 1)

            def kv_products(b):
                t_.wait_ge(kxT_ok, b + 1)
                wait(t_, k_ok, b)
                for a in range(CH):
                    mm = pe.matmul(p_kv, xnT[:, a, :], wq_sb[:, a, C:3 * C], start=(a == 0), stop=(a == CH - 1))
                mm.then_inc(kv_ok, 1)

            def kv_sums(b, u, rows, first, last):
                t_.wait_ge(k_ok, b + 1)
                for a in range(CH):
                    mm = pe.matmul(p_kk[a][:, 0:P + 2], kf[0:rows, u, a * P:(a + 1) * P], v1[0:rows, u, a, :],
                                   start=first, stop=last)
                mm.then_inc(kv_acc, 1)

            def kv_pass(it, blocks):
                for k in range(PER):
                    item(it, k)
                    j = k // KSTEP
                    b = it * KVB + j
                    if k % KSTEP == 1 and j < blocks:
                        kv_transposes(b)
                    if k % KSTEP == 3 and j <= blocks and j < KVB:
                        if not (isinstance(b, int) and b == 0):
                            last = isinstance(b, int) and b == NBLK
                            kv_sums(b - 1, (j - 1) % 2, LAST if last else P, isinstance(b, int) and b == 1, last)
                        if j < blocks:
                            kv_products(b)

            def mix_pass(it, first=False, last=False):
                b = it - first_mix
                for k in range(PER):
                    item(it, k)
                    if not first:
                        if k == 0:
                            transposes_x1(b - 1)
                        if k == 2:
                            hidden(b - 1)
                        if k == 7:
                            output(b - 1)
                    if not last:
                        if k == 3:
                            transposes_x(b)
                        if k == 5:
                            queries(b)
                        if k == 10:
                            attention(b)

            kv_pass(0, KVB)
            with t_.Fori(1, NKV - 1) as it:
                kv_pass(it, KVB)
            kv_pass(NKV - 1, NBLK - KVB * (NKV - 1))
            t_.wait_ge(kvz_st, 2 * CH)
            mix_pass(first_mix, first=True)
            with t_.Fori(first_mix + 1, first_mix + NBLK) as it:
                mix_pass(it)
            mix_pass(first_mix + NBLK, last=True)
            with t_.Fori(first_mix + NBLK + 1, NPASS) as it:
                for k in range(PER):
                    item(it, k)

        @block.scalar
        def _(s):
            s.wait_ge(const2, 2)
            s.wait_ge(dma_w, 16 * NDMA_W)

            def keys(b, u):
                wait(s, ktr, b)
                nc.scalar.activation(xn[:], dyn(res, b), ACT.Identity, scale=rstd[:, bass.ds(b, 1)],
                                     bias=nmr[:, bass.ds(b, 1)]).then_inc(kx_ok, 1)
                s.wait_ge(ktr, b + 1)
                wait(s, kv_ok, b)
                nc.scalar.copy(xnT[:], p_t[:, 0:CH, :]).then_inc(kxT_ok, 1)
                s.wait_ge(kv_ok, b + 1)
                wait(s, kv_act, b * 2)
                nc.scalar.activation(kr[:], p_kv[:, 0:C], ACT.Relu, scale=-1.0).then_inc(kr_ok, 1)
                wait(s, k_ok, b - 1)
                wait(s, kv_acc, b - 1)
                nc.scalar.copy(v1[:, u, :, 0:P], p_kv[:, C:2 * C].rearrange("p (a c) -> p a c", a=CH)
                               ).then_inc(kv_act, 1)
                s.wait_ge(kr_ok, b + 1)
                nc.scalar.activation(ke[:, u, :], kr[:], ACT.Exp, scale=-1.0).then_inc(kv_act, 1)

            def normalised_t(c):
                s.wait_ge(var1, c + 1)
                nc.scalar.activation(sd1[:], mv1[:, 1:2], ACT.Sqrt, bias=g["eps_ln"][:]).then_inc(std1, 1)
                s.wait_ge(n1, c * 6 + 6)
                wait(s, tr2_ok, c)
                nc.scalar.activation(x1n[:], t[:].rearrange("p a c -> p (a c)"), ACT.Identity, scale=r1[:],
                                     bias=nm1[:]).then_inc(x1n_ok, 1)

            def x1_transposed(c):
                s.wait_ge(tr2_ok, c + 1)
                wait(s, y_ps, c)
                for a in range(CH):
                    nc.scalar.activation(x1T[:, a, :], p_t[:, a, :], ACT.Identity,
                                         scale=g["cols"]["ln1g"][:, a:a + 1], bias=g["cols"]["ln1b"][:, a:a + 1]
                                         ).then_inc(x1T_ok, 1)

            def gelu(c):
                s.wait_ge(g_ps, c + 1)
                for a in range(CH):
                    nc.scalar.activation(gT[:, a, :], p_g[:, a, :], ACT.Gelu, bias=g["cols"]["b1"][:, a:a + 1]
                                         ).then_inc(gelu_ok, 1)

            def normalised_y(c):
                s.wait_ge(var2, c + 1)
                nc.scalar.activation(sd2[:], mv2[:, 1:2], ACT.Sqrt, bias=g["eps_ln"][:]).then_inc(std2, 1)
                s.wait_ge(n2, c * 6 + 6)
                wait(s, fin, c * 3)
                nc.scalar.activation(yn[:], p_y[:, 0:C], ACT.Identity, scale=r2[:], bias=nm2[:]
                                     ).then_inc(yn_ok, 1)

            def x_normalised(b):
                wait(s, tr1_ok, b)
                wait(s, t_add, b)
                nc.scalar.activation(xn[:], dyn(res, b), ACT.Identity, scale=rstd[:, bass.ds(b, 1)],
                                     bias=nmr[:, bass.ds(b, 1)]).then_inc(xn_ok, 1)

            def queries(b):
                s.wait_ge(tr1_ok, b + 1)
                wait(s, q_ps, b)
                nc.scalar.copy(xnT[:], p_t[:, 0:CH, :]).then_inc(xnT_ok, 1)
                s.wait_ge(q_ps, b + 1)
                wait(s, q_exp, b)
                nc.scalar.activation(qr[:], p_q[:, 0:CH, :], ACT.Relu, scale=-1.0).then_inc(q_rel, 1)
                s.wait_ge(q_rel, b + 1)
                wait(s, qT_ok, b)
                nc.scalar.activation(qe[:], qr[:], ACT.Exp, scale=-1.0).then_inc(q_exp, 1)

            def mix_pass(it, first=False, last=False):
                b = it - first_mix
                if not last:
                    x_normalised(b)
                if not first:
                    x1_transposed(b - 1)
                    gelu(b - 1)
                if not last:
                    queries(b)
                if not first:
                    normalised_y(b - 1)
                if not last:
                    normalised_t(b)

            for b in range(2):
                keys(b, b)
            with s.Fori(1, NBLK // 2) as it:
                for u in range(2):
                    keys(it * 2 + u, u)
            keys(NBLK - 1, 0)
            s.wait_ge(kv_acc, NBLK)
            mix_pass(first_mix, first=True)
            with s.Fori(first_mix + 1, first_mix + NBLK) as it:
                mix_pass(it)
            mix_pass(first_mix + NBLK, last=True)

        @block.vector
        def _(v):
            v.wait_ge(dma_w, 16 * NDMA_W)
            regs = [v.alloc_register(f"item_block{i}") for i in range(GRP)]

            def sources(it, q):
                nc.vector.tensor_copy(idx[:, q * GRP:(q + 1) * GRP],
                                      src_item[:, bass.ds(it * PER + q * GRP, GRP)]).then_inc(idx_ok, 1)

            def select(it, k):
                nc.vector.tensor_scalar(sel[:, k % RING, :], col[:], dst_item[:, bass.ds(it * PER + k, 1)], None,
                                        ALU.is_equal).then_inc(selected, 1)

            def add(j, slot, blk):
                v.wait_ge(multiplied, j + 1)
                wait(v, added, j)
                a = acc[:, bass.ds(blk, 1), 0:C].rearrange("p a c -> p (a c)")
                nc.vector.tensor_tensor(a, a, p_item[slot][:, 0:C], ALU.add).then_inc(added, 1)

            def queries(b):
                v.wait_ge(q_exp, b + 1)
                wait(v, nd_ps, b)
                nc.vector.scalar_tensor_tensor(qT[:], p_q[:, 0:CH, :], 0.0, qe[:], ALU.max, ALU.add
                                               ).then_inc(qT_ok, 1)

            def attention(b, n):
                if n == 0:
                    v.wait_ge(nd_ps, b + 1)
                    nc.vector.tensor_scalar(den[:], p_nd[:, :, P:P + P // DH], EPS_ATTN, None, ALU.add
                                            ).then_inc(den_ok, 1)
                    v.wait_ge(den_ok, b + 1)
                    nc.vector.reciprocal(den[:], den[:]).then_inc(t_rec, 1)
                if n == 1:
                    v.wait_ge(t_rec, b + 1)
                    wait(v, x1n_ok, b)
                    for a in range(CH):
                        heads = "p (h d) -> p h d"
                        nc.vector.tensor_tensor(t[:, a, :].rearrange(heads, d=DH),
                                                p_nd[:, a, 0:P].rearrange(heads, d=DH),
                                                den[:, a, :].rearrange("p (h d) -> p h d", d=1)
                                                .broadcast_to([P, P // DH, DH]), ALU.mult).then_inc(t_mul, 1)
                if n == 2:
                    v.wait_ge(t_mul, b * CH + CH)
                    t2 = t[:].rearrange("p a c -> p (a c)")
                    nc.vector.tensor_tensor(t2, t2, xn[:], ALU.add).then_inc(t_add, 1)

            def norm(b, n, src, ready, stt, st_sem, mv, var, sd, std, r, nm, tmp, s_n):
                V = nc.vector
                if n == 0:
                    wait_apart(v, ready, b + 1, g["consts"], 16)
                    V.bn_stats(stt[:], src).then_inc(st_sem, 1)
                if n == 1:
                    wait_apart(v, st_sem, b + 1, g["consts"], 16)
                    V.bn_aggr(mv[:], stt[:]).then_inc(var, 1)
                if n == 2:
                    v.wait_ge(std, b + 1)
                    V.reciprocal(r[:], sd[:]).then_inc(s_n, 1)
                if n > 2:
                    v.wait_ge(s_n, b * 6 + n - 2)
                if n == 3:
                    V.scalar_tensor_tensor(tmp[:], mv[:, 1:2], EPS, r[:], ALU.add, ALU.mult).then_inc(s_n, 1)
                if n == 4:
                    V.tensor_tensor(tmp[:], tmp[:], r[:], ALU.mult).then_inc(s_n, 1)
                if n == 5:
                    V.tensor_scalar(tmp[:], tmp[:], -0.5, 1.5, ALU.mult, ALU.add).then_inc(s_n, 1)
                if n == 6:
                    V.tensor_tensor(r[:], r[:], tmp[:], ALU.mult).then_inc(s_n, 1)
                if n == 7:
                    V.scalar_tensor_tensor(nm[:], mv[:, 0:1], -1.0, r[:], ALU.mult, ALU.mult).then_inc(s_n, 1)

            def norm1(b, n):
                norm(b, n, t[:].rearrange("p a c -> p (a c)"), t_add, st1, s_st1, mv1, var1, sd1, std1, r1, nm1,
                     tmp1, n1)

            def norm2(b, n):
                norm(b, n, p_y[:, 0:C], y_ps, st2, s_st2, mv2, var2, sd2, std2, r2, nm2, tmp2, n2)

            def finish(b, n):
                if n == 0:
                    v.wait_ge(yn_ok, b + 1)
                    nc.vector.tensor_tensor(yn[:], yn[:], g["bias_b"]["ln2g"][:], ALU.mult).then_inc(fin, 1)
                if n == 1:
                    v.wait_ge(fin, b * 3 + 1)
                    nc.vector.tensor_tensor(yn[:], yn[:], g["bias_b"]["ln2b"][:], ALU.add).then_inc(fin, 1)
                if n == 2:
                    v.wait_ge(fin, b * 3 + 2)
                    nc.vector.tensor_tensor(dyn(res, b), dyn(res, b), yn[:], ALU.add).then_inc(fin, 1)

            def keys_of(b, u):
                v.wait_ge(kv_act, b * 2 + 2)
                wait(v, kv_acc, b - 1)
                nc.vector.scalar_tensor_tensor(kf[:, u, :], p_kv[:, 0:C], 0.0, ke[:, u, :], ALU.max, ALU.add
                                               ).then_inc(k_ok, 1)

            def items(it, k, blk):
                if k % GRP == 0:
                    v.load(regs, blk_item[0:1, bass.ds(it * PER + k, GRP)])
                    blk[:] = [v.snap(r, min_val=0, max_val=NBLK - 1) for r in regs]
                select(it, k)
                if not (isinstance(it, int) and it * PER + k < LAG):
                    add(it * PER + k - LAG, (k - LAG) % PSLOT, blk[k % GRP])
                if k == 4:
                    sources(it, 2)
                if k == 11:
                    sources(it + 1, 0)
                if k == 18:
                    sources(it + 1, 1)

            def kv_pass(it, blocks):
                blk = []
                for k in range(PER):
                    items(it, k, blk)
                    j = k // KSTEP
                    b = it * KVB + j
                    if k % KSTEP == 3 and j <= blocks and j < KVB and not (isinstance(b, int) and b == 0):
                        keys_of(b - 1, (j - 1) % 2)

            def mix_pass(it, first=False, last=False):
                b = it - first_mix
                blk = []
                for k in range(PER):
                    items(it, k, blk)
                    if not first:
                        if k in (11, 12):
                            norm2(b - 1, k - 11)
                        if k in (13, 14, 15):
                            norm2(b - 1, 2 * (k - 13) + 2)
                            norm2(b - 1, 2 * (k - 13) + 3)
                        if k in (18, 19, 20):
                            finish(b - 1, k - 18)
                    if not last:
                        if k == 10:
                            queries(b)
                        if k in (14, 15, 16):
                            attention(b, k - 14)
                        if k == 17:
                            norm1(b, 0)
                            norm1(b, 1)
                        if k == 19:
                            norm1(b, 2)
                            norm1(b, 3)
                        if k == 20:
                            for n in range(4, 8):
                                norm1(b, n)

            sources(0, 0)
            sources(0, 1)
            kv_pass(0, KVB)
            with v.Fori(1, NKV - 1) as it:
                kv_pass(it, KVB)
            kv_pass(NKV - 1, NBLK - KVB * (NKV - 1))
            v.wait_ge(kv_acc, NBLK)
            for a in range(CH):
                nc.vector.tensor_tensor(kvz[:, a, 0:P], p_kk[a][:, 0:P], headmask[:], ALU.mult).then_inc(kvz_st, 1)
                nc.vector.tensor_scalar(kvz[:, a, P:P + P // DH],
                                        headmask[:].rearrange("p (h d) -> p h d", d=DH)[:, :, 0],
                                        p_kk[a][:, P:P + 1], None, ALU.mult).then_inc(kvz_st, 1)
            mix_pass(first_mix, first=True)
            with v.Fori(first_mix + 1, first_mix + NBLK) as it:
                mix_pass(it)
            mix_pass(first_mix + NBLK, last=True)
            with v.Fori(first_mix + NBLK + 1, NPASS) as it:
                blk = []
                for k in range(PER):
                    items(it, k, blk)
            v.load(regs[0:LAG], blk_item[0:1, NITEM:NITEM + LAG])
            for q in range(LAG):
                j = NITEM - LAG + q
                add(j, (PER - LAG + q) % PSLOT, v.snap(regs[q], min_val=0, max_val=NBLK - 1))


def route(nc, sb, ps, sem, g):
    (acc, res, rstd, nmr, dinv, ident, gate_sb, gateb_b, slots, dma_empty, dma_out, out) = (g[k] for k in (
        "acc", "res", "rstd", "nmr", "dinv", "ident", "gate_sb", "gateb_b", "slots", "dma_empty", "dma_out", "out"))
    GR = 7
    NG = NBLK // GR
    assert NG * GR == NBLK
    with ExitStack() as st:
        stt = sb("stt", [P, GR, 6], st=st)
        mvg = sb("mvg", [P, GR, 2], st=st)
        sdg = sb("sdg", [P, GR], st=st)
        tmp = sb("tmp_r", [P, GR], st=st)
        xr = sb("xr", [P, GR, C], st=st)
        xrT = sb("xrT", [P, GR, CH, P], st=st)
        triu = sb("triu", [P, P], st=st)
        ones = sb("ones", [P, P], st=st)
        e8 = sb("e8", [P, EXP], st=st)
        base = sb("base", [P, EXP], st=st)
        node_i = sb("node_i", [P, NBLK], I32, st)
        node_f = sb("node_f", [P, NBLK], st=st)
        B8 = [P, NBLK, EXP]
        lg, ex, oh, cand = sb("lg", B8, st=st), sb("ex", B8, st=st), sb("oh", B8, st=st), sb("cand", B8, st=st)
        sa, sc = sb("sa", B8, st=st), sb("sc", B8, st=st)
        tot = sb("tot", B8, st=st)
        m1 = sb("m1", [P, NBLK], st=st)
        prob = sb("prob", [P, NBLK], st=st)
        rowno = sb("rowno", [P, NBLK], st=st)
        kept = sb("kept", [P, NBLK], st=st)
        dest = sb("dest", [P, NBLK], I32, st)
        p_t = [ps(f"r_t{i}", [P, 4, P], st) for i in range(2)]
        p_l = ps("r_l", [P, 512], st)
        p_in = ps("r_in", [P, 512], st)
        p_to = ps("r_to", [P, 512], st)
        const3, s1, s2, s3, s4, g5, std, xr_ok, tr_ok, xT_ok, l_ps, dv, e_ok, e_act, oh_ok, cum, dest_ok, x2_ok, sent = (
            sem("r_" + n, st) for n in ("const3", "s1", "s2", "s3", "s4", "g5", "std", "xr", "tr", "xT", "lps",
                                        "dv", "e", "eact", "oh", "cum", "dest", "x2", "sent"))
        block = st.enter_context(nc.Block())

        def row(tile, b):
            return tile[:, bass.ds(b, 1), 0:C].rearrange("p a c -> p (a c)")

        @block.gpsimd
        def _(pool):
            nc.gpsimd.memset(ones[:], 1.0).then_inc(const3, 1)
            nc.gpsimd.memset(triu[:], 1.0).then_inc(const3, 1)
            nc.gpsimd.iota(e8[:], [[1, EXP]], 0, 0, allow_small_or_imprecise_dtypes=True).then_inc(const3, 1)
            nc.gpsimd.iota(base[:], [[CAP, EXP]], -1, 0, allow_small_or_imprecise_dtypes=True).then_inc(const3, 1)
            nc.gpsimd.iota(node_i[:], [[P, NBLK]], 0, 1).then_inc(const3, 1)
            nc.gpsimd.iota(node_f[:], [[P, NBLK]], 0, 1, allow_small_or_imprecise_dtypes=True).then_inc(const3, 1)
            pool.wait_ge(const3, 6)
            nc.gpsimd.affine_select(triu[:], triu[:], [[1, P]], ALU.is_ge, 0.0, 0, -1).then_inc(const3, 1)
            pool.wait_ge(dma_empty, 32)
            pool.wait_ge(dest_ok, 1)
            for b in range(NBLK):
                nc.gpsimd.indirect_dma_start(slots, bass.IndirectOffsetOnAxis(dest[:, b:b + 1], 0), acc[:, b, :],
                                             None, bounds_check=SLOTS - 1, oob_is_err=False).then_inc(sent, 16)
            pool.wait_ge(sent, 16 * NBLK)

        @block.sync
        def _(sp):
            sp.wait_ge(x2_ok, 1)
            sp.dma_start(out.rearrange("(b p) c -> p b c", p=P), acc[:, :, 0:C]).then_inc(dma_out, 16)
            sp.wait_ge(dma_out, 16)

        @block.vector
        def _(v):
            V = nc.vector

            def group(gi):
                for u in range(GR):
                    b = gi * GR + u
                    V.scalar_tensor_tensor(row(acc, b), row(acc, b), dinv[:, bass.ds(b, 1)], g["bias_b"]["gb"][:],
                                           ALU.mult, ALU.add).then_inc(s1, 1)
                for u in range(GR):
                    b = gi * GR + u
                    v.wait_ge(s1, b + 1)
                    V.scalar_tensor_tensor(row(acc, b), row(acc, b), 0.0, row(res, b), ALU.max, ALU.add
                                           ).then_inc(s2, 1)
                for u in range(GR):
                    b = gi * GR + u
                    wait_apart(v, s2, b + 1, const3, 7)
                    V.bn_stats(stt[:, u, :], row(acc, b)).then_inc(s3, 1)
                for u in range(GR):
                    b = gi * GR + u
                    wait_apart(v, s3, b + 1, const3, 7)
                    V.bn_aggr(mvg[:, u, :], stt[:, u, :]).then_inc(s4, 1)
                gs = slice(0, GR)
                r = rstd[:, bass.ds(gi * GR, GR)]
                nm = nmr[:, bass.ds(gi * GR, GR)]
                v.wait_ge(std, gi + 1)

                def step(n, ins):
                    ins.then_inc(g5, 1)
                    v.wait_ge(g5, gi * 6 + n)

                step(1, V.reciprocal(r, sdg[:]))
                step(2, V.scalar_tensor_tensor(tmp[:], mvg[:, :, 1], EPS, r, ALU.add, ALU.mult))
                step(3, V.tensor_tensor(tmp[:], tmp[:], r, ALU.mult))
                step(4, V.tensor_scalar(tmp[:], tmp[:], -0.5, 1.5, ALU.mult, ALU.add))
                step(5, V.tensor_tensor(r, r, tmp[:], ALU.mult))
                step(6, V.scalar_tensor_tensor(nm, mvg[:, :, 0], -1.0, r, ALU.mult, ALU.mult))

            v.wait_ge(const3, 7)
            group(0)
            with v.Fori(1, NG) as gi:
                group(gi)
            V.memset(m1[:], 0.0).then_inc(x2_ok, 1)

            n = [0]

            def link(ins):
                n[0] += 1
                ins.then_inc(dv, 1)
                v.wait_ge(dv, n[0])

            def over_e(a):
                return a[:].rearrange("p (b e) -> p b e", e=1).broadcast_to(B8)

            def over_b(a):
                return a[:].rearrange("p (b e) -> p b e", b=1).broadcast_to(B8)

            v.wait_ge(x2_ok, 1)
            v.wait_ge(l_ps, NBLK)
            link(V.tensor_tensor(lg[:], p_l[:, 0:NBLK * EXP].rearrange("p (b e) -> p b e", e=EXP),
                                 over_b(gateb_b), ALU.add))
            link(V.tensor_reduce(m1[:], lg[:], AX.X, ALU.max))
            V.tensor_tensor(ex[:], lg[:], over_e(m1), ALU.subtract).then_inc(e_ok, 1)
            link(V.tensor_tensor(cand[:], lg[:], over_e(m1), ALU.is_equal))
            link(V.tensor_scalar(cand[:], cand[:], -float(EXP), None, ALU.mult))
            link(V.tensor_tensor(cand[:], cand[:], over_b(e8), ALU.add))
            link(V.tensor_reduce(m1[:], cand[:], AX.X, ALU.min))
            V.tensor_tensor(oh[:], cand[:], over_e(m1), ALU.is_equal).then_inc(oh_ok, 1)
            v.wait_ge(oh_ok, 1)
            v.wait_ge(e_act, 1)
            link(V.tensor_reduce(prob[:], ex[:], AX.X, ALU.add))
            link(V.reciprocal(prob[:], prob[:]))
            v.wait_ge(cum, 2)
            link(V.tensor_copy(tot[:], p_to[:, 0:NBLK * EXP].rearrange("p (b e) -> p b e", e=EXP)))
            cur, nxt = tot, sa
            sh = 1
            while sh < NBLK:
                link(V.tensor_tensor(nxt[:, sh:, :], cur[:, sh:, :], cur[:, 0:NBLK - sh, :], ALU.add))
                link(V.tensor_copy(nxt[:, 0:sh, :], cur[:, 0:sh, :]))
                cur, nxt = nxt, (sc if nxt is sa else sa)
                sh *= 2
            link(V.tensor_tensor(nxt[:], cur[:], tot[:], ALU.subtract))
            link(V.tensor_tensor(nxt[:], nxt[:], p_in[:, 0:NBLK * EXP].rearrange("p (b e) -> p b e", e=EXP),
                                 ALU.add))
            link(V.tensor_tensor(cur[:], nxt[:], oh[:], ALU.mult))
            link(V.tensor_reduce(m1[:], cur[:], AX.X, ALU.add))
            link(V.tensor_tensor(nxt[:], nxt[:], over_b(base), ALU.add))
            link(V.tensor_tensor(nxt[:], nxt[:], oh[:], ALU.mult))
            link(V.tensor_reduce(rowno[:], nxt[:], AX.X, ALU.add))
            link(V.tensor_scalar(kept[:], node_f[:], float(N), None, ALU.is_lt))
            link(V.scalar_tensor_tensor(kept[:], m1[:], float(CAP), kept[:], ALU.is_le, ALU.mult))
            link(V.scalar_tensor_tensor(rowno[:], rowno[:], -float(NOWHERE), kept[:], ALU.add, ALU.mult))
            link(V.tensor_scalar(dest[:], rowno[:], float(NOWHERE), None, ALU.add))
            link(V.tensor_copy(acc[:, :, C], nmr[:]))
            link(V.tensor_copy(acc[:, :, C + 1], rstd[:]))
            link(V.tensor_copy(acc[:, :, C + 2], prob[:]))
            V.tensor_copy(acc[:, :, C + 3:C + 4].bitcast(I32).rearrange("p b a -> p (b a)"), node_i[:]
                          ).then_inc(dest_ok, 1)

        @block.scalar
        def _(s):
            def group(gi):
                s.wait_ge(s4, gi * GR + GR)
                wait(s, g5, gi * 6)
                nc.scalar.activation(sdg[:], mvg[:, :, 1], ACT.Sqrt, bias=g["eps_ln"][:]).then_inc(std, 1)
                s.wait_ge(g5, gi * 6 + 6)
                for u in range(GR):
                    b = gi * GR + u
                    wait(s, tr_ok, b - GR + 1)
                    nc.scalar.activation(xr[:, u, :], row(acc, b), ACT.Identity, scale=rstd[:, bass.ds(b, 1)],
                                         bias=nmr[:, bass.ds(b, 1)]).then_inc(xr_ok, 1)
                    if u > 0:
                        copy(b - 1, u - 1)
                copy(gi * GR + GR - 1, GR - 1)

            def copy(b, u):
                s.wait_ge(tr_ok, b + 1)
                wait(s, l_ps, b - GR + 1)
                nc.scalar.copy(xrT[:, u], p_t[u % 2][:, 0:CH, :]).then_inc(xT_ok, 1)

            group(0)
            with s.Fori(1, NG) as gi:
                group(gi)
            s.wait_ge(e_ok, 1)
            nc.scalar.activation(ex[:], ex[:], ACT.Exp).then_inc(e_act, 1)

        @block.tensor
        def _(t_):
            pe = nc.tensor
            t_.wait_ge(const3, 7)

            def group(gi):
                for u in range(GR):
                    b = gi * GR + u
                    t_.wait_ge(xr_ok, b + 1)
                    wait(t_, xT_ok, b if u == 0 else b - 1)
                    for a in range(CH):
                        mm = pe.transpose(p_t[u % 2][:, a, :], xr[:, u, a * P:(a + 1) * P], ident[:])
                    mm.then_inc(tr_ok, 1)
                    if u > 0:
                        logits(b - 1, u - 1)
                logits(gi * GR + GR - 1, GR - 1)

            def logits(b, u):
                t_.wait_ge(xT_ok, b + 1)
                o = p_l[:, bass.ds(b * EXP, EXP)]
                for a in range(CH):
                    mm = pe.matmul(o, xrT[:, u, a, :], gate_sb[:, a, :], start=(a == 0), stop=(a == CH - 1))
                mm.then_inc(l_ps, 1)

            group(0)
            with t_.Fori(1, NG) as gi:
                group(gi)
            t_.wait_ge(oh_ok, 1)
            ohf = oh[:].rearrange("p b e -> p (b e)")
            pe.matmul(p_in[:, 0:NBLK * EXP], triu[:], ohf, start=True, stop=True).then_inc(cum, 1)
            pe.matmul(p_to[:, 0:NBLK * EXP], ones[:], ohf, start=True, stop=True).then_inc(cum, 1)


def experts(nc, sb, ps, sem, g):
    slots, ident, out, fb1_sb = g["slots"], g["ident"], g["out"], g["fb1_sb"]
    w1, w2, fb2, dma_fb, dma_out = g["w1"], g["w2"], g["fb2"], g["dma_fb"], g["dma_out"]
    pads = g["pads"]
    LASTR = CAP - (RT - 1) * P
    CAPE = -(-CAP // 2) * 2
    NH = (-(-CAPE // 4) * 2, CAPE - -(-CAPE // 4) * 2)
    with ExitStack() as st:
        w1raw = sb("w1raw", [P, CH, F], st=st)
        w2raw = sb("w2raw", [P, FT, C], st=st)
        w1h, w1l = sb("w1h", [P, CH, F], F32R, st), sb("w1l", [P, CH, F], F32R, st)
        w2h, w2l = sb("w2h", [P, FT, C], F32R, st), sb("w2l", [P, FT, C], F32R, st)
        rows = sb("rows", [P, 2, RT, ROW], st=st)
        fb2_b = sb("fb2_b", [P, EXP, C], st=st)
        xe = sb("xe", [P, 2, C], st=st)
        bTh, bTl = sb("bTh", [P, CH, CAPE], F32R, st), sb("bTl", [P, CH, CAPE], F32R, st)
        hbuf = sb("hbuf", [P, 2, CAPE], st=st)
        hTh, hTl = sb("hTh", [P, FT, RT * P], F32R, st), sb("hTl", [P, FT, RT * P], F32R, st)
        yb, yv = sb("yb", [P, 2, C], st=st), sb("yv", [P, 2, C], st=st)
        finite = sb("finite", [P, 2, C], I32, st)
        low, big = sb("low", [P, 2, C], st=st), sb("big", [P, 2, C], st=st)
        total = sb("total", [P, 2, C], st=st)
        oo = sb("oo", [P, 2, C], st=st)
        p_f = [ps(f"e_f{i}", [P, 512], st) for i in range(4)]
        p_y = [ps(f"e_y{i}", [P, 512], st) for i in range(2)]
        p_t = [ps(f"e_t{i}", [P, 4, P], st) for i in range(2)]
        d_w1, d_w2 = sem("d_w1", st), sem("d_w2", st)
        d_r = [sem(f"d_r{i}", st) for i in range(2)]
        d_b, sent = sem("d_b", st), [sem(f"e_sent{i}", st) for i in range(2)]
        (xe_ok, tr_ok, bh_ok, bl_ok, f1_ps, r_ok, hi_ok, lo_ok, f2_ps, yb_ok, y_ok, pool_st, inf_ok, fin_ok, o_ok,
         w1h_ok, w1l_ok, w2h_ok, w2l_ok) = (sem("e_" + n, st) for n in (
            "xe", "tr", "bh", "bl", "f1", "r", "hi", "lo", "f2", "yb", "y", "pool", "inf", "fin", "o", "w1h", "w1l",
            "w2h", "w2l"))
        block = st.enter_context(nc.Block())

        def nrows(t):
            return P if t < RT - 1 else LASTR

        def all_experts(eng, expert):
            for e in range(2):
                expert(e, e, True)
            with eng.Fori(1, EXP // 2 - 1) as it:
                for u in range(2):
                    expert(it * 2 + u, u, True)
            expert(EXP - 2, 0, True)
            expert(EXP - 1, 1, False)

        def wait_rows(eng, e, u):
            if isinstance(e, int):
                eng.wait_ge(d_r[u], (e // 2 + 1) * 32)
            else:
                eng.wait_ge(d_r[u], (e - u) * 16 + 32)

        def load_rows(sp, e, u):
            sp.dma_start(rows[:, u, 0:RT - 1, :],
                         slots[bass.ds(e * CAP, (RT - 1) * P), :].rearrange("(t p) c -> p t c", p=P)
                         ).then_inc(d_r[u], 16)
            sp.dma_start(rows[0:LASTR, u, RT - 1, :], slots[bass.ds(e * CAP + (RT - 1) * P, LASTR), :]
                         ).then_inc(d_r[u], 16)

        def load_w1(sp, e):
            sp.dma_start(w1raw[:], w1[bass.ds(e, 1)].rearrange("e (k p) f -> p (e k) f", p=P)).then_inc(d_w1, 16)

        def load_w2(sp, e):
            sp.dma_start(w2raw[:], w2[bass.ds(e, 1)].rearrange("e (j p) c -> p (e j) c", p=P)).then_inc(d_w2, 16)

        @block.sync
        def _(sp):
            load_rows(sp, 0, 0)
            load_w1(sp, 0)
            load_w2(sp, 0)
            load_rows(sp, 1, 1)
            sp.dma_start(fb2_b[:].rearrange("p e c -> p (e c)"),
                         fb2.rearrange("(a e) c -> a (e c)", a=1).broadcast_to([P, EXP * C])).then_inc(d_b, 16)

            def expert(e, u, more):
                if more:
                    sp.wait_ge(w1l_ok, e + 1)
                    load_w1(sp, e + 1)
                    sp.wait_ge(w2l_ok, e + 1)
                    load_w2(sp, e + 1)
                if more and not (isinstance(e, int) and e == EXP - 2):
                    for q in range(2):
                        sp.wait_ge(sent[q], (e * (RT // 2) + RT // 2) * 16)
                    load_rows(sp, e + 2, u)

            all_experts(sp, expert)

        @block.gpsimd
        def _(pool):
            if CAPE > CAP:
                nc.gpsimd.memset(bTh[:, :, CAP:CAPE].bitcast(F32), 0.0).then_inc(pads, 1)
                nc.gpsimd.memset(bTl[:, :, CAP:CAPE].bitcast(F32), 0.0).then_inc(pads, 1)
            nc.gpsimd.memset(hTh[:, :, CAPE:RT * P].bitcast(F32), 0.0).then_inc(pads, 1)
            nc.gpsimd.memset(hTl[:, :, CAPE:RT * P].bitcast(F32), 0.0).then_inc(pads, 1)
            pool.wait_ge(dma_out, 16)

            def expert(e, u, more):
                def store(t):
                    r = nrows(t)
                    wait_apart(pool, o_ok, e * RT + t + 1, dma_out, 16)
                    nc.gpsimd.indirect_dma_start(
                        out, bass.IndirectOffsetOnAxis(rows[0:r, u, t, C + 3:C + 4].bitcast(I32), 0),
                        oo[0:r, t % 2, :], None, bounds_check=N - 1, oob_is_err=False).then_inc(sent[t % 2], 16)

                for t in range(RT):
                    r = nrows(t)
                    T = e * RT + t
                    wait_apart(pool, inf_ok, T * 2 + 2, dma_out, 16)
                    nc.gpsimd.tensor_tensor(low[0:r, t % 2, :], low[0:r, t % 2, :], big[0:r, t % 2, :], ALU.add
                                            ).then_inc(pool_st, 1)
                    pool.wait_ge(pool_st, T * 2 + 1)
                    wait(pool, sent[t % 2], (e * (RT // 2) + t // 2) * 16)
                    nc.gpsimd.tensor_tensor(oo[0:r, t % 2, :], low[0:r, t % 2, :], rows[0:r, u, t, 0:C], ALU.add
                                            ).then_inc(pool_st, 1)
                    if t > 0:
                        store(t - 1)
                store(RT - 1)

            all_experts(pool, expert)
            for q in range(2):
                pool.wait_ge(sent[q], 16 * EXP * RT // 2)

        @block.scalar
        def _(s):
            s.wait_ge(dma_fb, 16)

            def normalise(e, u, t):
                r = nrows(t)
                if t == 0:
                    wait_rows(s, e, u)
                wait(s, tr_ok, e * RT + t - 1)
                nc.scalar.activation(xe[0:r, t % 2, :], rows[0:r, u, t, 0:C], ACT.Identity,
                                     scale=rows[0:r, u, t, C + 1:C + 2], bias=rows[0:r, u, t, C:C + 1]
                                     ).then_inc(xe_ok, 1)

            def high_rows(e, t):
                r = nrows(t)
                s.wait_ge(tr_ok, e * RT + t + 1)
                nc.scalar.copy(bTh[:, :, t * P:t * P + r], p_t[t % 2][:, 0:CH, 0:r]).then_inc(bh_ok, 1)

            def high_w1(e):
                s.wait_ge(d_w1, e * 16 + 16)
                nc.scalar.copy(w1h[:], w1raw[:]).then_inc(w1h_ok, 1)

            def expert(e, u, more):
                for j in range(FT):
                    for h in range(2):
                        wait_apart(s, f1_ps, e * 2 * FT + 2 * j + h + 1, dma_fb, 16)
                        wait_apart(s, lo_ok, e * FT + j - 1, dma_fb, 16)
                        nc.scalar.activation(hbuf[:, j % 2, h * NH[0]:h * NH[0] + NH[h]],
                                             p_f[(2 * j + h) % 4][:, 0:NH[h]], ACT.Relu,
                                             bias=fb1_sb[:, bass.ds(e, 1), j]).then_inc(r_ok, 1)
                    if j == 3:
                        s.wait_ge(d_w2, e * 16 + 16)
                        wait(s, f2_ps, e * RT)
                        nc.scalar.copy(w2h[:], w2raw[:]).then_inc(w2h_ok, 1)
                if more:
                    normalise(e + 1, 1 - u, 0)
                for t in range(RT):
                    r = nrows(t)
                    if more:
                        high_rows(e + 1, t)
                        if t + 1 < RT:
                            normalise(e + 1, 1 - u, t + 1)
                    s.wait_ge(yb_ok, e * RT + t + 1)
                    wait(s, o_ok, e * RT + t - 1)
                    nc.scalar.activation(yv[0:r, t % 2, :], yb[0:r, t % 2, :], ACT.Identity,
                                         scale=rows[0:r, u, t, C + 2:C + 3]).then_inc(y_ok, 1)
                    if more and t == 3:
                        high_w1(e + 1)

            for t in range(RT):
                normalise(0, 0, t)
                if t > 0:
                    high_rows(0, t - 1)
            high_rows(0, RT - 1)
            high_w1(0)
            all_experts(s, expert)

        @block.tensor
        def _(t_):
            pe = nc.tensor

            def transposes(e, t):
                r = nrows(t)
                t_.wait_ge(xe_ok, e * RT + t + 1)
                wait(t_, bl_ok, e * RT + t - 1)
                for a in range(CH):
                    mm = pe.transpose(p_t[t % 2][:, a, 0:r], xe[0:r, t % 2, a * P:(a + 1) * P],
                                      ident[0:r, 0:r])
                mm.then_inc(tr_ok, 1)

            def expert(e, u, more):
                t_.wait_ge(w1l_ok, e + 1)
                for j in range(FT):
                    for h in range(2):
                        c = 2 * j + h
                        if j == 0:
                            t_.wait_ge(bl_ok, e * RT + (-(-NH[0] // P), RT)[h])
                        wait(t_, r_ok, e * 2 * FT + c - 3)
                        parts = [(w, b, a) for a in range(CH) for w, b in ((w1h, bTh), (w1h, bTl), (w1l, bTh))]
                        for q, (w, b, a) in enumerate(parts):
                            mm = pe.matmul(p_f[c % 4][:, 0:NH[h]], w[:, a, j * P:(j + 1) * P],
                                           b[:, a, h * NH[0]:h * NH[0] + NH[h]], start=(q == 0),
                                           stop=(q == len(parts) - 1))
                        mm.then_inc(f1_ps, 1)
                t_.wait_ge(w2l_ok, e + 1)
                for t in range(RT):
                    if more:
                        transposes(e + 1, t)
                    wait(t_, yb_ok, e * RT + t - 1)
                    parts = [(h, w, j) for j in range(FT) for h, w in ((hTh, w2h), (hTh, w2l), (hTl, w2h))]
                    for q, (h, w, j) in enumerate(parts):
                        if t == 0 and q % 3 == 0:
                            t_.wait_ge(lo_ok, e * FT + j + 1)
                        mm = pe.matmul(p_y[t % 2][:, 0:C], h[:, j, t * P:(t + 1) * P], w[:, j, :],
                                       start=(q == 0), stop=(q == len(parts) - 1))
                    mm.then_inc(f2_ps, 1)

            for t in range(RT):
                transposes(0, t)
            t_.wait_ge(pads, 4 if CAPE > CAP else 2)
            all_experts(t_, expert)

        @block.vector
        def _(v):
            V = nc.vector
            v.wait_ge(dma_fb, 16)
            v.wait_ge(d_b, 16)

            def low_rows(e, t):
                r = nrows(t)
                v.wait_ge(bh_ok, e * RT + t + 1)
                V.tensor_tensor(bTl[:, :, t * P:t * P + r], p_t[t % 2][:, 0:CH, 0:r],
                                bTh[:, :, t * P:t * P + r].bitcast(F32), ALU.subtract).then_inc(bl_ok, 1)

            def low_w1(e):
                v.wait_ge(w1h_ok, e + 1)
                V.tensor_tensor(w1l[:], w1raw[:], w1h[:].bitcast(F32), ALU.subtract).then_inc(w1l_ok, 1)

            def expert(e, u, more):
                for j in range(FT):
                    v.wait_ge(r_ok, e * 2 * FT + 2 * j + 2)
                    wait(v, f2_ps, e * RT)
                    V.tensor_copy(hTh[:, j, 0:CAPE], hbuf[:, j % 2, :]).then_inc(hi_ok, 1)
                    v.wait_ge(hi_ok, e * FT + j + 1)
                    V.tensor_tensor(hTl[:, j, 0:CAPE], hbuf[:, j % 2, :], hTh[:, j, 0:CAPE].bitcast(F32),
                                    ALU.subtract).then_inc(lo_ok, 1)
                    if j == 4:
                        v.wait_ge(w2h_ok, e + 1)
                        V.tensor_tensor(w2l[:], w2raw[:], w2h[:].bitcast(F32), ALU.subtract).then_inc(w2l_ok, 1)

                def result(t):
                    r = nrows(t)
                    T = e * RT + t
                    v.wait_ge(y_ok, T + 1)
                    y = yv[0:r, t % 2, :]
                    V.tensor_scalar(low[0:r, t % 2, :], y, -FLT_MAX, -1e4, ALU.is_lt, ALU.mult).then_inc(inf_ok, 1)
                    V.tensor_scalar(big[0:r, t % 2, :], y, FLT_MAX, 1e4, ALU.is_gt, ALU.mult).then_inc(inf_ok, 1)
                    V.tensor_scalar(finite[0:r, t % 2, :], yv[0:r, t % 2, :], 0.0, 0.0, ALU.mult, ALU.is_equal
                                    ).then_inc(fin_ok, 1)
                    V.tensor_tensor(total[0:r, t % 2, :], yv[0:r, t % 2, :], rows[0:r, u, t, 0:C], ALU.add
                                    ).then_inc(fin_ok, 1)
                    if isinstance(T, int):
                        v.wait_ge(fin_ok, T * 2 + 2)
                        v.wait_ge(pool_st, T * 2 + 2)
                    else:
                        both = v.to_reg(T * 2 + 2)
                        v.wait_ge(dma_fb, 16)
                        v.wait_ge(fin_ok, both)
                        v.wait_ge(pool_st, both)
                    V.copy_predicated(oo[0:r, t % 2, :], finite[0:r, t % 2, :], total[0:r, t % 2, :]
                                      ).then_inc(o_ok, 1)

                for t in range(RT):
                    r = nrows(t)
                    if more:
                        low_rows(e + 1, t)
                    v.wait_ge(f2_ps, e * RT + t + 1)
                    wait(v, y_ok, e * RT + t - 1)
                    V.tensor_tensor(yb[0:r, t % 2, :], p_y[t % 2][0:r, 0:C],
                                    fb2_b[0:r, bass.ds(e, 1), :].rearrange("p a c -> p (a c)"), ALU.add
                                    ).then_inc(yb_ok, 1)
                    if t > 0:
                        result(t - 1)
                    if more and t == 5:
                        low_w1(e + 1)
                result(RT - 1)

            for t in range(RT):
                low_rows(0, t)
            low_w1(0)
            all_experts(v, expert)


_OUT = "out_dram"


def kernel(**inputs):
    import concourse.bacc as bacc
    from concourse.bass_utils import run_bass_kernel_spmd as run

    nc = bacc.Bacc("TRN2", target_bir_lowering=False, num_devices=1)
    a = {k: np.asarray(v) for k, v in inputs.items()}

    def padded(v, n, fill):
        w = np.full((n,) + v.shape[1:], fill, v.dtype)
        w[:v.shape[0]] = v
        return w

    given = {
        "x": padded(a["x"], NPAD, 0),
        "srcR": padded(a["src"], EPAD + P, 0).reshape(-1, P),
        "dstR": padded(a["dst"], EPAD + P, PAD_DST).reshape(-1, P),
        "dstF": padded(a["dst"], EPAD + P, PAD_DST)[::P],
        "gW": a["L0_gnn_W"], "gb": a["L0_gnn_b"],
        "WqkvT": a["L0_mix_Wqkv"].T, "ln1g": a["L0_mix_ln1_g"], "ln1b": a["L0_mix_ln1_b"],
        "W1T": a["L0_mix_W1"].T, "b1": a["L0_mix_b1"], "W2T": a["L0_mix_W2"].T, "b2": a["L0_mix_b2"],
        "ln2g": a["L0_mix_ln2_g"], "ln2b": a["L0_mix_ln2_b"],
        "gateW": a["L0_ffn_gate_w"], "gateb": a["L0_ffn_gate_b"],
        "w1": a["L0_ffn_w1"], "fb1": a["L0_ffn_b1"].reshape(EXP, FT, P).transpose(2, 0, 1), "w2": a["L0_ffn_w2"], "fb2": a["L0_ffn_b2"],
    }
    arrays, args = {}, []
    for k, v in given.items():
        arrays["in_" + k] = np.ascontiguousarray(v)
        args.append(nc.dram_tensor("in_" + k, v.shape, mybir.dt.from_np(v.dtype), kind="ExternalInput").ap())
    out = nc.dram_tensor(_OUT, (NPAD, C), F32, kind="ExternalOutput").ap()
    build(nc, *args, out)
    r = run(nc, [arrays], core_ids=[0])
    return r.results[0][_OUT][:N]
```

```python
from contextlib import ExitStack

import numpy as np

import concourse.bass as bass
from concourse import mybir

ALU = mybir.AluOpType
ACT = mybir.ActivationFunctionType
F32 = mybir.dt.float32
F32R = mybir.dt.float32r
BF16 = mybir.dt.bfloat16
I32 = mybir.dt.int32
I16 = mybir.dt.int16
AX = mybir.AxisListType

P = 128
N = 6250
C = 256
CH = C // P
E = 200000
NBLK = -(-N // P)
NPAD = NBLK * P
NCHUNK = -(-E // P)
NT = -(-NCHUNK // P)
EPAD = NT * P * P
PAD_DST = 1 << 20
PER = 21
NPASS = -(-(NCHUNK + NBLK - 1) // PER)
NITEM = NPASS * PER
KVB = 4
NKV = -(-NBLK // KVB)
assert NKV + NBLK < NPASS
assert NITEM >= NCHUNK + NBLK - 1 and NITEM <= NT * P
RING = PER
GRP = 7
TRI = 3
LAG = 4
PSLOT = 3
H, DH = 8, C // 8
EXP = 8
F = 1024
CAP = -(-5 * N // (4 * EXP))
SLOTS = EXP * CAP
ROW = C + 4
NOWHERE = 1 << 17
EPS = 1e-5
EPS_ATTN = 1e-6
FT = F // P
RGR = 7
NOUT = NBLK // RGR
RT = -(-CAP // P)
FLT_MAX = 3.4028234e38
LAST = N - (NBLK - 1) * P


def wait(eng, sem, value):
    if isinstance(value, int) and value <= 0:
        return
    eng.wait_ge(sem, value)


def wait_apart(eng, sem, value, long_sem, long_value):
    if isinstance(value, int):
        if value > 0:
            eng.wait_ge(sem, value)
        return
    value = eng.to_reg(value)
    eng.wait_ge(long_sem, long_value)
    eng.wait_ge(sem, value)


def build(nc, x, srcR, dstR, dstF, gW, gb, WqkvT, ln1g, ln1b, W1T, b1, W2T, b2, ln2g, ln2b, gateW, gateb,
          w1, fb1, w2, fb2, out):
    table = nc.dram_tensor("node_rows", (NPAD, C), F32, kind="Internal").ap()
    slots = nc.dram_tensor("expert_rows", (SLOTS, ROW), F32, kind="Internal").ap()

    with ExitStack() as top:
        names = {}

        def sb(name, shape, dt=F32, st=top):
            return st.enter_context(nc.sbuf_tensor(name, shape, dt))

        def ps(name, shape, st):
            return st.enter_context(nc.psum_tensor(name, shape, F32))

        def sem(name, st=top):
            return st.enter_context(nc.semaphore(name))

        ident = sb("ident", [P, P])
        col = sb("col", [P, P])
        eps_ln = sb("eps_ln", [P, 1])
        fb1_sb = sb("fb1_sb", [P, EXP, FT])
        dma_fb = sem("dma_fb")
        dma_empty = sem("dma_empty")
        dma_out = sem("dma_out")
        pads = sem("pads")
        consts = sem("consts")

        with ExitStack() as mid:
            acc = sb("acc", [P, NBLK, ROW], st=mid)
            res = sb("res", [P, NBLK, C], st=mid)
            src_item = sb("src_item", [P, NT * P], I32, st=mid)
            dst_item = sb("dst_item", [P, NT * P], st=mid)
            blk_item = sb("blk_item", [1, LAG + NT * P], I16, st=mid)
            rstd = sb("rstd", [P, NBLK], st=mid)
            nmr = sb("nmr", [P, NBLK], st=mid)
            dinv = sb("dinv", [P, NBLK], st=mid)
            kvz = sb("kvz", [P, CH, P + P // DH], st=mid)
            headmask = sb("headmask", [P, P], st=mid)
            w1t_sb = sb("w1t_sb", [P, CH, C], st=mid)
            w2t_sb = sb("w2t_sb", [P, CH, C], st=mid)
            wq_sb = sb("wq_sb", [P, CH, 3 * C], st=mid)
            bias_b = {k: sb("bc_" + k, [P, C], st=mid) for k in ("gb", "ln2g", "ln2b")}
            b2row = sb("b2row", [1, C], st=mid)
            ones_row = sb("ones_row", [1, P], st=mid)
            cols = {k: sb("col_" + k, [P, CH], st=mid) for k in ("b1", "ln1g", "ln1b")}
            gate_sb = sb("gate_sb", [P, CH, EXP], st=mid)
            gateb_b = sb("gateb_b", [P, EXP], st=mid)
            v1 = sb("v1", [P, 2, CH, P + 2], st=mid)
            dma_w = sem("dma_w", mid)

            prepare(nc, mid, sb, ps, sem, locals())
            aggregate_and_mix(nc, sb, ps, sem, locals())
            route(nc, sb, ps, sem, locals())
        experts(nc, sb, ps, sem, locals())


def rsqrt_steps(nc, link, out, var, tmp, eps):
    link(nc.vector.scalar_tensor_tensor(tmp, var, eps, out, ALU.add, ALU.mult))
    link(nc.vector.scalar_tensor_tensor(tmp, tmp, -0.5, out, ALU.mult, ALU.mult))
    link(nc.vector.scalar_tensor_tensor(out, tmp, 1.5, out, ALU.add, ALU.mult))


def prepare(nc, mid, sb, ps, sem, g):
    (x, srcR, dstR, dstF, table, acc, res, src_item, dst_item, blk_item, rstd, nmr, dinv, headmask, ident,
     col, eps_ln, wq_sb, w1t_sb, w2t_sb, dma_w, consts, v1) = (g[k] for k in (
        "x", "srcR", "dstR", "dstF", "table", "acc", "res", "src_item", "dst_item", "blk_item", "rstd", "nmr",
        "dinv", "headmask", "ident", "col", "eps_ln", "wq_sb", "w1t_sb", "w2t_sb", "dma_w", "consts", "v1"))
    GR = 7
    NG = NBLK // GR
    SG = 6
    NRAW = SG * GR - 2
    CG = 4
    assert NG * GR == NBLK
    with ExitStack() as st:
        src_rows = sb("src_rows", [P, NT, P], I32, st)
        dst_rows = sb("dst_rows", [P, NT, P], I32, st)
        first = sb("first", [P, NT], I32, st)
        next_first = sb("next_first", [P, NT], I32, st)
        gw_sb = sb("gw_sb", [P, CH, C], st=st)
        blk_i = sb("blk_i", [P, 3, NT], I32, st)
        code_f = sb("code_f", [P, 2, NT], st=st)
        key = sb("key", [P, 2, NT], st=st)
        col256 = sb("col256", [P, 2 * P], st=st)
        col128x = sb("col128x", [P, P], st=st)
        part = sb("part", [P, 1], st=st)
        chunk0 = sb("chunk0", [P, NT], st=st)
        chunkn = sb("chunkn", [P, NT], st=st)
        node_n = sb("node_n", [P, NBLK], st=st)
        band_m = sb("band_m", [P, 2, 2 * P], BF16, st)
        bandf = sb("bandf", [P, 4, 2 * P], st=st)
        rowf = sb("rowf", [P, 4, 2, P], st=st)
        brow = sb("brow", [1, 2, P], st=st)
        one_lo = sb("one_lo", [P, NT, P], BF16, st)
        one_hi = sb("one_hi", [P, NT, NBLK], BF16, st)
        below = sb("below", [P, P], st=st)
        ones = sb("ones_p", [P, P], st=st)
        next_p = sb("next_p", [P, P], st=st)
        wrap_p = sb("wrap_p", [P, P], st=st)
        firsts = sb("firsts", [P, NBLK], st=st)
        block_n = sb("block_n", [NBLK, P], st=st)
        chunk_f = sb("chunk_f", [P, NBLK], st=st)
        chunk_i = sb("chunk_i", [P, NBLK], I32, st)
        crow = sb("crow", [P, CG * GR, P], I32, st)
        less = sb("less", [P, GR, P], BF16, st)
        place = sb("place", [P, NBLK + 1], st=st)
        stats = sb("stats", [P, 2, 6], st=st)
        mv = sb("mv", [P, NBLK, 2], st=st)
        tmp = sb("tmp", [P, NBLK], st=st)
        deg = sb("deg", [P, NBLK], st=st)
        count = sb("count", [P, NBLK], st=st)
        xn = sb("xn", [P, GR, C], st=st)
        xnT = sb("xnT", [P, GR, CH, P], st=st)

        p_it0 = ps("p_it", [P, 4, P], st)
        p_row0 = ps("p_row", [P, 512], st)
        p_deg = ps("p_deg", [P, 512], st)
        p_blk = ps("p_blk", [P, 512], st)
        p_it = [p_it0, p_deg[:].rearrange("p (a c) -> p a c", c=P)]
        p_row = [p_row0, p_blk]
        p_tr = [ps(f"p_tr{i}", [P, 4, P], st) for i in range(2)]
        p_h = [ps(f"p_h{i}", [P, 512], st) for i in range(2)]

        dma_first, dma_rows, dma_gw = sem("dma_first", st), sem("dma_rows", st), sem("dma_gw", st)
        dma_x = [sem(f"dma_x{i}", st) for i in range(NG)]
        dma_crow = [sem(f"dma_crow{i}", st) for i in range(NG)]
        dma_tab = sem("dma_tab", st)
        onehots, hist, hist_sb, blk_ps, blk_sb, less_ps, chunk_ok, place_ok, shifted = (
            sem(n, st) for n in ("onehots", "hist", "hist_sb", "blk_ps", "blk_sb", "less_ps", "chunk_ok",
                                 "place_ok", "shifted"))
        bands, rows_ok = sem("bands", st), sem("rows_ok", st)
        item_ps = sem("item_ps", st)
        items = sem("items", st)
        stat = sem("stat", st)
        dve = sem("dve1", st)
        std_ok, rstd_ok = sem("std_ok", st), sem("rstd_ok", st)
        xn_ok, tr_ok, xnT_ok = sem("xn_ok", st), sem("tr_ok", st), sem("xnT_ok", st)
        h_ok, h_out = sem("h_ok", st), sem("h_out", st)
        deg_ok, deg_std, dinv_ok, scaled = (sem(n, st) for n in ("deg_ok", "deg_std", "dinv_ok", "scaled"))
        compared = sem("compared", st)
        block = st.enter_context(nc.Block())
        cuts = [0, 2 * GR, 4 * GR, NRAW]

        @block.sync
        def _(sp):
            with nc.allow_non_contiguous_dma("first destination of every chunk"):
                sp.dma_start(first[:], dstF[0:NT * P].rearrange("(t p) -> p t", p=P)).then_inc(dma_first, 16)
                sp.dma_start(next_first[:], dstF[1:NT * P + 1].rearrange("(t p) -> p t", p=P)
                             ).then_inc(dma_first, 16)
            for i in range(NG):
                sp.dma_start(res[:, i * GR:(i + 1) * GR, :],
                             x[i * GR * P:(i + 1) * GR * P, :].rearrange("(b p) c -> p b c", p=P)
                             ).then_inc(dma_x[i], 16)
                if i == 0:
                    sp.dma_start(gw_sb[:], g["gW"].rearrange("(k p) c -> p k c", p=P)).then_inc(dma_gw, 16)
            sp.dma_start(dst_rows[:], dstR[0:NT * P, :].rearrange("(t p) e -> p t e", p=P)).then_inc(dma_rows, 16)
            sp.dma_start(src_rows[:], srcR[0:NT * P, :].rearrange("(t p) e -> p t e", p=P)).then_inc(dma_rows, 16)
            sp.dma_start(wq_sb[:], g["WqkvT"].rearrange("(k p) c -> p k c", p=P)).then_inc(dma_w, 16)
            sp.dma_start(w1t_sb[:], g["W1T"].rearrange("(k p) c -> p k c", p=P)).then_inc(dma_w, 16)
            sp.dma_start(w2t_sb[:], g["W2T"].rearrange("(k p) c -> p k c", p=P)).then_inc(dma_w, 16)
            sp.dma_start(g["gate_sb"][:], g["gateW"].rearrange("(k p) c -> p k c", p=P)).then_inc(dma_w, 16)
            for k, v in (("gb", g["gb"]), ("ln2g", g["ln2g"]), ("ln2b", g["ln2b"])):
                sp.dma_start(g["bias_b"][k][:], v.rearrange("(a c) -> a c", a=1).broadcast_to([P, C])
                             ).then_inc(dma_w, 16)
            sp.dma_start(g["gateb_b"][:], g["gateb"].rearrange("(a c) -> a c", a=1).broadcast_to([P, EXP])
                         ).then_inc(dma_w, 16)
            sp.dma_start(g["b2row"][:], g["b2"].rearrange("(a c) -> a c", a=1)).then_inc(dma_w, 16)
            with nc.allow_non_contiguous_dma("small per-feature columns"):
                for k in ("b1", "ln1g", "ln1b"):
                    sp.dma_start(g["cols"][k][:], g[k].rearrange("(k p) -> p k", p=P)).then_inc(dma_w, 16)

            def to_table(lo, hi):
                sp.dma_start(table[lo * P:hi * P, :].rearrange("(b p) c -> p b c", p=P), acc[:, lo:hi, 0:C]
                             ).then_inc(dma_tab, 16)

            for lo, hi in zip(cuts, cuts[1:]):
                sp.wait_ge(scaled, hi)
                to_table(lo, hi)
            sp.wait_ge(h_out, NBLK)
            to_table(NRAW, NBLK)
            sp.wait_ge(dma_tab, 16 * len(cuts))

        @block.gpsimd
        def _(pool):
            nc.gpsimd.iota(col[:], [[1, P]], 0, 0, allow_small_or_imprecise_dtypes=True).then_inc(consts, 1)
            nc.gpsimd.memset(below[:], 1.0).then_inc(consts, 1)
            nc.gpsimd.memset(ones[:], 1.0).then_inc(consts, 1)
            nc.gpsimd.memset(eps_ln[:], EPS).then_inc(consts, 1)
            nc.gpsimd.memset(ident[:], 0.0).then_inc(consts, 1)
            pool.wait_ge(consts, 5)
            nc.gpsimd.affine_select(below[:], below[:], [[1, P]], ALU.is_gt, 0.0, 0, -1).then_inc(consts, 1)
            nc.gpsimd.affine_select(ident[:], ident[:], [[-1, P]], ALU.not_equal, 1.0, 0, 1).then_inc(consts, 1)
            nc.gpsimd.iota(node_n[:], [[P, NBLK]], 0, 1, allow_small_or_imprecise_dtypes=True).then_inc(consts, 1)
            nc.gpsimd.iota(col256[:], [[1, 2 * P]], 0, 0, allow_small_or_imprecise_dtypes=True).then_inc(consts, 1)
            nc.gpsimd.iota(col128x[:], [[P, P]], 0, 0, allow_small_or_imprecise_dtypes=True).then_inc(consts, 1)
            nc.gpsimd.iota(part[:], [[0, 1]], 0, 1, allow_small_or_imprecise_dtypes=True).then_inc(consts, 1)
            nc.gpsimd.iota(chunk0[:], [[P * P, NT]], 0, P, allow_small_or_imprecise_dtypes=True).then_inc(consts, 1)
            nc.gpsimd.iota(chunkn[:], [[P, NT]], 0, 1, allow_small_or_imprecise_dtypes=True).then_inc(consts, 1)
            nc.gpsimd.memset(next_p[:], 0.0).then_inc(consts, 1)
            nc.gpsimd.memset(wrap_p[:], 0.0).then_inc(consts, 1)
            nc.gpsimd.memset(place[:], float(E)).then_inc(consts, 1)
            pool.wait_ge(chunk_ok, 1)
            for b in range(NBLK):
                if b % GR == 0 and b >= CG * GR:
                    pool.wait_ge(compared, b // GR - CG + 1)
                nc.gpsimd.indirect_dma_start(crow[:, b % (CG * GR), :], None, dstR,
                                             bass.IndirectOffsetOnAxis(chunk_i[:, b:b + 1], 0)
                                             ).then_inc(dma_crow[b // GR], 16)
                if b == GR:
                    pool.wait_ge(consts, 16)
                    nc.gpsimd.affine_select(next_p[:], next_p[:], [[-1, P]], ALU.not_equal, 1.0, -1, 1
                                            ).then_inc(consts, 1)
                    nc.gpsimd.affine_select(wrap_p[:], wrap_p[:], [[1, P]], ALU.not_equal, 1.0, 1 - P, -1
                                            ).then_inc(consts, 1)
                    nc.gpsimd.memset(headmask[:], 1.0).then_inc(consts, 1)
                    nc.gpsimd.memset(v1[:], 1.0).then_inc(consts, 1)
                    nc.gpsimd.memset(g["ones_row"][:], 1.0).then_inc(consts, 1)
                    nc.gpsimd.memset(blk_item[:], 0).then_inc(consts, 1)
                    pool.wait_ge(consts, 22)
                    hm = headmask[:].rearrange("p (h d) -> p h d", d=DH)
                    nc.gpsimd.affine_select(hm, hm, [[-DH, P // DH], [0, DH]], ALU.is_ge, 0.0, 0, 1
                                            ).then_inc(consts, 1)
                    pool.wait_ge(consts, 23)
                    nc.gpsimd.affine_select(hm, hm, [[DH, P // DH], [0, DH]], ALU.is_ge, 0.0, DH - 1, -1
                                            ).then_inc(consts, 1)

        @block.vector
        def _(v):
            n = [0]
            V = nc.vector

            def link(ins):
                n[0] += 1
                ins.then_inc(dve, 1)
                v.wait_ge(dve, n[0])

            def over_p(a, k):
                return a.rearrange("p (t e) -> p t e", e=1).broadcast_to([P, NT, k])

            v.wait_ge(consts, 9)
            v.wait_ge(dma_first, 32)
            link(V.tensor_scalar(blk_i[:, 0, :], first[:], 7, None, ALU.arith_shift_right))
            link(V.tensor_scalar(blk_i[:, 2, :], first[:], P - 1, None, ALU.bitwise_and))
            link(V.tensor_copy(code_f[:, 0, :], blk_i[:, 0, :]))
            link(V.tensor_copy(code_f[:, 1, :], blk_i[:, 2, :]))
            colb = col[:].rearrange("p (t e) -> p t e", t=1)
            V.tensor_tensor(one_lo[:], colb.broadcast_to([P, NT, P]), over_p(code_f[:, 1, :], P), ALU.is_equal
                            ).then_inc(onehots, 1)
            V.tensor_tensor(one_hi[:], colb[:, :, 0:NBLK].broadcast_to([P, NT, NBLK]),
                            over_p(code_f[:, 0, :], NBLK), ALU.is_equal).then_inc(onehots, 1)
            v.wait_ge(hist, 1)
            V.tensor_copy(firsts[:], p_deg[:, 0:NBLK]).then_inc(hist_sb, 1)
            v.wait_ge(blk_ps, 1)
            V.tensor_copy(block_n[:], p_blk[0:NBLK, 0:P]).then_inc(blk_sb, 1)
            v.wait_ge(less_ps, 1)
            link(V.tensor_scalar(chunk_f[:], p_deg[:, 0:NBLK], -1.0, 0.0, ALU.add, ALU.max))
            V.tensor_copy(chunk_i[:], chunk_f[:]).then_inc(chunk_ok, 1)

            def means(gi):
                v.wait_ge(dma_x[gi], 16)
                for b in range(gi * GR, gi * GR + GR):
                    link(V.bn_stats(stats[:, b % 2, :], res[:, b, :]))
                    V.bn_aggr(mv[:, b, :], stats[:, b % 2, :]).then_inc(stat, 1)

            def inverse_std(gi):
                w = slice(gi * GR, gi * GR + GR)
                v.wait_ge(stat, gi * GR + GR)
                v.wait_ge(std_ok, gi + 1)
                link(V.reciprocal(rstd[:, w], rstd[:, w]))
                rsqrt_steps(nc, link, rstd[:, w], mv[:, w, 1], tmp[:, w], EPS)
                V.scalar_tensor_tensor(nmr[:, w], mv[:, w, 0], -1.0, rstd[:, w], ALU.mult, ALU.mult
                                       ).then_inc(rstd_ok, 1)

            def compare(gi):
                w = slice(gi * GR, gi * GR + GR)
                v.wait_ge(dma_crow[gi], 16 * GR)
                c0 = gi % CG * GR
                link(V.tensor_tensor(less[:], crow[:, c0:c0 + GR, :],
                                     node_n[:, w].rearrange("p (b e) -> p b e", e=1).broadcast_to([P, GR, P]),
                                     ALU.is_lt))
                V.tensor_reduce(count[:, w], less[:], AX.X, ALU.add).then_inc(compared, 1)
                v.wait_ge(compared, gi + 1)

            for gi in range(NG + 1):
                if gi < NG:
                    means(gi)
                if gi > 0:
                    inverse_std(gi - 1)
                if gi >= 2:
                    compare(gi - 2)
            compare(NG - 1)
            v.wait_ge(consts, 24)
            V.scalar_tensor_tensor(place[:, 0:NBLK], chunk_f[:], float(P), count[:], ALU.mult, ALU.add
                                   ).then_inc(place_ok, 1)
            v.wait_ge(place_ok, 1)
            v.wait_ge(shifted, 1)
            V.scalar_tensor_tensor(deg[:], p_deg[:, 0:NBLK], 1.0, place[:, 0:NBLK], ALU.add, ALU.subtract
                                   ).then_inc(deg_ok, 1)
            v.wait_ge(deg_ok, 1)
            v.wait_ge(deg_std, 1)
            link(V.reciprocal(dinv[:], dinv[:]))
            link(V.tensor_tensor(tmp[:], dinv[:], dinv[:], ALU.mult))
            link(V.tensor_tensor(tmp[:], tmp[:], deg[:], ALU.mult))
            link(V.tensor_scalar(tmp[:], tmp[:], -0.5, 1.5, ALU.mult, ALU.add))
            V.tensor_tensor(dinv[:], dinv[:], tmp[:], ALU.mult).then_inc(dinv_ok, 1)
            v.wait_ge(dinv_ok, 1)
            for b in range(NRAW):
                v.wait_ge(h_out, b + 1)
                V.tensor_scalar(acc[:, b, 0:C], acc[:, b, 0:C], dinv[:, b:b + 1], None, ALU.mult
                                ).then_inc(scaled, 1)

            link(V.tensor_scalar(blk_i[:, 1, :], next_first[:], 7, None, ALU.arith_shift_right))
            link(V.memset(blk_i[0:1, 0, 0:1], 0))
            link(V.tensor_scalar(key[:, 0, :], blk_i[:, 0, :], part[:, 0:1], None, ALU.add))
            link(V.tensor_scalar(key[:, 1, :], blk_i[:, 1, :], part[:, 0:1], 1.0, ALU.add, ALU.add))

            def band(t):
                link(V.tensor_scalar(band_m[:, t % 2, :], col256[:], key[:, 1, t:t + 1], None, ALU.is_lt))
                V.scalar_tensor_tensor(bandf[:, t % 4, :], col256[:], key[:, 0, t:t + 1], band_m[:, t % 2, :],
                                       ALU.is_ge, ALU.mult).then_inc(bands, 1)

            band(0)
            band(1)
            for t in range(NT):
                if t + 2 < NT:
                    band(t + 2)
                v.wait_ge(item_ps, t + 1)
                w = slice(t * P, (t + 1) * P)
                V.tensor_copy(src_item[:, w], p_it[t % 2][:, 0, :]).then_inc(items, 1)
                V.scalar_tensor_tensor(dst_item[:, w], p_it[t % 2][:, 1, :], float(t * P * P), col128x[:],
                                       ALU.subtract, ALU.subtract).then_inc(items, 1)
                V.scalar_tensor_tensor(brow[:, t % 2, :], p_row[t % 2][0:1, 0:P], -1.0, col[0:1, :],
                                       ALU.mult, ALU.add).then_inc(items, 1)
                v.wait_ge(items, 3 * t + 3)
                link(V.tensor_scalar(blk_item[0:1, LAG + t * P:LAG + (t + 1) * P], brow[:, t % 2, :],
                                     float(t * P), float(NBLK - 1), ALU.add, ALU.min))

        @block.scalar
        def _(s):
            s.wait_ge(consts, 7)

            def root(gi):
                s.wait_ge(stat, gi * GR + GR)
                w = bass.ds(gi * GR, GR)
                nc.scalar.activation(rstd[:, w], mv[:, w, 1], ACT.Sqrt, bias=eps_ln[:]).then_inc(std_ok, 1)

            def normalise(b, u):
                wait(s, tr_ok, b - GR + 1)
                nc.scalar.activation(xn[:, u, :], res[:, bass.ds(b, 1), :].rearrange("p a c -> p (a c)"),
                                     ACT.Identity, scale=rstd[:, bass.ds(b, 1)], bias=nmr[:, bass.ds(b, 1)]
                                     ).then_inc(xn_ok, 1)

            def copy(b, u):
                s.wait_ge(tr_ok, b + 1)
                wait(s, h_ok, b - GR + 2)
                nc.scalar.copy(xnT[:, u], p_tr[u % 2][:, 0:CH, :]).then_inc(xnT_ok, 1)

            def store(b, u, scale):
                s.wait_ge(h_ok, b + 1)
                o = acc[:, bass.ds(b, 1), 0:C].rearrange("p a c -> p (a c)")
                if scale:
                    nc.scalar.activation(o, p_h[u % 2][:, 0:C], ACT.Copy, scale=dinv[:, bass.ds(b, 1)]
                                         ).then_inc(h_out, 1)
                else:
                    nc.scalar.copy(o, p_h[u % 2][:, 0:C]).then_inc(h_out, 1)

            def group(gi, scale):
                s.wait_ge(rstd_ok, gi + 1)
                for u in range(GR):
                    b = gi * GR + u
                    normalise(b, u)
                    if not (isinstance(b, int) and b < 1):
                        copy(b - 1, (u - 1) % GR)
                    if not (isinstance(b, int) and b < 2):
                        store(b - 2, (u - 2) % GR, scale)

            root(0)
            root(1)
            group(0, False)
            with s.Fori(1, SG) as gi:
                root(gi + 1)
                group(gi, False)
            for gi in range(SG + 1, NG):
                root(gi)
            s.wait_ge(deg_ok, 1)
            nc.scalar.activation(dinv[:], deg[:], ACT.Sqrt).then_inc(deg_std, 1)
            s.wait_ge(dinv_ok, 1)
            for gi in range(SG, NG):
                group(gi, True)
            copy(NBLK - 1, GR - 1)
            store(NBLK - 2, GR - 2, True)
            store(NBLK - 1, GR - 1, True)
            s.wait_ge(dma_rows, 32)
            for t in range(NT):
                wait(s, item_ps, t - 2)
                nc.scalar.copy(rowf[:, t % 4, 0, :], src_rows[:, t, :]).then_inc(rows_ok, 1)
                nc.scalar.activation(rowf[:, t % 4, 1, :], dst_rows[:, t, :], ACT.Identity,
                                     bias=chunk0[:, t:t + 1]).then_inc(rows_ok, 1)

        @block.tensor
        def _(t_):
            pe = nc.tensor
            t_.wait_ge(onehots, 2)
            for t in range(NT):
                mm = pe.matmul(p_deg[:, 0:NBLK], one_lo[:, t, :], one_hi[:, t, :], start=(t == 0),
                               stop=(t == NT - 1))
            mm.then_inc(hist, 1)
            t_.wait_ge(consts, 7)
            t_.wait_ge(hist_sb, 1)
            pe.matmul(p_blk[0:NBLK, 0:P], firsts[:], ones[:], start=True, stop=True).then_inc(blk_ps, 1)
            t_.wait_ge(blk_sb, 1)
            pe.matmul(p_deg[:, 0:NBLK], below[:], firsts[:], start=True, stop=False)
            pe.matmul(p_deg[:, 0:NBLK], block_n[:], below[0:NBLK, 0:NBLK], start=False, stop=True
                      ).then_inc(less_ps, 1)
            t_.wait_ge(dma_gw, 16)

            def transposes(b, u):
                t_.wait_ge(xn_ok, b + 1)
                wait(t_, xnT_ok, b if u == 0 else b - 1)
                for a in range(CH):
                    mm = pe.transpose(p_tr[u % 2][:, a, :], xn[:, u, a * P:(a + 1) * P], ident[:])
                mm.then_inc(tr_ok, 1)

            def products(b, u):
                t_.wait_ge(xnT_ok, b + 1)
                wait(t_, h_out, b if u == 0 else b - 1)
                for a in range(CH):
                    mm = pe.matmul(p_h[u % 2][:, 0:C], xnT[:, u, a, :], gw_sb[:, a, :], start=(a == 0),
                                   stop=(a == CH - 1))
                mm.then_inc(h_ok, 1)

            def group(gi):
                for u in range(GR):
                    b = gi * GR + u
                    transposes(b, u)
                    if not (isinstance(b, int) and b < 1):
                        products(b - 1, (u - 1) % GR)

            group(0)
            with t_.Fori(1, SG) as gi:
                group(gi)
            t_.wait_ge(consts, 24)
            t_.wait_ge(place_ok, 1)
            pe.matmul(p_deg[:, 0:NBLK], next_p[:], place[:, 0:NBLK], start=True, stop=False)
            pe.matmul(p_deg[:, 0:NBLK], wrap_p[:], place[:, 1:NBLK + 1], start=False, stop=True
                      ).then_inc(shifted, 1)
            with t_.Fori(SG, NG) as gi:
                group(gi)
            products(NBLK - 1, GR - 1)

            for t in range(NT):
                t_.wait_ge(bands, t + 1)
                t_.wait_ge(rows_ok, 2 * t + 2)
                wait(t_, items, 3 * t - 3)
                for k, wt in enumerate([t - 1, t] if t else [t]):
                    f = slice(P, 2 * P) if wt < t else slice(0, P)
                    lastk = wt == t
                    for q in range(2):
                        pe.matmul(p_it[t % 2][:, q, :], rowf[:, wt % 4, q, :], bandf[:, wt % 4, f],
                                  start=(k == 0 and q == 0), stop=lastk, skip_group_check=True)
                    mm = pe.matmul(p_row[t % 2][0:1, 0:P], chunkn[:, wt:wt + 1], bandf[:, wt % 4, f],
                                   start=(k == 0), stop=lastk)
                mm.then_inc(item_ps, 1)


def aggregate_and_mix(nc, sb, ps, sem, g):
    (table, acc, res, src_item, dst_item, blk_item, rstd, nmr, kvz, ident, col, wq_sb, w1t_sb, w2t_sb,
     dma_w, v1, headmask) = (g[k] for k in ("table", "acc", "res", "src_item", "dst_item", "blk_item", "rstd", "nmr", "kvz",
                              "ident", "col", "wq_sb", "w1t_sb", "w2t_sb", "dma_w", "v1", "headmask"))
    slots, dma_empty = g["slots"], g["dma_empty"]
    NDMA_W = 12
    first_mix = NKV
    with ExitStack() as st:
        ring = sb("ring", [P, RING, C], st=st)
        sel = sb("sel", [P, RING, P], st=st)
        idx = sb("idx", [P, PER], I32, st)
        empty = sb("empty", [P, ROW], st=st)
        xn = sb("xn_m", [P, C], st=st)
        xnT = sb("xnT_m", [P, CH, P], st=st)
        qr = sb("qr", [P, CH, P], st=st)
        qe = sb("qe", [P, CH, P], st=st)
        qT = sb("qT", [P, CH, P], st=st)
        den = sb("den", [P, CH, P // DH], st=st)
        t = sb("t_m", [P, CH, P], st=st)
        st1, st2 = sb("st1", [P, 6], st=st), sb("st2", [P, 6], st=st)
        mv1, mv2 = sb("mv1", [P, 2], st=st), sb("mv2", [P, 2], st=st)
        sd1, sd2 = sb("sd1", [P, 1], st=st), sb("sd2", [P, 1], st=st)
        r1, r2 = sb("r1", [P, 1], st=st), sb("r2", [P, 1], st=st)
        nm1, nm2 = sb("nm1", [P, 1], st=st), sb("nm2", [P, 1], st=st)
        tmp1, tmp2 = sb("tmp1", [P, 1], st=st), sb("tmp2", [P, 1], st=st)
        x1n = sb("x1n", [P, C], st=st)
        x1T = sb("x1T", [P, CH, P], st=st)
        gT = sb("gT", [P, CH, P], st=st)
        yn = sb("yn", [P, C], st=st)
        kr = sb("kr", [P, C], st=st)
        ke = sb("ke", [P, 2, C], st=st)
        kf = sb("kf", [P, 2, C], st=st)
        p_item = [ps(f"p_item{i}", [P, 512], st) for i in range(PSLOT)]
        p_t = ps("p_t", [P, 4, P], st)
        p_q = ps("p_q", [P, 4, P], st)
        p_nd = ps("p_nd", [P, CH, 2 * P], st)
        p_g = ps("p_g", [P, 4, P], st)
        p_y = ps("p_y", [P, 512], st)
        p_kv = p_q[:].rearrange("p a c -> p (a c)")
        p_kk = [p_g[:].rearrange("p a c -> p (a c)"), p_y[:]]
        KSTEP = PER // KVB

        gathered = [sem(f"gathered{i}", st) for i in range(RING // TRI)]
        multiplied = sem("multiplied", st)
        selected = sem("selected", st)
        added = sem("added", st)
        idx_ok = sem("idx_ok", st)
        kx_ok, ktr, kxT_ok, kv_ok, kr_ok, kv_act, k_ok, kv_acc, kvz_st = (sem("k_" + n, st) for n in (
            "xn", "tr", "xnT", "kv", "kr", "act", "k", "acc", "z"))
        const2 = sem("const2", st)
        xn_ok, tr1_ok, xnT_ok, q_ps, q_rel, q_exp, qT_ok, nd_ps, den_ok = (sem("m_" + n, st) for n in (
            "xn", "tr1", "xnT", "qps", "qrel", "qexp", "qT", "ndps", "den"))
        t_rec, t_mul, t_add, s_st1, var1, std1, n1 = (sem("m_" + n, st) for n in (
            "trec", "tmul", "tadd", "st1", "var1", "std1", "n1"))
        x1n_ok, tr2_ok, x1T_ok, g_ps, gelu_ok, y_ps = (sem("m_" + n, st) for n in (
            "x1n", "tr2", "x1T", "gps", "gelu", "yps"))
        s_st2, var2, std2, n2, yn_ok, fin = (sem("m_" + n, st) for n in ("st2", "var2", "std2", "n2", "yn", "fin"))
        block = st.enter_context(nc.Block())

        def dyn(tile, b):
            return tile[:, bass.ds(b, 1), :].rearrange("p a c -> p (a c)")

        @block.sync
        def _(sp):
            sp.dma_start(g["fb1_sb"][:], g["fb1"]).then_inc(g["dma_fb"], 16)
            sp.wait_ge(const2, 2)
            sp.wait_ge(multiplied, 4 * PER)
            full = SLOTS // P
            sp.dma_start(slots[0:full * P, :].rearrange("(a p) c -> p a c", p=P),
                         empty[:].rearrange("p (a c) -> p a c", a=1).broadcast_to([P, full, ROW])
                         ).then_inc(dma_empty, 16)
            sp.dma_start(slots[full * P:SLOTS, :], empty[0:SLOTS - full * P, :]).then_inc(dma_empty, 16)
            sp.wait_ge(dma_empty, 32)

        @block.gpsimd
        def _(pool):
            nc.gpsimd.memset(empty[:], 0.0).then_inc(const2, 1)
            pool.wait_ge(const2, 1)
            nc.gpsimd.memset(empty[:, C + 3:C + 4].bitcast(I32), NOWHERE).then_inc(const2, 1)

            def gathers(it):
                for k in range(PER):
                    if k % GRP == 0:
                        pool.wait_ge(idx_ok, it * (PER // GRP) + k // GRP + 1)
                    wait_apart(pool, multiplied, it * PER + k - RING + 1, const2, 2)
                    nc.gpsimd.indirect_dma_start(ring[:, k % RING, :], None, table,
                                                 bass.IndirectOffsetOnAxis(idx[:, k:k + 1], 0)
                                                 ).then_inc(gathered[k // TRI], 16)

            gathers(0)
            with pool.Fori(1, NPASS) as it:
                gathers(it)

        @block.tensor
        def _(t_):
            pe = nc.tensor
            t_.wait_ge(dma_w, 16 * NDMA_W)

            def item(it, k):
                i = it * PER + k
                if k % TRI == 0:
                    t_.wait_ge(gathered[k // TRI], (it + 1) * 16 * TRI)
                t_.wait_ge(selected, i + 1)
                wait(t_, added, i - PSLOT + 1)
                pe.matmul(p_item[k % PSLOT][:, 0:C], sel[:, k % RING, :], ring[:, k % RING, :],
                          start=True, stop=True).then_inc(multiplied, 1)

            def transposes_x(b):
                t_.wait_ge(xn_ok, b + 1)
                wait(t_, x1T_ok, b * 2)
                for a in range(CH):
                    mm = pe.transpose(p_t[:, a, :], xn[:, a * P:(a + 1) * P], ident[:])
                mm.then_inc(tr1_ok, 1)

            def queries(b):
                t_.wait_ge(xnT_ok, b + 1)
                wait(t_, qT_ok, b)
                for m in range(CH):
                    for a in range(CH):
                        mm = pe.matmul(p_q[:, m, :], wq_sb[:, a, m * P:(m + 1) * P], xnT[:, a, :],
                                       start=(a == 0), stop=(a == CH - 1))
                mm.then_inc(q_ps, 1)

            def attention(b):
                t_.wait_ge(qT_ok, b + 1)
                wait(t_, t_mul, b * CH)
                for a in range(CH):
                    mm = pe.matmul(p_nd[:, a, 0:P + P // DH], qT[:, a, :], kvz[:, a, :], start=True, stop=True)
                mm.then_inc(nd_ps, 1)

            def transposes_x1(b):
                t_.wait_ge(x1n_ok, b + 1)
                t_.wait_ge(xnT_ok, b + 1)
                for a in range(CH):
                    mm = pe.transpose(p_t[:, a, :], x1n[:, a * P:(a + 1) * P], ident[:])
                mm.then_inc(tr2_ok, 1)

            def hidden(b):
                t_.wait_ge(x1T_ok, b * 2 + 2)
                for m in range(CH):
                    for a in range(CH):
                        mm = pe.matmul(p_g[:, m, :], w1t_sb[:, a, m * P:(m + 1) * P], x1T[:, a, :],
                                       start=(a == 0), stop=(a == CH - 1))
                mm.then_inc(g_ps, 1)

            def output(b):
                t_.wait_ge(gelu_ok, b * 2 + 2)
                for a in range(CH):
                    pe.matmul(p_y[:, 0:C], gT[:, a, :], w2t_sb[:, a, :], start=(a == 0), stop=False,
                              skip_group_check=True)
                for a in range(CH):
                    pe.matmul(p_y[:, a * P:(a + 1) * P], x1T[:, a, :], ident[:], start=False, stop=False,
                              skip_group_check=True)
                pe.matmul(p_y[:, 0:C], g["ones_row"][:], g["b2row"][:], start=False, stop=True,
                          skip_group_check=True).then_inc(y_ps, 1)

            def kv_transposes(b):
                t_.wait_ge(kx_ok, b + 1)
                wait(t_, kxT_ok, b)
                for a in range(CH):
                    mm = pe.transpose(p_t[:, a, :], xn[:, a * P:(a + 1) * P], ident[:])
                mm.then_inc(ktr, 1)

            def kv_products(b):
                t_.wait_ge(kxT_ok, b + 1)
                wait(t_, k_ok, b)
                for a in range(CH):
                    mm = pe.matmul(p_kv, xnT[:, a, :], wq_sb[:, a, C:3 * C], start=(a == 0), stop=(a == CH - 1))
                mm.then_inc(kv_ok, 1)

            def kv_sums(b, u, rows, first, last):
                t_.wait_ge(k_ok, b + 1)
                for a in range(CH):
                    mm = pe.matmul(p_kk[a][:, 0:P + 2], kf[0:rows, u, a * P:(a + 1) * P], v1[0:rows, u, a, :],
                                   start=first, stop=last)
                mm.then_inc(kv_acc, 1)

            def kv_pass(it, blocks):
                for k in range(PER):
                    item(it, k)
                    j = k // KSTEP
                    b = it * KVB + j
                    if k % KSTEP == 1 and j < blocks:
                        kv_transposes(b)
                    if k % KSTEP == 3 and j <= blocks and j < KVB:
                        if not (isinstance(b, int) and b == 0):
                            last = isinstance(b, int) and b == NBLK
                            kv_sums(b - 1, (j - 1) % 2, LAST if last else P, isinstance(b, int) and b == 1, last)
                        if j < blocks:
                            kv_products(b)

            def mix_pass(it, first=False, last=False):
                b = it - first_mix
                for k in range(PER):
                    item(it, k)
                    if not first:
                        if k == 0:
                            transposes_x1(b - 1)
                        if k == 2:
                            hidden(b - 1)
                        if k == 7:
                            output(b - 1)
                    if not last:
                        if k == 3:
                            transposes_x(b)
                        if k == 5:
                            queries(b)
                        if k == 10:
                            attention(b)

            kv_pass(0, KVB)
            with t_.Fori(1, NKV - 1) as it:
                kv_pass(it, KVB)
            kv_pass(NKV - 1, NBLK - KVB * (NKV - 1))
            t_.wait_ge(kvz_st, 2 * CH)
            mix_pass(first_mix, first=True)
            with t_.Fori(first_mix + 1, first_mix + NBLK) as it:
                mix_pass(it)
            mix_pass(first_mix + NBLK, last=True)
            with t_.Fori(first_mix + NBLK + 1, NPASS) as it:
                for k in range(PER):
                    item(it, k)

        @block.scalar
        def _(s):
            s.wait_ge(const2, 2)
            s.wait_ge(dma_w, 16 * NDMA_W)

            def keys(b, u):
                wait(s, ktr, b)
                nc.scalar.activation(xn[:], dyn(res, b), ACT.Identity, scale=rstd[:, bass.ds(b, 1)],
                                     bias=nmr[:, bass.ds(b, 1)]).then_inc(kx_ok, 1)
                s.wait_ge(ktr, b + 1)
                wait(s, kv_ok, b)
                nc.scalar.copy(xnT[:], p_t[:, 0:CH, :]).then_inc(kxT_ok, 1)
                s.wait_ge(kv_ok, b + 1)
                wait(s, kv_act, b * 2)
                nc.scalar.activation(kr[:], p_kv[:, 0:C], ACT.Relu, scale=-1.0).then_inc(kr_ok, 1)
                wait(s, k_ok, b - 1)
                wait(s, kv_acc, b - 1)
                nc.scalar.copy(v1[:, u, :, 0:P], p_kv[:, C:2 * C].rearrange("p (a c) -> p a c", a=CH)
                               ).then_inc(kv_act, 1)
                s.wait_ge(kr_ok, b + 1)
                nc.scalar.activation(ke[:, u, :], kr[:], ACT.Exp, scale=-1.0).then_inc(kv_act, 1)

            def normalised_t(c):
                s.wait_ge(var1, c + 1)
                nc.scalar.activation(sd1[:], mv1[:, 1:2], ACT.Sqrt, bias=g["eps_ln"][:]).then_inc(std1, 1)
                s.wait_ge(n1, c * 5 + 5)
                wait(s, tr2_ok, c)
                nc.scalar.activation(x1n[:], t[:].rearrange("p a c -> p (a c)"), ACT.Identity, scale=r1[:],
                                     bias=nm1[:]).then_inc(x1n_ok, 1)

            def x1_transposed(c):
                s.wait_ge(tr2_ok, c + 1)
                for a in range(CH):
                    nc.scalar.activation(x1T[:, a, :], p_t[:, a, :], ACT.Identity,
                                         scale=g["cols"]["ln1g"][:, a:a + 1], bias=g["cols"]["ln1b"][:, a:a + 1]
                                         ).then_inc(x1T_ok, 1)

            def gelu(c):
                s.wait_ge(g_ps, c + 1)
                for a in range(CH):
                    nc.scalar.activation(gT[:, a, :], p_g[:, a, :], ACT.Gelu, bias=g["cols"]["b1"][:, a:a + 1]
                                         ).then_inc(gelu_ok, 1)

            def normalised_y(c):
                s.wait_ge(var2, c + 1)
                nc.scalar.activation(sd2[:], mv2[:, 1:2], ACT.Sqrt, bias=g["eps_ln"][:]).then_inc(std2, 1)
                s.wait_ge(n2, c * 5 + 5)
                nc.scalar.activation(yn[:], p_y[:, 0:C], ACT.Identity, scale=r2[:], bias=nm2[:]
                                     ).then_inc(yn_ok, 1)

            def x_normalised(b):
                wait(s, tr1_ok, b)
                wait(s, t_add, b)
                nc.scalar.activation(xn[:], dyn(res, b), ACT.Identity, scale=rstd[:, bass.ds(b, 1)],
                                     bias=nmr[:, bass.ds(b, 1)]).then_inc(xn_ok, 1)

            def queries(b):
                s.wait_ge(tr1_ok, b + 1)
                wait(s, q_ps, b)
                nc.scalar.copy(xnT[:], p_t[:, 0:CH, :]).then_inc(xnT_ok, 1)
                s.wait_ge(q_ps, b + 1)
                wait(s, q_exp, b)
                nc.scalar.activation(qr[:], p_q[:, 0:CH, :], ACT.Relu, scale=-1.0).then_inc(q_rel, 1)
                s.wait_ge(q_rel, b + 1)
                wait(s, qT_ok, b)
                nc.scalar.activation(qe[:], qr[:], ACT.Exp, scale=-1.0).then_inc(q_exp, 1)

            def mix_pass(it, first=False, last=False):
                b = it - first_mix
                if not last:
                    x_normalised(b)
                if not first:
                    x1_transposed(b - 1)
                    gelu(b - 1)
                if not last:
                    queries(b)
                if not first:
                    normalised_y(b - 1)
                if not last:
                    normalised_t(b)

            for b in range(2):
                keys(b, b)
            with s.Fori(1, NBLK // 2) as it:
                for u in range(2):
                    keys(it * 2 + u, u)
            keys(NBLK - 1, 0)
            s.wait_ge(kv_acc, NBLK)
            mix_pass(first_mix, first=True)
            with s.Fori(first_mix + 1, first_mix + NBLK) as it:
                mix_pass(it)
            mix_pass(first_mix + NBLK, last=True)

        @block.vector
        def _(v):
            v.wait_ge(dma_w, 16 * NDMA_W)
            regs = [v.alloc_register(f"item_block{i}") for i in range(GRP)]

            def sources(it, q):
                nc.vector.tensor_copy(idx[:, q * GRP:(q + 1) * GRP],
                                      src_item[:, bass.ds(it * PER + q * GRP, GRP)]).then_inc(idx_ok, 1)

            def select(it, k):
                nc.vector.tensor_scalar(sel[:, k % RING, :], col[:], dst_item[:, bass.ds(it * PER + k, 1)], None,
                                        ALU.is_equal).then_inc(selected, 1)

            def add(j, slot, blk):
                v.wait_ge(multiplied, j + 1)
                wait(v, added, j)
                a = acc[:, bass.ds(blk, 1), 0:C].rearrange("p a c -> p (a c)")
                nc.vector.tensor_tensor(a, a, p_item[slot][:, 0:C], ALU.add).then_inc(added, 1)

            def queries(b):
                v.wait_ge(q_exp, b + 1)
                wait(v, nd_ps, b)
                nc.vector.scalar_tensor_tensor(qT[:], p_q[:, 0:CH, :], 0.0, qe[:], ALU.max, ALU.add
                                               ).then_inc(qT_ok, 1)

            def attention(b, n):
                if n == 0:
                    v.wait_ge(nd_ps, b + 1)
                    nc.vector.tensor_scalar(den[:], p_nd[:, :, P:P + P // DH], EPS_ATTN, None, ALU.add
                                            ).then_inc(den_ok, 1)
                    v.wait_ge(den_ok, b + 1)
                    nc.vector.reciprocal(den[:], den[:]).then_inc(t_rec, 1)
                if n == 1:
                    v.wait_ge(t_rec, b + 1)
                    wait(v, x1n_ok, b)
                    for a in range(CH):
                        heads = "p (h d) -> p h d"
                        nc.vector.tensor_tensor(t[:, a, :].rearrange(heads, d=DH),
                                                p_nd[:, a, 0:P].rearrange(heads, d=DH),
                                                den[:, a, :].rearrange("p (h d) -> p h d", d=1)
                                                .broadcast_to([P, P // DH, DH]), ALU.mult).then_inc(t_mul, 1)
                if n == 2:
                    v.wait_ge(t_mul, b * CH + CH)
                    t2 = t[:].rearrange("p a c -> p (a c)")
                    nc.vector.tensor_tensor(t2, t2, xn[:], ALU.add).then_inc(t_add, 1)

            def norm(b, n, src, ready, stt, st_sem, mv, var, sd, std, r, nm, tmp, s_n):
                V = nc.vector
                if n == 0:
                    wait_apart(v, ready, b + 1, g["consts"], 16)
                    V.bn_stats(stt[:], src).then_inc(st_sem, 1)
                if n == 1:
                    wait_apart(v, st_sem, b + 1, g["consts"], 16)
                    V.bn_aggr(mv[:], stt[:]).then_inc(var, 1)
                if n == 2:
                    v.wait_ge(std, b + 1)
                    V.reciprocal(r[:], sd[:]).then_inc(s_n, 1)
                if n > 2:
                    v.wait_ge(s_n, b * 5 + n - 2)
                if n == 3:
                    V.scalar_tensor_tensor(tmp[:], mv[:, 1:2], EPS, r[:], ALU.add, ALU.mult).then_inc(s_n, 1)
                if n == 4:
                    V.scalar_tensor_tensor(tmp[:], tmp[:], -0.5, r[:], ALU.mult, ALU.mult).then_inc(s_n, 1)
                if n == 5:
                    V.scalar_tensor_tensor(r[:], tmp[:], 1.5, r[:], ALU.add, ALU.mult).then_inc(s_n, 1)
                if n == 6:
                    V.scalar_tensor_tensor(nm[:], mv[:, 0:1], -1.0, r[:], ALU.mult, ALU.mult).then_inc(s_n, 1)

            def norm1(b, n):
                norm(b, n, t[:].rearrange("p a c -> p (a c)"), t_add, st1, s_st1, mv1, var1, sd1, std1, r1, nm1,
                     tmp1, n1)

            def norm2(b, n):
                norm(b, n, p_y[:, 0:C], y_ps, st2, s_st2, mv2, var2, sd2, std2, r2, nm2, tmp2, n2)

            def finish(b, n):
                if n == 0:
                    v.wait_ge(yn_ok, b + 1)
                    nc.vector.tensor_tensor(yn[:], yn[:], g["bias_b"]["ln2g"][:], ALU.mult).then_inc(fin, 1)
                if n == 1:
                    v.wait_ge(fin, b * 3 + 1)
                    nc.vector.tensor_tensor(yn[:], yn[:], g["bias_b"]["ln2b"][:], ALU.add).then_inc(fin, 1)
                if n == 2:
                    v.wait_ge(fin, b * 3 + 2)
                    nc.vector.tensor_tensor(dyn(res, b), dyn(res, b), yn[:], ALU.add).then_inc(fin, 1)

            def keys_of(b, u):
                v.wait_ge(kv_act, b * 2 + 2)
                wait(v, kv_acc, b - 1)
                nc.vector.scalar_tensor_tensor(kf[:, u, :], p_kv[:, 0:C], 0.0, ke[:, u, :], ALU.max, ALU.add
                                               ).then_inc(k_ok, 1)

            def items(it, k, blk):
                if k % GRP == 0:
                    v.load(regs, blk_item[0:1, bass.ds(it * PER + k, GRP)])
                    blk[:] = [v.snap(r, min_val=0, max_val=NBLK - 1) for r in regs]
                select(it, k)
                if not (isinstance(it, int) and it * PER + k < LAG):
                    add(it * PER + k - LAG, (k - LAG) % PSLOT, blk[k % GRP])
                if k == 4:
                    sources(it, 2)
                if k == 11:
                    sources(it + 1, 0)
                if k == 18:
                    sources(it + 1, 1)

            def kv_pass(it, blocks):
                blk = []
                for k in range(PER):
                    items(it, k, blk)
                    j = k // KSTEP
                    b = it * KVB + j
                    if k % KSTEP == 3 and j <= blocks and j < KVB and not (isinstance(b, int) and b == 0):
                        keys_of(b - 1, (j - 1) % 2)

            def mix_pass(it, first=False, last=False):
                b = it - first_mix
                blk = []
                for k in range(PER):
                    items(it, k, blk)
                    if not first:
                        for n, at in enumerate((11, 12, 13, 13, 14, 14, 15)):
                            if k == at:
                                norm2(b - 1, n)
                        for n, at in enumerate((18, 19, 20)):
                            if k == at:
                                finish(b - 1, n)
                    if not last:
                        if k == 11:
                            queries(b)
                        for n, at in enumerate((13, 14, 15)):
                            if k == at:
                                attention(b, n)
                        for n, at in enumerate((16, 17, 18, 18, 19, 19, 20)):
                            if k == at:
                                norm1(b, n)

            sources(0, 0)
            sources(0, 1)
            kv_pass(0, KVB)
            with v.Fori(1, NKV - 1) as it:
                kv_pass(it, KVB)
            kv_pass(NKV - 1, NBLK - KVB * (NKV - 1))
            v.wait_ge(kv_acc, NBLK)
            for a in range(CH):
                nc.vector.tensor_tensor(kvz[:, a, 0:P], p_kk[a][:, 0:P], headmask[:], ALU.mult).then_inc(kvz_st, 1)
                nc.vector.tensor_scalar(kvz[:, a, P:P + P // DH],
                                        headmask[:].rearrange("p (h d) -> p h d", d=DH)[:, :, 0],
                                        p_kk[a][:, P:P + 1], None, ALU.mult).then_inc(kvz_st, 1)
            mix_pass(first_mix, first=True)
            with v.Fori(first_mix + 1, first_mix + NBLK) as it:
                mix_pass(it)
            mix_pass(first_mix + NBLK, last=True)
            with v.Fori(first_mix + NBLK + 1, NPASS) as it:
                blk = []
                for k in range(PER):
                    items(it, k, blk)
            v.load(regs[0:LAG], blk_item[0:1, NITEM:NITEM + LAG])
            for q in range(LAG):
                j = NITEM - LAG + q
                add(j, (PER - LAG + q) % PSLOT, v.snap(regs[q], min_val=0, max_val=NBLK - 1))


def route(nc, sb, ps, sem, g):
    (acc, res, dinv, ident, gate_sb, gateb_b, slots, dma_empty, dma_out, out) = (g[k] for k in (
        "acc", "res", "dinv", "ident", "gate_sb", "gateb_b", "slots", "dma_empty", "dma_out", "out"))
    GR = RGR
    NG = NBLK // GR
    assert NG * GR == NBLK and NBLK <= 256
    GE = GR * EXP
    with ExitStack() as st:
        stt = sb("stt", [P, 2, GR, 6], st=st)
        mvg = sb("mvg", [P, 2, GR, 2], st=st)
        sdg = sb("sdg", [P, 2, GR], st=st)
        tmp = sb("tmp_r", [P, GR], st=st)
        xr = sb("xr", [P, GR, C], st=st)
        xrT = sb("xrT", [P, GR, CH, P], st=st)
        triu = sb("triu", [P, P], BF16, st)
        ones = sb("ones", [P, P], BF16, st)
        e8 = sb("e8", [P, EXP], st=st)
        node_i = sb("node_i", [P, NBLK], I32, st)
        real = sb("real", [P, NBLK], st=st)
        G8 = [P, GR, EXP]
        lg, cand, cur = sb("lg", G8, st=st), sb("cand", G8, st=st), sb("cur", G8, st=st)
        ex = sb("ex", [P, 2, GR, EXP], st=st)
        oh = sb("oh", [P, 2, GR, EXP], BF16, st)
        before = sb("before", [P, 2, EXP], BF16, st)
        inside = sb("inside", [P, EXP], st=st)
        m1, m2 = sb("m1", [P, GR], st=st), sb("m2", [P, 2, GR], st=st)
        psum_e = sb("psum_e", [P, GR], st=st)
        place = sb("place_r", [P, GR], st=st)
        rowno = sb("rowno", [P, GR], st=st)
        kept = sb("kept", [P, GR], st=st)
        dest = sb("dest", [P, NBLK], I32, st)
        p_t = [ps(f"r_t{i}", [P, 4, P], st) for i in range(2)]
        p_l = [ps(f"r_l{i}", [P, 512], st) for i in range(2)]
        p_in = [ps(f"r_in{i}", [P, 512], st) for i in range(2)]
        (const3, s1, s2, s3, s4, std, norm_ok, xr_ok, tr_ok, xT_ok, l_ps, dv, e_ok, e_act, oh_ok, cum, dest_ok,
         sent) = (sem("r_" + n, st) for n in (
            "const3", "s1", "s2", "s3", "s4", "std", "norm", "xr", "tr", "xT", "lps", "dv", "e", "eact", "oh",
            "cum", "dest", "sent"))
        block = st.enter_context(nc.Block())

        def blocks(gi):
            return slice(gi * GR, gi * GR + GR)

        @block.gpsimd
        def _(pool):
            nc.gpsimd.iota(node_i[:], [[P, NBLK]], 0, 1).then_inc(const3, 1)
            nc.gpsimd.iota(real[:], [[P, NBLK]], 0, 1, allow_small_or_imprecise_dtypes=True).then_inc(const3, 1)
            nc.gpsimd.iota(e8[:], [[1, EXP]], 0, 0, allow_small_or_imprecise_dtypes=True).then_inc(const3, 1)
            nc.gpsimd.memset(ones[:], 1.0).then_inc(const3, 1)
            nc.gpsimd.memset(triu[:], 1.0).then_inc(const3, 1)
            pool.wait_ge(const3, 5)
            nc.gpsimd.affine_select(triu[:], triu[:], [[1, P]], ALU.is_ge, 0.0, 0, -1).then_inc(const3, 1)
            pool.wait_ge(dma_empty, 32)
            for b in range(NBLK):
                if b % GR == 0:
                    pool.wait_ge(dest_ok, b // GR + 1)
                nc.gpsimd.indirect_dma_start(slots, bass.IndirectOffsetOnAxis(dest[:, b:b + 1], 0), acc[:, b, :],
                                             None, bounds_check=SLOTS - 1, oob_is_err=False).then_inc(sent, 16)
            pool.wait_ge(sent, 16 * NBLK)

        @block.sync
        def _(sp):
            for gi in range(NG):
                sp.wait_ge(s2, gi * GR + GR)
                sp.dma_start(out[gi * GR * P:(gi + 1) * GR * P, :].rearrange("(b p) c -> p b c", p=P),
                             acc[:, blocks(gi), 0:C]).then_inc(dma_out, 16)
            sp.wait_ge(dma_out, 16 * NOUT)

        @block.vector
        def _(v):
            V = nc.vector
            n = [0]

            def link(ins):
                n[0] += 1
                ins.then_inc(dv, 1)
                v.wait_ge(dv, n[0])

            def over_e(a):
                return a.rearrange("p (b e) -> p b e", e=1).broadcast_to(G8)

            def over_b(a):
                return a.rearrange("p (b e) -> p b e", b=1).broadcast_to(G8)

            def x2(gi):
                for b in range(gi * GR, gi * GR + GR):
                    V.scalar_tensor_tensor(acc[:, b, 0:C], acc[:, b, 0:C], dinv[:, b:b + 1], g["bias_b"]["gb"][:],
                                           ALU.mult, ALU.add).then_inc(s1, 1)
                for b in range(gi * GR, gi * GR + GR):
                    v.wait_ge(s1, b + 1)
                    V.scalar_tensor_tensor(acc[:, b, 0:C], acc[:, b, 0:C], 0.0, res[:, b, :], ALU.max, ALU.add
                                           ).then_inc(s2, 1)
                for b in range(gi * GR, gi * GR + GR):
                    v.wait_ge(s2, b + 1)
                    V.bn_stats(stt[:, gi % 2, b % GR, :], acc[:, b, 0:C]).then_inc(s3, 1)
                for b in range(gi * GR, gi * GR + GR):
                    v.wait_ge(s3, b + 1)
                    V.bn_aggr(mvg[:, gi % 2, b % GR, :], stt[:, gi % 2, b % GR, :]).then_inc(s4, 1)

            def inverse_std(gi):
                r = acc[:, blocks(gi), C + 1]
                mv = mvg[:, gi % 2]
                v.wait_ge(std, gi + 1)
                link(V.reciprocal(r, sdg[:, gi % 2]))
                rsqrt_steps(nc, link, r, mv[:, :, 1], tmp[:], EPS)
                V.scalar_tensor_tensor(acc[:, blocks(gi), C], mv[:, :, 0], -1.0, r, ALU.mult, ALU.mult
                                       ).then_inc(norm_ok, 1)

            def choose(gi):
                q = gi % 2
                v.wait_ge(l_ps, gi * GR + GR)
                link(V.tensor_tensor(lg[:], p_l[q][:, 0:GE].rearrange("p (b e) -> p b e", e=EXP),
                                     over_b(gateb_b[:]), ALU.add))
                link(V.tensor_reduce(m1[:], lg[:], AX.X, ALU.max))
                V.tensor_tensor(ex[:, q], lg[:], over_e(m1[:]), ALU.subtract).then_inc(e_ok, 1)
                link(V.tensor_tensor(cand[:], lg[:], over_e(m1[:]), ALU.is_equal))
                link(V.scalar_tensor_tensor(cand[:], cand[:], -float(EXP), over_b(e8[:]), ALU.mult, ALU.add))
                link(V.tensor_reduce(m2[:, q], cand[:], AX.X, ALU.min))
                link(V.tensor_tensor(oh[:, q], cand[:], over_e(m2[:, q]), ALU.is_equal))
                V.tensor_copy(cur[:], oh[:, q]).then_inc(oh_ok, 1)
                if gi + 1 < NG:
                    link(V.tensor_reduce(inside[:], oh[:, q].rearrange("p b e -> p e b"), AX.X, ALU.add))
                    if gi == 0:
                        link(V.tensor_copy(before[:, 1], inside[:]))
                    else:
                        link(V.tensor_tensor(before[:, 1 - q], before[:, q], inside[:], ALU.add))

            def assign(gi):
                q = gi % 2
                v.wait_ge(e_act, gi + 1)
                link(V.tensor_reduce(psum_e[:], ex[:, q], AX.X, ALU.add))
                link(V.reciprocal(acc[:, blocks(gi), C + 2], psum_e[:]))
                v.wait_ge(cum, gi + 1)
                v.wait_ge(oh_ok, gi + 1)
                link(V.tensor_tensor(cur[:], cur[:], p_in[q][:, 0:GE].rearrange("p (b e) -> p b e", e=EXP),
                                     ALU.mult))
                link(V.tensor_reduce(place[:], cur[:], AX.X, ALU.add))
                link(V.scalar_tensor_tensor(rowno[:], m2[:, q], float(CAP), place[:], ALU.mult, ALU.add))
                link(V.scalar_tensor_tensor(kept[:], place[:], float(CAP), real[:, blocks(gi)], ALU.is_le,
                                            ALU.mult))
                link(V.scalar_tensor_tensor(rowno[:], rowno[:], float(EXP * CAP - 1 - NOWHERE), kept[:],
                                            ALU.add, ALU.mult))
                V.tensor_scalar(dest[:, blocks(gi)], rowno[:], float(NOWHERE), None, ALU.add).then_inc(dest_ok, 1)
                v.wait_ge(dest_ok, gi + 1)

            v.wait_ge(const3, 6)
            link(V.tensor_scalar(real[:], real[:], float(N), None, ALU.is_lt))
            link(V.tensor_copy(acc[:, :, C + 3:C + 4].bitcast(I32).rearrange("p b a -> p (b a)"), node_i[:]))
            for gi in range(NG + 1):
                if gi < NG:
                    x2(gi)
                if gi > 0:
                    choose(gi - 1)
                if gi < NG:
                    inverse_std(gi)
                if gi > 0:
                    assign(gi - 1)

        @block.scalar
        def _(s):
            def copy(b):
                s.wait_ge(tr_ok, b + 1)
                wait(s, l_ps, b - GR + 1)
                nc.scalar.copy(xrT[:, b % GR], p_t[b % 2][:, 0:CH, :]).then_inc(xT_ok, 1)

            for gi in range(NG + 1):
                if gi < NG:
                    s.wait_ge(s4, gi * GR + GR)
                    nc.scalar.activation(sdg[:, gi % 2], mvg[:, gi % 2, :, 1], ACT.Sqrt, bias=g["eps_ln"][:]
                                         ).then_inc(std, 1)
                if gi > 0:
                    s.wait_ge(e_ok, gi)
                    nc.scalar.activation(ex[:, (gi - 1) % 2], ex[:, (gi - 1) % 2], ACT.Exp).then_inc(e_act, 1)
                if gi == NG:
                    break
                s.wait_ge(norm_ok, gi + 1)
                for b in range(gi * GR, gi * GR + GR):
                    wait(s, tr_ok, b - GR + 1)
                    nc.scalar.activation(xr[:, b % GR, :], acc[:, b, 0:C], ACT.Identity,
                                         scale=acc[:, b, C + 1:C + 2], bias=acc[:, b, C:C + 1]).then_inc(xr_ok, 1)
                    if b % GR > 0:
                        copy(b - 1)
                copy(gi * GR + GR - 1)

        @block.tensor
        def _(t_):
            pe = nc.tensor
            t_.wait_ge(const3, 6)

            def logits(b):
                t_.wait_ge(xT_ok, b + 1)
                gi, u = b // GR, b % GR
                wait(t_, e_ok, gi - 1)
                for a in range(CH):
                    mm = pe.matmul(p_l[gi % 2][:, u * EXP:(u + 1) * EXP], xrT[:, u, a, :], gate_sb[:, a, :],
                                   start=(a == 0), stop=(a == CH - 1))
                mm.then_inc(l_ps, 1)

            def places(gi):
                q = gi % 2
                o = p_in[q]
                t_.wait_ge(oh_ok, gi + 1)
                wait(t_, dest_ok, gi - 1)
                last = gi == 0 and GR == 1
                pe.matmul(o[:, 0:GE], triu[:], oh[:, q].rearrange("p b e -> p (b e)"), start=True, stop=last,
                          skip_group_check=True)
                for u in range(GR - 1):
                    left = GR - 1 - u
                    mm = pe.matmul(o[:, (u + 1) * EXP:GE], ones[:], oh[:, q, u:u + 1, :]
                                   .broadcast_to([P, left, EXP]), start=False, stop=(gi == 0 and left == 1),
                                   skip_group_check=True)
                if gi > 0:
                    mm = pe.matmul(o[:, 0:GE], ones[:], before[:, q:q + 1, :].broadcast_to([P, GR, EXP]),
                                   start=False, stop=True, skip_group_check=True)
                mm.then_inc(cum, 1)

            for gi in range(NG + 1):
                if gi > 0:
                    places(gi - 1)
                if gi == NG:
                    break
                for b in range(gi * GR, gi * GR + GR):
                    t_.wait_ge(xr_ok, b + 1)
                    wait(t_, xT_ok, b - 1)
                    for a in range(CH):
                        mm = pe.transpose(p_t[b % 2][:, a, :], xr[:, b % GR, a * P:(a + 1) * P], ident[:])
                    mm.then_inc(tr_ok, 1)
                    if b % GR > 0:
                        logits(b - 1)
                logits(gi * GR + GR - 1)


def experts(nc, sb, ps, sem, g):
    slots, ident, out, fb1_sb = g["slots"], g["ident"], g["out"], g["fb1_sb"]
    w1, w2, fb2, dma_fb, dma_out = g["w1"], g["w2"], g["fb2"], g["dma_fb"], g["dma_out"]
    pads = g["pads"]
    LASTR = CAP - (RT - 1) * P
    PC = 4
    CAPE = -(-CAP // 2) * 2
    NH = (-(-CAPE // 4) * 2, CAPE - -(-CAPE // 4) * 2)
    with ExitStack() as st:
        w1raw = sb("w1raw", [P, CH, F], st=st)
        w2raw = sb("w2raw", [P, FT, C], st=st)
        w1h, w1l = sb("w1h", [P, CH, F], F32R, st), sb("w1l", [P, CH, F], F32R, st)
        w2h, w2l = sb("w2h", [P, FT, C], F32R, st), sb("w2l", [P, FT, C], F32R, st)
        rows = sb("rows", [P, 2, RT, ROW], st=st)
        fb2_b = sb("fb2_b", [P, EXP, C], st=st)
        xe = sb("xe", [P, 2, C], st=st)
        bTh, bTl = sb("bTh", [P, CH, CAPE], F32R, st), sb("bTl", [P, CH, CAPE], F32R, st)
        hbuf = sb("hbuf", [P, 2, CAPE], st=st)
        hTh, hTl = sb("hTh", [P, FT, RT * P], F32R, st), sb("hTl", [P, FT, RT * P], F32R, st)
        yb, yv = sb("yb", [P, 2, C], st=st), sb("yv", [P, 2, C], st=st)
        finite = sb("finite", [P, 2, C], I32, st)
        low, big = sb("low", [P, 2, C], st=st), sb("big", [P, 2, C], st=st)
        total = sb("total", [P, 2, C], st=st)
        oo = sb("oo", [P, 2, C], st=st)
        p_f = [ps(f"e_f{i}", [P, 512], st) for i in range(4)]
        p_y = [ps(f"e_y{i}", [P, 512], st) for i in range(2)]
        p_t = [ps(f"e_t{i}", [P, 4, P], st) for i in range(2)]
        d_w1, d_w2 = sem("d_w1", st), sem("d_w2", st)
        d_r = [sem(f"d_r{i}", st) for i in range(2)]
        d_b, sent = sem("d_b", st), [sem(f"e_sent{i}", st) for i in range(2)]
        (xe_ok, tr_ok, bh_ok, bl_ok, f1_ps, r_ok, hi_ok, lo_ok, f2_ps, yb_ok, y_ok, pool_st, inf_ok, fin_ok, o_ok,
         w1h_ok, w1l_ok, w2h_ok, w2l_ok) = (sem("e_" + n, st) for n in (
            "xe", "tr", "bh", "bl", "f1", "r", "hi", "lo", "f2", "yb", "y", "pool", "inf", "fin", "o", "w1h", "w1l",
            "w2h", "w2l"))
        block = st.enter_context(nc.Block())

        def nrows(t):
            return P if t < RT - 1 else LASTR

        def w1_piece(w, q):
            n = F * CH // PC
            return w[:, q * n // F, q * n % F:q * n % F + n]

        def w2_piece(w, q):
            return w[:, q * FT // PC:(q + 1) * FT // PC, :]

        def all_experts(eng, expert):
            for e in range(2):
                expert(e, e, True)
            with eng.Fori(1, EXP // 2 - 1) as it:
                for u in range(2):
                    expert(it * 2 + u, u, True)
            expert(EXP - 2, 0, True)
            expert(EXP - 1, 1, False)

        def wait_rows(eng, e, u):
            if isinstance(e, int):
                eng.wait_ge(d_r[u], (e // 2 + 1) * 32)
            else:
                eng.wait_ge(d_r[u], (e - u) * 16 + 32)

        def load_rows(sp, e, u):
            sp.dma_start(rows[:, u, 0:RT - 1, :],
                         slots[bass.ds(e * CAP, (RT - 1) * P), :].rearrange("(t p) c -> p t c", p=P)
                         ).then_inc(d_r[u], 16)
            sp.dma_start(rows[0:LASTR, u, RT - 1, :], slots[bass.ds(e * CAP + (RT - 1) * P, LASTR), :]
                         ).then_inc(d_r[u], 16)

        def load_w1(sp, e):
            sp.dma_start(w1raw[:], w1[bass.ds(e, 1)].rearrange("e (k p) f -> p (e k) f", p=P)).then_inc(d_w1, 16)

        def load_w2(sp, e):
            sp.dma_start(w2raw[:], w2[bass.ds(e, 1)].rearrange("e (j p) c -> p (e j) c", p=P)).then_inc(d_w2, 16)

        @block.sync
        def _(sp):
            load_w1(sp, 0)
            load_rows(sp, 0, 0)
            load_w2(sp, 0)
            load_rows(sp, 1, 1)
            sp.dma_start(fb2_b[:].rearrange("p e c -> p (e c)"),
                         fb2.rearrange("(a e) c -> a (e c)", a=1).broadcast_to([P, EXP * C])).then_inc(d_b, 16)

            def expert(e, u, more):
                if more:
                    sp.wait_ge(w1l_ok, e * PC + PC)
                    load_w1(sp, e + 1)
                    sp.wait_ge(w2l_ok, e * PC + PC)
                    load_w2(sp, e + 1)
                if more and not (isinstance(e, int) and e == EXP - 2):
                    for q in range(2):
                        sp.wait_ge(sent[q], (e * (RT // 2) + RT // 2) * 16)
                    load_rows(sp, e + 2, u)

            all_experts(sp, expert)

        @block.gpsimd
        def _(pool):
            if CAPE > CAP:
                nc.gpsimd.memset(bTh[:, :, CAP:CAPE].bitcast(F32), 0.0).then_inc(pads, 1)
                nc.gpsimd.memset(bTl[:, :, CAP:CAPE].bitcast(F32), 0.0).then_inc(pads, 1)
            nc.gpsimd.memset(hTh[:, :, CAPE:RT * P].bitcast(F32), 0.0).then_inc(pads, 1)
            nc.gpsimd.memset(hTl[:, :, CAPE:RT * P].bitcast(F32), 0.0).then_inc(pads, 1)
            pool.wait_ge(dma_out, 16 * NOUT)

            def expert(e, u, more):
                def store(t):
                    r = nrows(t)
                    wait_apart(pool, o_ok, e * RT + t + 1, dma_out, 16 * NOUT)
                    nc.gpsimd.indirect_dma_start(
                        out, bass.IndirectOffsetOnAxis(rows[0:r, u, t, C + 3:C + 4].bitcast(I32), 0),
                        oo[0:r, t % 2, :], None, bounds_check=N - 1, oob_is_err=False).then_inc(sent[t % 2], 16)

                for t in range(RT):
                    r = nrows(t)
                    T = e * RT + t
                    wait_apart(pool, inf_ok, T * 2 + 2, dma_out, 16 * NOUT)
                    nc.gpsimd.tensor_tensor(low[0:r, t % 2, :], low[0:r, t % 2, :], big[0:r, t % 2, :], ALU.add
                                            ).then_inc(pool_st, 1)
                    pool.wait_ge(pool_st, T * 2 + 1)
                    wait(pool, sent[t % 2], (e * (RT // 2) + t // 2) * 16)
                    nc.gpsimd.tensor_tensor(oo[0:r, t % 2, :], low[0:r, t % 2, :], rows[0:r, u, t, 0:C], ALU.add
                                            ).then_inc(pool_st, 1)
                    if t > 0:
                        store(t - 1)
                store(RT - 1)

            all_experts(pool, expert)
            for q in range(2):
                pool.wait_ge(sent[q], 16 * EXP * RT // 2)

        @block.scalar
        def _(s):
            s.wait_ge(dma_fb, 16)

            def normalise(e, u, t):
                r = nrows(t)
                if t == 0:
                    wait_rows(s, e, u)
                wait(s, tr_ok, e * RT + t - 1)
                nc.scalar.activation(xe[0:r, t % 2, :], rows[0:r, u, t, 0:C], ACT.Identity,
                                     scale=rows[0:r, u, t, C + 1:C + 2], bias=rows[0:r, u, t, C:C + 1]
                                     ).then_inc(xe_ok, 1)

            def high_rows(e, t):
                r = nrows(t)
                s.wait_ge(tr_ok, e * RT + t + 1)
                nc.scalar.copy(bTh[:, :, t * P:t * P + r], p_t[t % 2][:, 0:CH, 0:r]).then_inc(bh_ok, 1)

            def high_w1(e, q):
                if q == 0:
                    s.wait_ge(d_w1, e * 16 + 16)
                nc.scalar.copy(w1_piece(w1h, q), w1_piece(w1raw, q)).then_inc(w1h_ok, 1)

            def high_w2(e, q):
                if q == 0:
                    s.wait_ge(d_w2, e * 16 + 16)
                    wait(s, f2_ps, e * RT)
                nc.scalar.copy(w2_piece(w2h, q), w2_piece(w2raw, q)).then_inc(w2h_ok, 1)

            def expert(e, u, more):
                for j in range(FT):
                    for h in range(2):
                        wait_apart(s, f1_ps, e * 2 * FT + 2 * j + h + 1, dma_fb, 16)
                        wait_apart(s, lo_ok, e * FT + j - 1, dma_fb, 16)
                        nc.scalar.activation(hbuf[:, j % 2, h * NH[0]:h * NH[0] + NH[h]],
                                             p_f[(2 * j + h) % 4][:, 0:NH[h]], ACT.Relu,
                                             bias=fb1_sb[:, bass.ds(e, 1), j]).then_inc(r_ok, 1)
                    if 1 <= j < 1 + PC:
                        high_w2(e, j - 1)
                    if more and j == FT - 2:
                        normalise(e + 1, 1 - u, 0)
                for t in range(RT):
                    r = nrows(t)
                    if more:
                        high_rows(e + 1, t)
                        if t + 1 < RT:
                            normalise(e + 1, 1 - u, t + 1)
                    s.wait_ge(yb_ok, e * RT + t + 1)
                    wait(s, o_ok, e * RT + t - 1)
                    nc.scalar.activation(yv[0:r, t % 2, :], yb[0:r, t % 2, :], ACT.Identity,
                                         scale=rows[0:r, u, t, C + 2:C + 3]).then_inc(y_ok, 1)
                    if more and 1 <= t < 1 + PC:
                        high_w1(e + 1, t - 1)

            for q in range(PC):
                high_w1(0, q)
            for t in range(RT):
                normalise(0, 0, t)
                if t > 0:
                    high_rows(0, t - 1)
            high_rows(0, RT - 1)
            all_experts(s, expert)

        @block.tensor
        def _(t_):
            pe = nc.tensor

            def transposes(e, t):
                r = nrows(t)
                t_.wait_ge(xe_ok, e * RT + t + 1)
                wait(t_, bl_ok, e * RT + t - 1)
                for a in range(CH):
                    mm = pe.transpose(p_t[t % 2][:, a, 0:r], xe[0:r, t % 2, a * P:(a + 1) * P],
                                      ident[0:r, 0:r])
                mm.then_inc(tr_ok, 1)

            def expert(e, u, more):
                t_.wait_ge(w1l_ok, e * PC + PC)
                for j in range(FT):
                    for h in range(2):
                        c = 2 * j + h
                        if j == 0:
                            t_.wait_ge(bl_ok, e * RT + (-(-NH[0] // P), RT)[h])
                        wait(t_, r_ok, e * 2 * FT + c - 3)
                        parts = [(w, b, a) for a in range(CH) for w, b in ((w1h, bTh), (w1h, bTl), (w1l, bTh))]
                        for q, (w, b, a) in enumerate(parts):
                            mm = pe.matmul(p_f[c % 4][:, 0:NH[h]], w[:, a, j * P:(j + 1) * P],
                                           b[:, a, h * NH[0]:h * NH[0] + NH[h]], start=(q == 0),
                                           stop=(q == len(parts) - 1))
                        mm.then_inc(f1_ps, 1)
                t_.wait_ge(w2l_ok, e * PC + PC)
                for t in range(RT):
                    if more:
                        transposes(e + 1, t)
                    wait(t_, yb_ok, e * RT + t - 1)
                    parts = [(h, w, j) for j in range(FT) for h, w in ((hTh, w2h), (hTh, w2l), (hTl, w2h))]
                    for q, (h, w, j) in enumerate(parts):
                        if t == 0 and q % 3 == 0:
                            t_.wait_ge(lo_ok, e * FT + j + 1)
                        mm = pe.matmul(p_y[t % 2][:, 0:C], h[:, j, t * P:(t + 1) * P], w[:, j, :],
                                       start=(q == 0), stop=(q == len(parts) - 1))
                    mm.then_inc(f2_ps, 1)

            for t in range(RT):
                transposes(0, t)
            t_.wait_ge(pads, 4 if CAPE > CAP else 2)
            all_experts(t_, expert)

        @block.vector
        def _(v):
            V = nc.vector
            v.wait_ge(dma_fb, 16)

            def low_rows(e, t):
                r = nrows(t)
                v.wait_ge(bh_ok, e * RT + t + 1)
                V.tensor_tensor(bTl[:, :, t * P:t * P + r], p_t[t % 2][:, 0:CH, 0:r],
                                bTh[:, :, t * P:t * P + r].bitcast(F32), ALU.subtract).then_inc(bl_ok, 1)

            def low_w1(e, q):
                v.wait_ge(w1h_ok, e * PC + q + 1)
                V.tensor_tensor(w1_piece(w1l, q), w1_piece(w1raw, q), w1_piece(w1h, q).bitcast(F32), ALU.subtract
                                ).then_inc(w1l_ok, 1)

            def low_w2(e, q):
                v.wait_ge(w2h_ok, e * PC + q + 1)
                V.tensor_tensor(w2_piece(w2l, q), w2_piece(w2raw, q), w2_piece(w2h, q).bitcast(F32), ALU.subtract
                                ).then_inc(w2l_ok, 1)

            def result(e, t):
                r = nrows(t)
                T = e * RT + t
                if isinstance(T, int):
                    v.wait_ge(fin_ok, T * 2 + 2)
                    v.wait_ge(pool_st, T * 2 + 2)
                else:
                    both = v.to_reg(T * 2 + 2)
                    v.wait_ge(dma_fb, 16)
                    v.wait_ge(fin_ok, both)
                    v.wait_ge(pool_st, both)
                V.copy_predicated(oo[0:r, t % 2, :], finite[0:r, t % 2, :], total[0:r, t % 2, :]
                                  ).then_inc(o_ok, 1)

            def expert(e, u, more):
                for j in range(FT):
                    v.wait_ge(r_ok, e * 2 * FT + 2 * j + 2)
                    wait(v, f2_ps, e * RT)
                    V.tensor_copy(hTh[:, j, 0:CAPE], hbuf[:, j % 2, :]).then_inc(hi_ok, 1)
                    v.wait_ge(hi_ok, e * FT + j + 1)
                    V.tensor_tensor(hTl[:, j, 0:CAPE], hbuf[:, j % 2, :], hTh[:, j, 0:CAPE].bitcast(F32),
                                    ALU.subtract).then_inc(lo_ok, 1)
                    if 2 <= j < 2 + PC:
                        low_w2(e, j - 2)
                    if j == 1 and not (isinstance(e, int) and e == 0):
                        result(e - 1, RT - 1)

                def classify(t):
                    r = nrows(t)
                    T = e * RT + t
                    v.wait_ge(y_ok, T + 1)
                    y = yv[0:r, t % 2, :]
                    V.tensor_scalar(low[0:r, t % 2, :], y, -FLT_MAX, -1e4, ALU.is_lt, ALU.mult).then_inc(inf_ok, 1)
                    V.tensor_scalar(big[0:r, t % 2, :], y, FLT_MAX, 1e4, ALU.is_gt, ALU.mult).then_inc(inf_ok, 1)
                    V.tensor_scalar(finite[0:r, t % 2, :], yv[0:r, t % 2, :], 0.0, 0.0, ALU.mult, ALU.is_equal
                                    ).then_inc(fin_ok, 1)
                    V.tensor_tensor(total[0:r, t % 2, :], yv[0:r, t % 2, :], rows[0:r, u, t, 0:C], ALU.add
                                    ).then_inc(fin_ok, 1)

                for t in range(RT):
                    r = nrows(t)
                    if more:
                        low_rows(e + 1, t)
                    v.wait_ge(f2_ps, e * RT + t + 1)
                    wait(v, y_ok, e * RT + t - 1)
                    V.tensor_tensor(yb[0:r, t % 2, :], p_y[t % 2][0:r, 0:C],
                                    fb2_b[0:r, bass.ds(e, 1), :].rearrange("p a c -> p (a c)"), ALU.add
                                    ).then_inc(yb_ok, 1)
                    if t > 1:
                        result(e, t - 2)
                    if t > 0:
                        classify(t - 1)
                    if more and 2 <= t < 2 + PC:
                        low_w1(e + 1, t - 2)
                result(e, RT - 2)
                classify(RT - 1)

            for q in range(PC):
                low_w1(0, q)
            for t in range(RT):
                low_rows(0, t)
            v.wait_ge(d_b, 16)
            all_experts(v, expert)
            result(EXP - 1, RT - 1)


_OUT = "out_dram"


def kernel(**inputs):
    import concourse.bacc as bacc
    from concourse.bass_utils import run_bass_kernel_spmd as run

    nc = bacc.Bacc("TRN2", target_bir_lowering=False, num_devices=1)
    a = {k: np.asarray(v) for k, v in inputs.items()}

    def padded(v, n, fill):
        w = np.full((n,) + v.shape[1:], fill, v.dtype)
        w[:v.shape[0]] = v
        return w

    given = {
        "x": padded(a["x"], NPAD, 0),
        "srcR": padded(a["src"], EPAD + P, 0).reshape(-1, P),
        "dstR": padded(a["dst"], EPAD + P, PAD_DST).reshape(-1, P),
        "dstF": padded(a["dst"], EPAD + P, PAD_DST)[::P],
        "gW": a["L0_gnn_W"], "gb": a["L0_gnn_b"],
        "WqkvT": a["L0_mix_Wqkv"].T, "ln1g": a["L0_mix_ln1_g"], "ln1b": a["L0_mix_ln1_b"],
        "W1T": a["L0_mix_W1"].T, "b1": a["L0_mix_b1"], "W2T": a["L0_mix_W2"].T, "b2": a["L0_mix_b2"],
        "ln2g": a["L0_mix_ln2_g"], "ln2b": a["L0_mix_ln2_b"],
        "gateW": a["L0_ffn_gate_w"], "gateb": a["L0_ffn_gate_b"],
        "w1": a["L0_ffn_w1"], "fb1": a["L0_ffn_b1"].reshape(EXP, FT, P).transpose(2, 0, 1), "w2": a["L0_ffn_w2"], "fb2": a["L0_ffn_b2"],
    }
    arrays, args = {}, []
    for k, v in given.items():
        arrays["in_" + k] = np.ascontiguousarray(v)
        args.append(nc.dram_tensor("in_" + k, v.shape, mybir.dt.from_np(v.dtype), kind="ExternalInput").ap())
    out = nc.dram_tensor(_OUT, (NPAD, C), F32, kind="ExternalOutput").ap()
    build(nc, *args, out)
    r = run(nc, [arrays], core_ids=[0])
    return r.results[0][_OUT][:N]
```
